# Optimizing a Trainium2 kernel written in Bass

```python
import numpy as np
import jax
import jax.numpy as jnp

def _softmax(x, axis=-1):
    return jax.nn.softmax(x, axis=axis)

def _gelu(x):
    return jax.nn.gelu(x, approximate=True)

def _silu(x):
    return jax.nn.silu(x)

def _sigmoid(x):
    return jax.nn.sigmoid(x)

def _layernorm(x, axis=-1, eps=1e-05):
    m = jnp.mean(x, axis=axis, keepdims=True)
    v = jnp.var(x, axis=axis, keepdims=True)
    return (x - m) / jnp.sqrt(v + eps)

def _scatter_add(tgt, idx, src, axis=0):
    return tgt.at[idx].add(src)

def _segment_sum(src, seg, n):
    return jax.ops.segment_sum(src, seg, n)
kernel_name = 'mk_conv_seq_d4_conv_nchw192_r4_7481a6'

def setup_inputs(seed: int=0):
    np.random.seed(seed)
    _w = jnp.asarray

    def _rec_inputs():
        import jax
        import jax.numpy as jnp
        _gk = jax.random.key(seed)
        x = -0.0004039 + 1 * jax.random.normal(jax.random.fold_in(_gk, 1), (16, 48, 16, 16), jnp.float32)
        return x
    x = _rec_inputs()

    def _L0_conv_setup():
        import jax, jax.numpy as jnp
        import numpy as np
        B, DIM, HEADS, BLOCKS = (16, 48, 6, 6)
        H = W = 16
        WS, SHIFT, MLP = (8, 4, 4)
        N = WS * WS
        HD = DIM // HEADS
        NW = H // WS * (W // WS)
        SCALE = HD ** (-0.5)

        def _ln(x, g, b, eps=1e-05):
            mu = jnp.mean(x, -1, keepdims=True)
            var = jnp.mean(jnp.square(x - mu), -1, keepdims=True)
            return (x - mu) * jax.lax.rsqrt(var + eps) * g + b

        def _win_part(x):
            x = x.reshape(B, H // WS, WS, W // WS, WS, DIM)
            return x.transpose(0, 1, 3, 2, 4, 5).reshape(-1, N, DIM)

        def _win_rev(w):
            x = w.reshape(B, H // WS, W // WS, WS, WS, DIM)
            return x.transpose(0, 1, 3, 2, 4, 5).reshape(B, H, W, DIM)

        def _rel_pos_index():
            coords = np.stack(np.meshgrid(np.arange(WS), np.arange(WS), indexing='ij')).reshape(2, -1)
            rel = (coords[:, :, None] - coords[:, None, :]).transpose(1, 2, 0)
            rel[:, :, 0] += WS - 1
            rel[:, :, 1] += WS - 1
            rel[:, :, 0] *= 2 * WS - 1
            return jnp.asarray(rel.sum(-1))

        def _attn_mask():
            img = np.zeros((H, W))
            cnt = 0
            for hs in (slice(0, -WS), slice(-WS, -SHIFT), slice(-SHIFT, None)):
                for ws_ in (slice(0, -WS), slice(-WS, -SHIFT), slice(-SHIFT, None)):
                    img[hs, ws_] = cnt
                    cnt += 1
            mw = img.reshape(H // WS, WS, W // WS, WS).transpose(0, 2, 1, 3).reshape(-1, N)
            am = mw[:, None, :] - mw[:, :, None]
            return jnp.asarray(np.where(am != 0, -100.0, 0.0).astype(np.float32))
        RPI = _rel_pos_index()
        MASK = _attn_mask()

        def _block(x, shifted, n1g, n1b, qkvw, qkvb, pw, pb, rpb, n2g, n2b, f1w, f1b, f2w, f2b):
            shortcut = x
            x = _ln(x, n1g, n1b).reshape(B, H, W, DIM)
            if shifted:
                x = jnp.roll(x, (-SHIFT, -SHIFT), (1, 2))
            xw = _win_part(x)
            qkv = (xw @ qkvw.T + qkvb).reshape(-1, N, 3, HEADS, HD).transpose(2, 0, 3, 1, 4)
            q, k, v = (qkv[0], qkv[1], qkv[2])
            attn = jnp.einsum('bhnd,bhmd->bhnm', q * SCALE, k)
            attn = attn + rpb[RPI].transpose(2, 0, 1)[None]
            if shifted:
                attn = (attn.reshape(B, NW, HEADS, N, N) + MASK[None, :, None]).reshape(-1, HEADS, N, N)
            attn = jax.nn.softmax(attn, -1)
            xw = jnp.einsum('bhnm,bhmd->bnhd', attn, v).reshape(-1, N, DIM)
            xw = xw @ pw.T + pb
            x = _win_rev(xw)
            if shifted:
                x = jnp.roll(x, (SHIFT, SHIFT), (1, 2))
            x = shortcut + x.reshape(B, H * W, DIM)
            h = _ln(x, n2g, n2b)
            h = jax.nn.gelu(h @ f1w.T + f1b, approximate=False) @ f2w.T + f2b
            return x + h

        def _forward(x, en_g, en_b, n1_g, n1_b, qkv_w, qkv_b, proj_w, proj_b, rpb, n2_g, n2_b, fc1_w, fc1_b, fc2_w, fc2_b, fn_g, fn_b, conv_w):
            y = x.reshape(B, DIM, H * W).transpose(0, 2, 1)
            y = _ln(y, en_g, en_b)
            for i in range(BLOCKS):
                y = _block(y, i % 2 == 1, n1_g[i], n1_b[i], qkv_w[i], qkv_b[i], proj_w[i], proj_b[i], rpb[i], n2_g[i], n2_b[i], fc1_w[i], fc1_b[i], fc2_w[i], fc2_b[i])
            y = _ln(y, fn_g, fn_b)
            y = y.transpose(0, 2, 1).reshape(B, DIM, H, W)
            return y + jax.lax.conv_general_dilated(y, conv_w, (1, 1), 'SAME', dimension_numbers=('NCHW', 'OIHW', 'NCHW'))
        key = jax.random.key(seed)
        ks = jax.random.split(key, 7)
        s = 0.02
        f32 = jnp.float32
        return {'x': jax.random.normal(ks[0], (B, DIM, H, W), f32), 'en_g': jnp.ones((DIM,), f32), 'en_b': jnp.zeros((DIM,), f32), 'n1_g': jnp.ones((BLOCKS, DIM), f32), 'n1_b': jnp.zeros((BLOCKS, DIM), f32), 'qkv_w': s * jax.random.normal(ks[1], (BLOCKS, 3 * DIM, DIM), f32), 'qkv_b': jnp.zeros((BLOCKS, 3 * DIM), f32), 'proj_w': s * jax.random.normal(ks[2], (BLOCKS, DIM, DIM), f32), 'proj_b': jnp.zeros((BLOCKS, DIM), f32), 'rpb': s * jax.random.normal(ks[3], (BLOCKS, (2 * WS - 1) ** 2, HEADS), f32), 'n2_g': jnp.ones((BLOCKS, DIM), f32), 'n2_b': jnp.zeros((BLOCKS, DIM), f32), 'fc1_w': s * jax.random.normal(ks[4], (BLOCKS, MLP * DIM, DIM), f32), 'fc1_b': jnp.zeros((BLOCKS, MLP * DIM), f32), 'fc2_w': s * jax.random.normal(ks[5], (BLOCKS, DIM, MLP * DIM), f32), 'fc2_b': jnp.zeros((BLOCKS, DIM), f32), 'fn_g': jnp.ones((DIM,), f32), 'fn_b': jnp.zeros((DIM,), f32), 'conv_w': s * jax.random.normal(ks[6], (DIM, DIM, 3, 3), f32)}
    _L0_conv_all = _L0_conv_setup()
    _L0_conv_in = {k: v for k, v in _L0_conv_all.items() if k in ('en_g', 'en_b', 'n1_g', 'n1_b', 'qkv_w', 'qkv_b', 'proj_w', 'proj_b', 'rpb', 'n2_g', 'n2_b', 'fc1_w', 'fc1_b', 'fc2_w', 'fc2_b', 'fn_g', 'fn_b', 'conv_w')}
    del _L0_conv_all

    def _L1_conv_setup():
        import jax, jax.numpy as jnp
        import numpy as np
        B, DIM, H, W = (2, 48, 64, 64)
        WIN = 4
        EPS = 1e-05

        def _cd_conj(x):
            if len(x) == 1:
                return x
            h = len(x) // 2
            return np.concatenate([_cd_conj(x[:h]), -x[h:]])

        def _cd_mult(a, b):
            n = len(a)
            if n == 1:
                return a * b
            h = n // 2
            a1, a2, b1, b2 = (a[:h], a[h:], b[:h], b[h:])
            c1 = _cd_mult(a1, b1) - _cd_mult(_cd_conj(b2), a2)
            c2 = _cd_mult(b2, a1) + _cd_mult(a2, _cd_conj(b1))
            return np.concatenate([c1, c2])

        def _sedenion_table(n=16):
            eye = np.eye(n, dtype=np.float32)
            M = np.zeros((n, n, n), dtype=np.float32)
            for i in range(n):
                for j in range(n):
                    M[i, j] = _cd_mult(eye[i], eye[j])
            return M
        SED_TABLE = jnp.asarray(_sedenion_table(16))

        def layer_norm(x, g, b):
            m = x.mean(-1, keepdims=True)
            v = ((x - m) ** 2).mean(-1, keepdims=True)
            return (x - m) * jax.lax.rsqrt(v + EPS) * g + b

        def get_window(x):
            b, c, h, w = x.shape
            x = x.reshape(b, c, h // WIN, WIN, w // WIN, WIN)
            x = x.transpose(0, 2, 4, 3, 5, 1)
            return x.reshape(b, h // WIN, w // WIN, WIN * WIN * c)

        def reverse_window(x, c):
            b, hh, ww, _ = x.shape
            x = x.reshape(b, hh, ww, WIN, WIN, c)
            x = x.transpose(0, 5, 1, 3, 2, 4)
            return x.reshape(b, c, hh * WIN, ww * WIN)

        def sedenion_full_weight(w_sed):
            d = w_sed.shape[1]
            wf = jnp.einsum('ijk,jde->idke', SED_TABLE, w_sed)
            return wf.reshape(16 * d, 16 * w_sed.shape[2])
        key = jax.random.key(seed)
        ks = jax.random.split(key, 8)
        d, dh = (DIM, 4 * DIM)
        s = 0.02
        return {'x': jax.random.normal(ks[0], (B, DIM, H, W), jnp.float32), 'norm1_g': jnp.ones((d,), jnp.float32), 'norm1_b': jnp.zeros((d,), jnp.float32), 'w_sed': jax.random.normal(ks[1], (16, d, d), jnp.float32) * s, 'proj_w': jax.random.normal(ks[2], (d, d), jnp.float32) * s, 'proj_b': jnp.zeros((d,), jnp.float32), 'norm2_g': jnp.ones((d,), jnp.float32), 'norm2_b': jnp.zeros((d,), jnp.float32), 'fc1_w': jax.random.normal(ks[3], (d, dh), jnp.float32) * s, 'fc1_b': jnp.zeros((dh,), jnp.float32), 'fc2_w': jax.random.normal(ks[4], (dh, d), jnp.float32) * s, 'fc2_b': jnp.zeros((d,), jnp.float32)}
    _L1_conv_all = _L1_conv_setup()
    _L1_conv_in = {k: v for k, v in _L1_conv_all.items() if k in ('norm1_g', 'norm1_b', 'w_sed', 'proj_w', 'proj_b', 'norm2_g', 'norm2_b', 'fc1_w', 'fc1_b', 'fc2_w', 'fc2_b')}
    del _L1_conv_all

    def _L2_conv_setup():
        import jax, jax.numpy as jnp
        import numpy as np
        DIM = 48
        K = 3
        RED = 4
        B, H, W = (4, 64, 64)
        EPS = 1e-05

        def _make_mask():
            m = np.ones((DIM, 1, K, K), np.float32)
            m[:, :, K // 2, K // 2:] = 0.0
            m[:, :, K // 2 + 1:] = 0.0
            return jnp.asarray(m)
        MASK = _make_mask()
        key = jax.random.key(seed)
        ks = jax.random.split(key, 4)
        r = DIM // RED
        return {'x': jax.random.normal(ks[0], (B, DIM, H, W), jnp.float32), 'w1': jax.random.normal(ks[1], (r, DIM), jnp.float32) * 0.05, 'gamma': jnp.ones((r,), jnp.float32), 'beta': jnp.zeros((r,), jnp.float32), 'running_mean': jnp.zeros((r,), jnp.float32), 'running_var': jnp.ones((r,), jnp.float32), 'w2': jax.random.normal(ks[2], (DIM * K * K, r), jnp.float32) * 0.05, 'b2': jnp.zeros((DIM * K * K,), jnp.float32), 'bias': jnp.zeros((DIM,), jnp.float32)}
    _L2_conv_all = _L2_conv_setup()
    _L2_conv_in = {k: v for k, v in _L2_conv_all.items() if k in ('w1', 'gamma', 'beta', 'running_mean', 'running_var', 'w2', 'b2', 'bias')}
    del _L2_conv_all

    def _L3_conv_setup():
        import jax, jax.numpy as jnp
        import numpy as np
        CHUNK = 8

        def conv1x1(x, w):
            return jnp.einsum('bchw,oc->bohw', x, w)

        def layernorm2d(x, w, b, eps=1e-05):
            mu = x.mean(axis=1, keepdims=True)
            var = ((x - mu) ** 2).mean(axis=1, keepdims=True)
            return (x - mu) / jnp.sqrt(var + eps) * w[None, :, None, None] + b[None, :, None, None]

        def grn(x, gamma, beta, eps=1e-06):
            Gx = jnp.sqrt(jnp.sum(x * x, axis=(2, 3), keepdims=True))
            Nx = Gx / (Gx.mean(axis=1, keepdims=True) + eps)
            return gamma[None, :, None, None] * (x * Nx) + beta[None, :, None, None] + x

        def normalize_w(Gl, Gm, Gr, eps=1e-07):
            s = jnp.abs(Gl) + jnp.abs(Gm) + jnp.abs(Gr) + eps
            return (Gl / s, Gm / s, Gr / s)

        def gate_scan(X, L, Gl, Gm, Gr, chunk):
            B, C, H, W = X.shape
            nc = W // chunk

            def prep(a):
                return a.reshape(B, C, H, nc, chunk).transpose(4, 0, 1, 2, 3)
            xs, ls, gls, gms, grs = map(prep, (X, L, Gl, Gm, Gr))
            h0 = jnp.zeros((B, C, H, nc), X.dtype)

            def step(h, inp):
                x, l, gl, gm, gr = inp
                z = jnp.zeros_like(h[:, :, :1])
                h_up = jnp.concatenate([z, h[:, :, :-1]], axis=2)
                h_dn = jnp.concatenate([h[:, :, 1:], z], axis=2)
                hn = l * x + gl * h_up + gm * h + gr * h_dn
                return (hn, hn)
            _, hs = jax.lax.scan(step, h0, (xs, ls, gls, gms, grs))
            return hs.transpose(1, 2, 3, 4, 0).reshape(B, C, H, W)

        def ss2d_forward(x, W_in, W_dw, b_dw, W_xd, W_w, W_l, W_u, W_d, w_m, grn_gamma, grn_beta, ln_w, ln_b, W_out):
            B, _, H, W = x.shape
            Din = W_in.shape[0]
            x = conv1x1(x, W_in)
            x = jax.lax.conv_general_dilated(x, W_dw, (1, 1), 'SAME', feature_group_count=Din, dimension_numbers=('NCHW', 'OIHW', 'NCHW'))
            x = x + b_dw[None, :, None, None]
            x_proxy = conv1x1(x, W_xd)
            ws = conv1x1(x_proxy, W_w)
            Ls = conv1x1(x_proxy, W_l)
            Us = conv1x1(x_proxy, W_u)
            Ds = conv1x1(x_proxy, W_d)
            x_t = x.transpose(0, 1, 3, 2)
            x_hwwh = jnp.stack([x, x_t], axis=1)
            xs = jnp.concatenate([x_hwwh, jnp.flip(x_hwwh, axis=-1)], axis=1)
            xs = xs.reshape(B, 4 * Din, H, W)
            nd = 4 * Din
            Gl, Gm, Gr = (ws[:, :nd], ws[:, nd:2 * nd], ws[:, 2 * nd:])
            Gl, Gm, Gr = normalize_w(Gl, Gm, Gr)
            out = gate_scan(xs, Ls, Gl, Gm, Gr, CHUNK)
            out = out * Us + xs * Ds
            out_y = out.reshape(B, 4, Din, H, W)
            y = jnp.einsum('bdchw,d->bchw', out_y, w_m)
            y = layernorm2d(y, ln_w, ln_b)
            y = grn(y, grn_gamma, grn_beta)
            return conv1x1(y, W_out)
        key = jax.random.key(seed)
        ks = jax.random.split(key, 16)
        B, d_model, H, W = (8, 48, 16, 16)
        d_inner, d_state, nd = (96, 16, 4)

        def w(k, shape, fan_in):
            return jax.random.normal(k, shape, jnp.float32) / np.sqrt(fan_in)
        return {'x': jax.random.normal(ks[0], (B, d_model, H, W), jnp.float32), 'W_in': w(ks[1], (d_inner, d_model), d_model), 'W_dw': w(ks[2], (d_inner, 1, 3, 3), 9), 'b_dw': jnp.zeros((d_inner,), jnp.float32), 'W_xd': w(ks[3], (d_state, d_inner), d_inner), 'W_w': w(ks[4], (12 * d_inner, d_state), d_state), 'W_l': w(ks[5], (nd * d_inner, d_state), d_state), 'W_u': w(ks[6], (nd * d_inner, d_state), d_state), 'W_d': w(ks[7], (nd * d_inner, d_state), d_state), 'w_m': w(ks[8], (nd,), nd), 'grn_gamma': 0.1 * jax.random.normal(ks[9], (d_inner,), jnp.float32), 'grn_beta': 0.1 * jax.random.normal(ks[10], (d_inner,), jnp.float32), 'ln_w': jnp.ones((d_inner,), jnp.float32), 'ln_b': jnp.zeros((d_inner,), jnp.float32), 'W_out': w(ks[11], (d_model, d_inner), d_inner)}
    _L3_conv_all = _L3_conv_setup()
    _L3_conv_in = {k: v for k, v in _L3_conv_all.items() if k in ('W_in', 'W_dw', 'b_dw', 'W_xd', 'W_w', 'W_l', 'W_u', 'W_d', 'w_m', 'grn_gamma', 'grn_beta', 'ln_w', 'ln_b', 'W_out')}
    del _L3_conv_all
    return {'x': x, 'L0_conv_en_g': _L0_conv_in['en_g'], 'L0_conv_en_b': _L0_conv_in['en_b'], 'L0_conv_n1_g': _L0_conv_in['n1_g'], 'L0_conv_n1_b': _L0_conv_in['n1_b'], 'L0_conv_qkv_w': _L0_conv_in['qkv_w'], 'L0_conv_qkv_b': _L0_conv_in['qkv_b'], 'L0_conv_proj_w': _L0_conv_in['proj_w'], 'L0_conv_proj_b': _L0_conv_in['proj_b'], 'L0_conv_rpb': _L0_conv_in['rpb'], 'L0_conv_n2_g': _L0_conv_in['n2_g'], 'L0_conv_n2_b': _L0_conv_in['n2_b'], 'L0_conv_fc1_w': _L0_conv_in['fc1_w'], 'L0_conv_fc1_b': _L0_conv_in['fc1_b'], 'L0_conv_fc2_w': _L0_conv_in['fc2_w'], 'L0_conv_fc2_b': _L0_conv_in['fc2_b'], 'L0_conv_fn_g': _L0_conv_in['fn_g'], 'L0_conv_fn_b': _L0_conv_in['fn_b'], 'L0_conv_conv_w': _L0_conv_in['conv_w'], 'L1_conv_norm1_g': _L1_conv_in['norm1_g'], 'L1_conv_norm1_b': _L1_conv_in['norm1_b'], 'L1_conv_w_sed': _L1_conv_in['w_sed'], 'L1_conv_proj_w': _L1_conv_in['proj_w'], 'L1_conv_proj_b': _L1_conv_in['proj_b'], 'L1_conv_norm2_g': _L1_conv_in['norm2_g'], 'L1_conv_norm2_b': _L1_conv_in['norm2_b'], 'L1_conv_fc1_w': _L1_conv_in['fc1_w'], 'L1_conv_fc1_b': _L1_conv_in['fc1_b'], 'L1_conv_fc2_w': _L1_conv_in['fc2_w'], 'L1_conv_fc2_b': _L1_conv_in['fc2_b'], 'L2_conv_w1': _L2_conv_in['w1'], 'L2_conv_gamma': _L2_conv_in['gamma'], 'L2_conv_beta': _L2_conv_in['beta'], 'L2_conv_running_mean': _L2_conv_in['running_mean'], 'L2_conv_running_var': _L2_conv_in['running_var'], 'L2_conv_w2': _L2_conv_in['w2'], 'L2_conv_b2': _L2_conv_in['b2'], 'L2_conv_bias': _L2_conv_in['bias'], 'L3_conv_W_in': _L3_conv_in['W_in'], 'L3_conv_W_dw': _L3_conv_in['W_dw'], 'L3_conv_b_dw': _L3_conv_in['b_dw'], 'L3_conv_W_xd': _L3_conv_in['W_xd'], 'L3_conv_W_w': _L3_conv_in['W_w'], 'L3_conv_W_l': _L3_conv_in['W_l'], 'L3_conv_W_u': _L3_conv_in['W_u'], 'L3_conv_W_d': _L3_conv_in['W_d'], 'L3_conv_w_m': _L3_conv_in['w_m'], 'L3_conv_grn_gamma': _L3_conv_in['grn_gamma'], 'L3_conv_grn_beta': _L3_conv_in['grn_beta'], 'L3_conv_ln_w': _L3_conv_in['ln_w'], 'L3_conv_ln_b': _L3_conv_in['ln_b'], 'L3_conv_W_out': _L3_conv_in['W_out']}

def reference(x, L0_conv_en_g, L0_conv_en_b, L0_conv_n1_g, L0_conv_n1_b, L0_conv_qkv_w, L0_conv_qkv_b, L0_conv_proj_w, L0_conv_proj_b, L0_conv_rpb, L0_conv_n2_g, L0_conv_n2_b, L0_conv_fc1_w, L0_conv_fc1_b, L0_conv_fc2_w, L0_conv_fc2_b, L0_conv_fn_g, L0_conv_fn_b, L0_conv_conv_w, L1_conv_norm1_g, L1_conv_norm1_b, L1_conv_w_sed, L1_conv_proj_w, L1_conv_proj_b, L1_conv_norm2_g, L1_conv_norm2_b, L1_conv_fc1_w, L1_conv_fc1_b, L1_conv_fc2_w, L1_conv_fc2_b, L2_conv_w1, L2_conv_gamma, L2_conv_beta, L2_conv_running_mean, L2_conv_running_var, L2_conv_w2, L2_conv_b2, L2_conv_bias, L3_conv_W_in, L3_conv_W_dw, L3_conv_b_dw, L3_conv_W_xd, L3_conv_W_w, L3_conv_W_l, L3_conv_W_u, L3_conv_W_d, L3_conv_w_m, L3_conv_grn_gamma, L3_conv_grn_beta, L3_conv_ln_w, L3_conv_ln_b, L3_conv_W_out):
    import jax
    import jax.numpy as jnp

    def _L0_conv_ref(x, en_g, en_b, n1_g, n1_b, qkv_w, qkv_b, proj_w, proj_b, rpb, n2_g, n2_b, fc1_w, fc1_b, fc2_w, fc2_b, fn_g, fn_b, conv_w):
        import jax, jax.numpy as jnp
        import numpy as np
        B, DIM, HEADS, BLOCKS = (16, 48, 6, 6)
        H = W = 16
        WS, SHIFT, MLP = (8, 4, 4)
        N = WS * WS
        HD = DIM // HEADS
        NW = H // WS * (W // WS)
        SCALE = HD ** (-0.5)

        def _ln(x, g, b, eps=1e-05):
            mu = jnp.mean(x, -1, keepdims=True)
            var = jnp.mean(jnp.square(x - mu), -1, keepdims=True)
            return (x - mu) * jax.lax.rsqrt(var + eps) * g + b

        def _win_part(x):
            x = x.reshape(B, H // WS, WS, W // WS, WS, DIM)
            return x.transpose(0, 1, 3, 2, 4, 5).reshape(-1, N, DIM)

        def _win_rev(w):
            x = w.reshape(B, H // WS, W // WS, WS, WS, DIM)
            return x.transpose(0, 1, 3, 2, 4, 5).reshape(B, H, W, DIM)

        def _rel_pos_index():
            coords = np.stack(np.meshgrid(np.arange(WS), np.arange(WS), indexing='ij')).reshape(2, -1)
            rel = (coords[:, :, None] - coords[:, None, :]).transpose(1, 2, 0)
            rel[:, :, 0] += WS - 1
            rel[:, :, 1] += WS - 1
            rel[:, :, 0] *= 2 * WS - 1
            return jnp.asarray(rel.sum(-1))

        def _attn_mask():
            img = np.zeros((H, W))
            cnt = 0
            for hs in (slice(0, -WS), slice(-WS, -SHIFT), slice(-SHIFT, None)):
                for ws_ in (slice(0, -WS), slice(-WS, -SHIFT), slice(-SHIFT, None)):
                    img[hs, ws_] = cnt
                    cnt += 1
            mw = img.reshape(H // WS, WS, W // WS, WS).transpose(0, 2, 1, 3).reshape(-1, N)
            am = mw[:, None, :] - mw[:, :, None]
            return jnp.asarray(np.where(am != 0, -100.0, 0.0).astype(np.float32))
        RPI = _rel_pos_index()
        MASK = _attn_mask()

        def _block(x, shifted, n1g, n1b, qkvw, qkvb, pw, pb, rpb, n2g, n2b, f1w, f1b, f2w, f2b):
            shortcut = x
            x = _ln(x, n1g, n1b).reshape(B, H, W, DIM)
            if shifted:
                x = jnp.roll(x, (-SHIFT, -SHIFT), (1, 2))
            xw = _win_part(x)
            qkv = (xw @ qkvw.T + qkvb).reshape(-1, N, 3, HEADS, HD).transpose(2, 0, 3, 1, 4)
            q, k, v = (qkv[0], qkv[1], qkv[2])
            attn = jnp.einsum('bhnd,bhmd->bhnm', q * SCALE, k)
            attn = attn + rpb[RPI].transpose(2, 0, 1)[None]
            if shifted:
                attn = (attn.reshape(B, NW, HEADS, N, N) + MASK[None, :, None]).reshape(-1, HEADS, N, N)
            attn = jax.nn.softmax(attn, -1)
            xw = jnp.einsum('bhnm,bhmd->bnhd', attn, v).reshape(-1, N, DIM)
            xw = xw @ pw.T + pb
            x = _win_rev(xw)
            if shifted:
                x = jnp.roll(x, (SHIFT, SHIFT), (1, 2))
            x = shortcut + x.reshape(B, H * W, DIM)
            h = _ln(x, n2g, n2b)
            h = jax.nn.gelu(h @ f1w.T + f1b, approximate=False) @ f2w.T + f2b
            return x + h

        def _forward(x, en_g, en_b, n1_g, n1_b, qkv_w, qkv_b, proj_w, proj_b, rpb, n2_g, n2_b, fc1_w, fc1_b, fc2_w, fc2_b, fn_g, fn_b, conv_w):
            y = x.reshape(B, DIM, H * W).transpose(0, 2, 1)
            y = _ln(y, en_g, en_b)
            for i in range(BLOCKS):
                y = _block(y, i % 2 == 1, n1_g[i], n1_b[i], qkv_w[i], qkv_b[i], proj_w[i], proj_b[i], rpb[i], n2_g[i], n2_b[i], fc1_w[i], fc1_b[i], fc2_w[i], fc2_b[i])
            y = _ln(y, fn_g, fn_b)
            y = y.transpose(0, 2, 1).reshape(B, DIM, H, W)
            return y + jax.lax.conv_general_dilated(y, conv_w, (1, 1), 'SAME', dimension_numbers=('NCHW', 'OIHW', 'NCHW'))
        return _forward(x, en_g, en_b, n1_g, n1_b, qkv_w, qkv_b, proj_w, proj_b, rpb, n2_g, n2_b, fc1_w, fc1_b, fc2_w, fc2_b, fn_g, fn_b, conv_w)

    def _L1_conv_ref(x, norm1_g, norm1_b, w_sed, proj_w, proj_b, norm2_g, norm2_b, fc1_w, fc1_b, fc2_w, fc2_b):
        import jax, jax.numpy as jnp
        import numpy as np
        B, DIM, H, W = (2, 48, 64, 64)
        WIN = 4
        EPS = 1e-05

        def _cd_conj(x):
            if len(x) == 1:
                return x
            h = len(x) // 2
            return np.concatenate([_cd_conj(x[:h]), -x[h:]])

        def _cd_mult(a, b):
            n = len(a)
            if n == 1:
                return a * b
            h = n // 2
            a1, a2, b1, b2 = (a[:h], a[h:], b[:h], b[h:])
            c1 = _cd_mult(a1, b1) - _cd_mult(_cd_conj(b2), a2)
            c2 = _cd_mult(b2, a1) + _cd_mult(a2, _cd_conj(b1))
            return np.concatenate([c1, c2])

        def _sedenion_table(n=16):
            eye = np.eye(n, dtype=np.float32)
            M = np.zeros((n, n, n), dtype=np.float32)
            for i in range(n):
                for j in range(n):
                    M[i, j] = _cd_mult(eye[i], eye[j])
            return M
        SED_TABLE = jnp.asarray(_sedenion_table(16))

        def layer_norm(x, g, b):
            m = x.mean(-1, keepdims=True)
            v = ((x - m) ** 2).mean(-1, keepdims=True)
            return (x - m) * jax.lax.rsqrt(v + EPS) * g + b

        def get_window(x):
            b, c, h, w = x.shape
            x = x.reshape(b, c, h // WIN, WIN, w // WIN, WIN)
            x = x.transpose(0, 2, 4, 3, 5, 1)
            return x.reshape(b, h // WIN, w // WIN, WIN * WIN * c)

        def reverse_window(x, c):
            b, hh, ww, _ = x.shape
            x = x.reshape(b, hh, ww, WIN, WIN, c)
            x = x.transpose(0, 5, 1, 3, 2, 4)
            return x.reshape(b, c, hh * WIN, ww * WIN)

        def sedenion_full_weight(w_sed):
            d = w_sed.shape[1]
            wf = jnp.einsum('ijk,jde->idke', SED_TABLE, w_sed)
            return wf.reshape(16 * d, 16 * w_sed.shape[2])
        b, c, h, w = x.shape
        xn = layer_norm(x.transpose(0, 2, 3, 1), norm1_g, norm1_b).transpose(0, 3, 1, 2)
        xw = get_window(xn)
        wf = sedenion_full_weight(w_sed)
        xw = xw @ wf
        x1 = reverse_window(xw, c)
        y = x1.transpose(0, 2, 3, 1)
        y = jax.nn.gelu(y, approximate=False)
        y = y @ proj_w + proj_b
        x = x + y.transpose(0, 3, 1, 2)
        hbr = layer_norm(x.transpose(0, 2, 3, 1), norm2_g, norm2_b)
        hbr = jax.nn.gelu(hbr @ fc1_w + fc1_b, approximate=False)
        hbr = hbr @ fc2_w + fc2_b
        x = x + hbr.transpose(0, 3, 1, 2)
        return x

    def _L2_conv_ref(x, w1, gamma, beta, running_mean, running_var, w2, b2, bias):
        import jax, jax.numpy as jnp
        import numpy as np
        DIM = 48
        K = 3
        RED = 4
        B, H, W = (4, 64, 64)
        EPS = 1e-05

        def _make_mask():
            m = np.ones((DIM, 1, K, K), np.float32)
            m[:, :, K // 2, K // 2:] = 0.0
            m[:, :, K // 2 + 1:] = 0.0
            return jnp.asarray(m)
        MASK = _make_mask()
        b, c, h, w = x.shape
        pooled = x.mean(axis=(2, 3))
        t = pooled @ w1.T
        t = gamma * (t - running_mean) * jax.lax.rsqrt(running_var + EPS) + beta
        t = jax.nn.relu(t)
        wt = t @ w2.T + b2
        wt = wt.reshape(b * DIM, 1, K, K) * jnp.tile(MASK, (b, 1, 1, 1))
        out = jax.lax.conv_general_dilated(x.reshape(1, b * c, h, w), wt, window_strides=(1, 1), padding=((1, 1), (1, 1)), feature_group_count=b * DIM, dimension_numbers=('NCHW', 'OIHW', 'NCHW'))
        out = out + jnp.tile(bias, (b,))[None, :, None, None]
        return out.reshape(b, c, h, w)

    def _L3_conv_ref(x, W_in, W_dw, b_dw, W_xd, W_w, W_l, W_u, W_d, w_m, grn_gamma, grn_beta, ln_w, ln_b, W_out):
        import jax, jax.numpy as jnp
        import numpy as np
        CHUNK = 8

        def conv1x1(x, w):
            return jnp.einsum('bchw,oc->bohw', x, w)

        def layernorm2d(x, w, b, eps=1e-05):
            mu = x.mean(axis=1, keepdims=True)
            var = ((x - mu) ** 2).mean(axis=1, keepdims=True)
            return (x - mu) / jnp.sqrt(var + eps) * w[None, :, None, None] + b[None, :, None, None]

        def grn(x, gamma, beta, eps=1e-06):
            Gx = jnp.sqrt(jnp.sum(x * x, axis=(2, 3), keepdims=True))
            Nx = Gx / (Gx.mean(axis=1, keepdims=True) + eps)
            return gamma[None, :, None, None] * (x * Nx) + beta[None, :, None, None] + x

        def normalize_w(Gl, Gm, Gr, eps=1e-07):
            s = jnp.abs(Gl) + jnp.abs(Gm) + jnp.abs(Gr) + eps
            return (Gl / s, Gm / s, Gr / s)

        def gate_scan(X, L, Gl, Gm, Gr, chunk):
            B, C, H, W = X.shape
            nc = W // chunk

            def prep(a):
                return a.reshape(B, C, H, nc, chunk).transpose(4, 0, 1, 2, 3)
            xs, ls, gls, gms, grs = map(prep, (X, L, Gl, Gm, Gr))
            h0 = jnp.zeros((B, C, H, nc), X.dtype)

            def step(h, inp):
                x, l, gl, gm, gr = inp
                z = jnp.zeros_like(h[:, :, :1])
                h_up = jnp.concatenate([z, h[:, :, :-1]], axis=2)
                h_dn = jnp.concatenate([h[:, :, 1:], z], axis=2)
                hn = l * x + gl * h_up + gm * h + gr * h_dn
                return (hn, hn)
            _, hs = jax.lax.scan(step, h0, (xs, ls, gls, gms, grs))
            return hs.transpose(1, 2, 3, 4, 0).reshape(B, C, H, W)

        def ss2d_forward(x, W_in, W_dw, b_dw, W_xd, W_w, W_l, W_u, W_d, w_m, grn_gamma, grn_beta, ln_w, ln_b, W_out):
            B, _, H, W = x.shape
            Din = W_in.shape[0]
            x = conv1x1(x, W_in)
            x = jax.lax.conv_general_dilated(x, W_dw, (1, 1), 'SAME', feature_group_count=Din, dimension_numbers=('NCHW', 'OIHW', 'NCHW'))
            x = x + b_dw[None, :, None, None]
            x_proxy = conv1x1(x, W_xd)
            ws = conv1x1(x_proxy, W_w)
            Ls = conv1x1(x_proxy, W_l)
            Us = conv1x1(x_proxy, W_u)
            Ds = conv1x1(x_proxy, W_d)
            x_t = x.transpose(0, 1, 3, 2)
            x_hwwh = jnp.stack([x, x_t], axis=1)
            xs = jnp.concatenate([x_hwwh, jnp.flip(x_hwwh, axis=-1)], axis=1)
            xs = xs.reshape(B, 4 * Din, H, W)
            nd = 4 * Din
            Gl, Gm, Gr = (ws[:, :nd], ws[:, nd:2 * nd], ws[:, 2 * nd:])
            Gl, Gm, Gr = normalize_w(Gl, Gm, Gr)
            out = gate_scan(xs, Ls, Gl, Gm, Gr, CHUNK)
            out = out * Us + xs * Ds
            out_y = out.reshape(B, 4, Din, H, W)
            y = jnp.einsum('bdchw,d->bchw', out_y, w_m)
            y = layernorm2d(y, ln_w, ln_b)
            y = grn(y, grn_gamma, grn_beta)
            return conv1x1(y, W_out)
        return ss2d_forward(x, W_in, W_dw, b_dw, W_xd, W_w, W_l, W_u, W_d, w_m, grn_gamma, grn_beta, ln_w, ln_b, W_out)

    def _gn(v, G=32, eps=1e-05):
        B_, C_, H_, W_ = v.shape
        g = v.reshape(B_, G, C_ // G, H_, W_)
        m = jnp.mean(g, axis=(2, 3, 4), keepdims=True)
        s = jnp.var(g, axis=(2, 3, 4), keepdims=True)
        return ((g - m) / jnp.sqrt(s + eps)).reshape(v.shape)

    def _ln_c(v, eps=1e-06):
        m = jnp.mean(v, axis=1, keepdims=True)
        s = jnp.var(v, axis=1, keepdims=True)
        return (v - m) / jnp.sqrt(s + eps)

    def _ln_t(v, eps=1e-05):
        m = jnp.mean(v, axis=-1, keepdims=True)
        s = jnp.var(v, axis=-1, keepdims=True)
        return (v - m) / jnp.sqrt(s + eps)

    def _to_tokens(v):
        B_, C_, H_, W_ = v.shape
        return v.reshape(B_, C_, H_ * W_).transpose(0, 2, 1)

    def _from_tokens(t, like):
        B_, C_, H_, W_ = like.shape
        return t.transpose(0, 2, 1).reshape(B_, C_, H_, W_)
    x = _L0_conv_ref(x, L0_conv_en_g, L0_conv_en_b, L0_conv_n1_g, L0_conv_n1_b, L0_conv_qkv_w, L0_conv_qkv_b, L0_conv_proj_w, L0_conv_proj_b, L0_conv_rpb, L0_conv_n2_g, L0_conv_n2_b, L0_conv_fc1_w, L0_conv_fc1_b, L0_conv_fc2_w, L0_conv_fc2_b, L0_conv_fn_g, L0_conv_fn_b, L0_conv_conv_w)
    x = _L1_conv_ref(x, L1_conv_norm1_g, L1_conv_norm1_b, L1_conv_w_sed, L1_conv_proj_w, L1_conv_proj_b, L1_conv_norm2_g, L1_conv_norm2_b, L1_conv_fc1_w, L1_conv_fc1_b, L1_conv_fc2_w, L1_conv_fc2_b)
    x = _L2_conv_ref(x, L2_conv_w1, L2_conv_gamma, L2_conv_beta, L2_conv_running_mean, L2_conv_running_var, L2_conv_w2, L2_conv_b2, L2_conv_bias)
    x = _L3_conv_ref(x, L3_conv_W_in, L3_conv_W_dw, L3_conv_b_dw, L3_conv_W_xd, L3_conv_W_w, L3_conv_W_l, L3_conv_W_u, L3_conv_W_d, L3_conv_w_m, L3_conv_grn_gamma, L3_conv_grn_beta, L3_conv_ln_w, L3_conv_ln_b, L3_conv_W_out)
    return x

_drawn_inputs = setup_inputs


def setup_inputs(seed=0):
    import zlib

    import numpy as np

    out = dict(_drawn_inputs(seed))
    spreads = {'L0_conv_en_g': (1.0, 0.2),
     'L0_conv_en_b': (0.0, 0.1),
     'L0_conv_n1_g': (1.0, 0.6),
     'L0_conv_n1_b': (0.0, 0.8),
     'L0_conv_qkv_b': (0.0, 0.1),
     'L0_conv_proj_b': (0.0, 0.1),
     'L0_conv_n2_g': (1.0, 0.6),
     'L0_conv_n2_b': (0.0, 0.8),
     'L0_conv_fc1_b': (0.0, 0.1),
     'L0_conv_fc2_b': (0.0, 0.1),
     'L0_conv_fn_g': (1.0, 0.2),
     'L0_conv_fn_b': (0.0, 0.1),
     'L1_conv_norm1_g': (1.0, 0.6),
     'L1_conv_norm1_b': (0.0, 0.8),
     'L1_conv_proj_b': (0.0, 0.1),
     'L1_conv_norm2_g': (1.0, 0.6),
     'L1_conv_norm2_b': (0.0, 2.0),
     'L1_conv_fc1_b': (0.0, 0.321),
     'L1_conv_fc2_b': (0.0, 0.1),
     'L2_conv_gamma': (1.0, 0.2),
     'L2_conv_beta': (0.0, 0.1),
     'L2_conv_running_mean': (0.0, 0.1),
     'L2_conv_running_var': (1.0, 0.2),
     'L2_conv_b2': (0.0, 0.1),
     'L2_conv_bias': (0.0, 0.1),
     'L3_conv_b_dw': (0.0, 0.1),
     'L3_conv_ln_w': (1.0, 0.2),
     'L3_conv_ln_b': (0.0, 0.1)}
    factors = {'L0_conv_qkv_w': 2.954, 'L0_conv_rpb': 58.308}
    for name, (base, spread) in spreads.items():
        noise = np.random.default_rng([zlib.crc32(name.encode()), seed]).standard_normal(out[name].shape)
        drawn = base * np.exp(spread * noise) if base else spread * noise
        out[name] = jnp.asarray(drawn.astype(out[name].dtype))
    for name, factor in factors.items():
        out[name] = (out[name] * factor).astype(out[name].dtype)
    return out
```

```python
import numpy as np
from contextlib import ExitStack

import concourse.bass as bass
from concourse import mybir
from concourse.alu_op_type import AluOpType as ALU

F32 = mybir.dt.float32
BF16 = mybir.dt.bfloat16
ACT = mybir.ActivationFunctionType
AX = mybir.AxisListType

B, C, IMG = 16, 48, 16
HEADS, HD, BLOCKS, MLP = 6, 8, 6, 192
N = 64
STREAMS = 2
CHUNK_B = 2
GROUPS = B // (STREAMS * CHUNK_B)
TOK = CHUNK_B * IMG * IMG
TILES = TOK // 128
PAIRS = 4
SC = HEADS * N
KA = C + 1
ZW = 65
HP = HEADS // 2
PADW = IMG + 2
EPS = 1e-5

W_QK, W_V, W_PROJ, W_FC1, W_FC2, W_GB, W_PB, W_B2 = np.cumsum([0, 384, 48, 48, 192, 96, 4, 48])
W_COLS = int(W_B2) + 48

V_PROJ, V_FC1, V_FC2, V_GB, V_F1B, V_PB, V_B2 = (int(n) for n in np.cumsum([0, 96, 2 * 192, 96, 4, 2, 48]))
L1_COLS = V_B2 + 48
DIN, HB = 96, 8 * 256
Q_XD, Q_OUT, Q_ONE, Q_BDW, Q_LN, Q_GRN, Q_WM, Q_MASK = (int(n) for n in np.cumsum([0, 128, 48, 96, 1, 2, 2, 4]))
L3_COLS = Q_MASK + 3
U_W1, U_W2, U_BN, U_B2, U_BIAS = (int(n) for n in np.cumsum([0, 64, 4 * 112, 4, 4]))
L2_COLS = U_BIAS + 1


M_MEAN, M_VAR, M_RT, M_SPREAD, M_GM, M_OUT, M_ALL = (int(n) for n in np.cumsum([0, 4, 1, 1, 4, 1, 4]))
D_YC, D_VAR, D_RT, D_YN, D_V2, D_ALL = (int(n) for n in np.cumsum([0, 4, 1, 1, 4, 8]))


class Step:
    pass


def blocks_of(shifted, u):
    if not shifted:
        return slice(2 * u, 2 * u + 2)
    return slice(1, 3) if u == 0 else slice(0, 4, 3)


def window_pieces(shifted):
    for p in range(PAIRS):
        ys, xs = blocks_of(shifted, p // 2), blocks_of(shifted, p % 2)
        wide = xs.step is None
        for b in ((slice(0, CHUNK_B),) if wide else (slice(0, 1), slice(1, 2))):
            yield slice(128 * p + N * b.start, 128 * p + N * b.stop), b, ys, xs


def build(nc, x_tok, wpack, rpb_raw, mask_in, ident_in, ident2_in, en_in, fn_in,
          conv_in, sed_in, sign_in, l1_in, l2_in,
          front_in, taps_in, gates_in, l3_in, spread_in, out):
    with ExitStack() as ctx:

        def sb(name, shape, dt=F32):
            return ctx.enter_context(nc.sbuf_tensor(name, shape, dt))

        l01_memory, l0_memory, l1_memory = (ctx.enter_context(ExitStack()) for _ in range(3))

        def l01(name, shape, dt=F32):
            return l01_memory.enter_context(nc.sbuf_tensor(name, shape, dt))

        def l1(name, shape, dt=F32):
            return l1_memory.enter_context(nc.sbuf_tensor(name, shape, dt))

        def l0(name, shape, dt=F32):
            return l0_memory.enter_context(nc.sbuf_tensor(name, shape, dt))

        def sem(name):
            return ctx.enter_context(nc.semaphore(name))

        def sems(name, n):
            return [sem(f"{name}{i}") for i in range(n)]

        bank = [[ctx.enter_context(nc.psum_tensor(f"bank{s}{i}", [128, 512], F32)) for i in range(4)]
                for s in range(STREAMS)]
        ident = sb("ident", [128, 128])
        ident2 = sb("ident2", [128, 128], BF16)
        a2 = sb("a2", [64 + C, 8, PADW, PADW])
        front_w = sb("front_w", [64 + C, DIN])
        taps_w = sb("taps_w", [64 + C, 9, DIN])
        gates_w = sb("gates_w", [128, 6 * 4 * DIN], BF16)
        l3w = sb("l3w", [128, L3_COLS])
        spread = sb("spread", [16, 16, DIN])
        l2w = sb("l2w", [128, L2_COLS])
        neg_half8 = sb("neg_half8", [128, 16])
        half8 = sb("half8", [128, 8])

        sed_w = l01("sed_w", [128, 16 * SC])
        rpb_sb = sed_w[:, 0:15 * SC].rearrange("p (t c) -> p t c", c=SC)
        ypad = l01("ypad", [64 + C, B, PADW, PADW])
        conv_w = l01("conv_w", [64 + C, 6, C])
        signs = l01("signs", [96, 128])
        l1w = l01("l1w", [128, L1_COLS])

        en_gb = l0("en_gb", [128, 2, C])
        fn_gb = l0("fn_gb", [KA, 2])
        neg_half = l0("neg_half", [128, 4])
        wts = [l0(f"wts{i}", [128, W_COLS]) for i in range(2)]
        bias_hm = l0("bias_hm", [128, 15, SC], BF16)
        bias_lm = l0("bias_lm", [128, 15, SC], BF16)
        st = []
        for s in range(STREAMS):
            t = Step()
            t.bank = bank[s]
            t.xin = l0(f"xin{s}", [128, TILES, C])
            t.x = l0(f"x{s}", [128, TILES, C])
            t.xc = l0(f"xc{s}", [128, TILES, C])
            t.sq = l0(f"sq{s}", [128, TILES, C])
            t.z = l0(f"z{s}", [128, TILES, ZW])
            t.s4 = l0(f"s4{s}", [128, 4, TILES])
            t.xT = l0(f"xT{s}", [KA, TOK])
            t.q0, t.k0 = l0(f"q0{s}", [128, TOK]), l0(f"k0{s}", [128, TOK])
            t.q1, t.k1 = l0(f"q1{s}", [64, TOK]), l0(f"k1{s}", [64, TOK])
            t.mx = l0(f"mx{s}", [128, 4, 2, PAIRS])
            t.d = l0(f"d{s}", [128, HP, PAIRS, 2 * N])
            t.pt = l0(f"pt{s}", [128, HP, PAIRS, 128])
            t.v = l0(f"v{s}", [128, 2 * PAIRS, 432])
            t.rd = l0(f"rd{s}", [C, TOK])
            t.oT = l0(f"oT{s}", [C, TOK])
            t.g = l0(f"g{s}", [96, 2, TOK])
            st.append(t)
        l0_memory.close()

        y2 = l1("y2", [C, 16, 256])
        x1 = l1("wx", [128, 2, 16, C])
        xc1, sq1, z1 = l1("wxc", [128, 2, 16, C]), l1("wsq", [128, 2, 16, C]), l1("wz", [128, 2, 16, C])
        st1 = l1("st1", [128, 4, 4, 8])
        xs = l1("xs", [96, 8, 256])
        hs = l1("sed_h", [96, 8, 256])
        g1 = l1("hid1", [96, 4, 2048])
        x2 = l1("x2", [64 + C, 8, IMG, PADW])
        pooled = l1("pooled", [64 + C, 8])
        t2 = l1("t2", [64, 4, 8])
        wt2 = l1("wt2", [64 + C, 4, 8])
        graw = l1("graw", [128, 6 * 4 * DIN])
        gpart = [l1(f"gpart{i}", [128, 6 * 4 * DIN], BF16) for i in range(3)]
        l1_memory.close()
        l01_memory.close()

        x3 = sb("x3", [DIN, B, 256])
        xb = sb("xb", [128, 8, 512], BF16)
        rest3 = [sb(f"rest3{i}", [128, 512]) for i in range(2)]
        mid3 = sb("mid3", [128, 512], BF16)
        gate = [[sb(f"gate{i}{k}", [DIN, HB]) for k in range(3)] for i in range(2)]
        mag = [sb(f"mag{k}", [DIN, HB]) for k in range(2)]
        gsum = [sb(f"gsum{i}", [DIN, HB]) for i in range(2)]
        lx = sb("lx", [DIN, HB])
        xd = sb("xd", [DIN, HB])
        hst = sb("hst", [DIN, 8, PADW, IMG])
        tmp = [sb(f"tmp{i}", [DIN, 256]) for i in range(3)]
        ysum = [sb(f"ysum{i}", [DIN, HB]) for i in range(2)]
        yc, yq = sb("yc", [DIN, HB]), sb("yq", [DIN, HB])
        tvar = sb("tvar", [128, 2, 16])
        rT = sb("rT", [16, 128])
        gx = sb("gx", [DIN, 6, 8])
        ob = sb("ob", [C, 8, 256])

        ld_const, ld_x, ld_w = sem("ld_const"), sems("ld_x", 2), sems("ld_w", 2)
        setup = sem("setup")
        split = sem("split")
        x_used = sems("x_used", 2)
        en = sems("en", 8)
        fin = sems("fin", 7)
        ln1, ln2 = sems("ln1_", 7), sems("ln2_", 7)
        pe_zT, pe_qk, pe_v, pe_S, pe_PT = sem("pe_zT"), sems("pe_qk", 3), sem("pe_v"), sems("pe_S", 4), sems("pe_PT", 4)
        pe_O, pe_proj, pe_z2T, pe_fc1, pe_fc2 = sem("pe_O"), sem("pe_proj"), sem("pe_z2T"), sems("pe_fc1", 2), sem("pe_fc2")
        pe_fin = sem("pe_fin")
        xT_ready, xT2_ready, qk_ready, v_ready = sem("xT_ready"), sem("xT2_ready"), sems("qk_ready", 3), sem("v_ready")
        mx_ready, d_ready, p_ready, pt_ready = sems("mx_ready", 4), sems("d_ready", 4), sems("p_ready", 4), sems("pt_ready", 4)
        rd_ready, o_ready, x1_ready, x2_ready, g_ready = sem("rd_ready"), sem("o_ready"), sem("x1_ready"), sem("x2_ready"), sems("g_ready", 2)
        pb_added, b2_added, y_ready = sem("pb_added"), sem("b2_added"), sem("y_ready")
        stored = sem("stored")
        ld_sed, sed_ready, ld_late, conv_ready, y_copied, late_set = (sem(n) for n in (
            "ld_sed", "sed_ready", "ld_late", "conv_ready", "y_copied", "late_set"))
        conv_done, conv_a, conv_d, back_done = sem("conv_done"), sem("conv_a"), sem("conv_d"), sem("back_done")
        var_ready, rstd_ready, norm_ready, zT_done, xs_ready, bias_added = (sem(n) for n in (
            "var_ready", "rstd_ready", "norm_ready", "zT_done", "xs_ready", "bias_added"))
        dve_step, sed_done, h_ready, proj1_done, fc1_done, g1_ready, fc2_done, x1_final = (sem(n) for n in (
            "dve_step", "sed_done", "h_ready", "proj1_done", "fc1_done", "g1_ready", "fc2_done", "x1_final"))
        x2T_done, x2_a, x2_d, pooled_ready, t_done, t_ready, wt_done, bn_ready, a_ready = (sem(n) for n in (
            "x2T_done", "x2_a", "x2_d", "pooled_ready", "t_done", "t_ready", "wt_done", "bn_ready", "a_ready"))
        ld_gates = sem("ld_gates")
        x3_done, x3_ready, px_done, px_hi, px_left, xb_ready = (sem(n) for n in (
            "x3_done", "x3_ready", "px_done", "px_hi", "px_left", "xb_ready"))
        gate_done, gate_taken = sems("gate_done", 3), sems("gate_taken", 3)
        l_done, l_taken, d_done, d_taken, u_done, u_taken = (sem(n) for n in (
            "l_done", "l_taken", "d_done", "d_taken", "u_done", "u_taken"))
        low_ready, sum_ready, scan_done, y_added, recip_done, all_ready = (sem(n) for n in (
            "low_ready", "sum_ready", "scan_done", "y_added", "recip_done", "all_ready"))
        tail_pe, tail_dve = sem("tail_pe"), sem("tail_dve")
        yq_ready, trstd_ready, v_norm, gx2_ready, gx_ready, out_ready = (
            sem(n) for n in ("yq_ready", "trstd_ready", "v_norm", "gx2_ready", "gx_ready", "out_ready"))

        block = ctx.enter_context(nc.Block())

        def group_value(eng, v, s, k):
            return k * ((v - s + 1) // 2) if isinstance(v, int) else eng.snap((v + (1 - s)) // 2 * k)

        def pipeline(eng, slot, first, last):
            def step(n, v, lp, wv, **kw):
                o = Step()
                o.t, o.par, o.v, o.lp, o.wv = st[n % 2], n // 2 % 2, v, lp, wv
                o.first, o.before = kw.get("first"), kw.get("before")
                return o

            if first:
                first(0, 1)
            slot(step(0, 1, 0, 16, first=1 if first else None), None)
            with eng.Fori(0, GROUPS) as g:
                ga = [eng.snap(g * 2 + k) for k in (1, 2, 3)]
                start = dict(first=ga[1], before=ga[0])
                if first:
                    first(1, ga[1])
                wg = eng.snap(g * 48 + 16)
                with eng.Fori(0, 2) as lp:
                    vs = [eng.snap(g * 12 + lp * 4 + (k + 1)) for k in range(5)]
                    wv = eng.snap(g * 48 + lp * 16 + 16)
                    wn = eng.snap(g * 48 + lp * 16 + 32)
                    for k in range(1, 5):
                        x = step(k % 4, vs[k], lp if k < 4 else lp + 1, wv if k < 4 else wn, **start if k == 1 else {})
                        slot(x, step(k - 1, vs[k - 1], lp, wv))
                vs = [eng.snap(g * 12 + (8 + k + 1)) for k in range(5)]
                wv, wn = eng.snap(g * 48 + 48), eng.snap(g * 48 + 64)
                for k in range(1, 4):
                    slot(step(k, vs[k], 2, wv), step(k - 1, vs[k - 1], 2, wv))
                last(0, ga[0])
                if first:
                    first(0, ga[2])
                slot(step(0, vs[4], 0, wn, first=ga[2], before=ga[1]), step(3, vs[3], 2, wv))
                last(1, ga[1])

        def tokens(ap):
            return ap.rearrange("p (b y x i) -> p b y x i", b=CHUNK_B, y=4, x=4)

        def chunk(t, n):
            return t[:, n % 2, 8 * (n // 2):8 * (n // 2) + 8, :]

        B8 = bank[0] + bank[1]

        def x2_rows(k):
            h, iy = k % 2, k // 2
            v = x2[64 * h:64 * h + C].rearrange("p b (y j) x -> p (b y) j x", j=4)
            return v[:, :, iy, 1:1 + IMG].rearrange("p y (x i) -> p y x i", i=4)

        def window_view(ap, b, ys, xs):
            if xs.step is None:
                v = ap.rearrange("p (b y i) -> p b y i", b=CHUNK_B, y=4)
                return v[:, b, ys, 16 * xs.start:16 * xs.stop]
            return tokens(ap)[:, b, ys, xs, :]

        @block.sync
        def _(sp):
            for dst, src in ((ident[:], ident_in), (ident2[:], ident2_in), (rpb_sb[0:64], rpb_raw),
                             (rpb_sb[64:128], rpb_raw), (bias_lm[64:128], mask_in), (en_gb[:], en_in),
                             (fn_gb[:], fn_in)):
                sp.dma_start(dst, src).then_inc(ld_const, 16)
            for s in range(STREAMS):
                sp.dma_start(st[s].xin[:], x_tok[s]).then_inc(ld_x[s], 16)
            for dst, src in ((conv_w[:], conv_in), (l1w[:], l1_in), (l2w[:], l2_in), (front_w[:], front_in),
                             (taps_w[:], taps_in), (l3w[:], l3_in), (spread[:], spread_in)):
                sp.dma_start(dst, src).then_inc(ld_late, 16)
            for par in range(2):
                sp.dma_start(wts[par][:], wpack[par]).then_inc(ld_w[par], 16)
            def reload(par, nxt, done):
                sp.wait_ge(pe_fc2, done)
                sp.wait_ge(b2_added, done)
                sp.dma_start(wts[par][:], nxt).then_inc(ld_w[par], 16)

            sp.wait_ge(split, 5)
            sp.dma_start(sed_w[0:96, :], sed_in).then_inc(ld_sed, 16)
            sp.dma_start(signs[:], sign_in).then_inc(ld_sed, 16)
            with sp.Fori(0, GROUPS) as g:
                sp.wait_ge(x_used[0], g + 1)
                sp.dma_start(st[0].xin[:], x_tok[bass.ds(g * STREAMS + 2, 1)].rearrange("a p t c -> (a p) t c")).then_inc(ld_x[0], 16)
                sp.wait_ge(x_used[1], g + 1)
                sp.dma_start(st[1].xin[:], x_tok[bass.ds(g * STREAMS + 3, 1)].rearrange("a p t c -> (a p) t c")).then_inc(ld_x[1], 16)
                with sp.Fori(0, BLOCKS // 2) as lp:
                    for par in range(2):
                        reload(par, wpack[bass.ds(lp * 2 + (2 + par), 1)].rearrange("a p c -> (a p) c"),
                               sp.snap(g * 12 + lp * 4 + (2 * par + 2)))
            for s in range(STREAMS):
                sp.wait_ge(ld_x[s], 16 * (GROUPS + 1))
            for par in range(2):
                sp.wait_ge(ld_w[par], 16 * (GROUPS * 3 + 1))
            sp.wait_ge(y_copied, 8)
            sp.wait_ge(fin[5], 8)
            sp.dma_start(graw[:], gates_in).then_inc(ld_gates, 16)
            for hb in range(2):
                for e in range(4):
                    sp.wait_ge(out_ready, 4 * hb + e + 1)
                    sp.dma_start(out[8 * hb + 2 * e:8 * hb + 2 * e + 2].rearrange("b c y x -> c b (y x)"),
                                 ob[:, 2 * e:2 * e + 2, :]).then_inc(stored, 16)
            sp.wait_ge(stored, 16 * 8)

        @block.gpsimd
        def _(pool):
            pool.memset(neg_half[:], -0.5).then_inc(setup, 1)
            pool.memset(ypad[:], 0.0).then_inc(y_ready, 1)
            for s in range(STREAMS):
                pool.memset(st[s].z[:, :, C:ZW], 1.0).then_inc(setup if s else pe_fin, 1)
                pool.memset(st[s].v[:], 0.0).then_inc(setup, 1)
            pool.wait_ge(setup, 2 * STREAMS)
            for s in range(STREAMS):
                v = st[s].v[:].rearrange("p w (h c) -> p w h c", h=3)
                for r in range(2):
                    pool.memset(v[64 * r:64 * r + 64, :, :, 64 + 8 * r:72 + 8 * r], 1.0).then_inc(setup, 1)

            def rstd(t, chain, v):
                pool.wait_ge(chain[3], v)
                pool.tensor_tensor(t.s4[:, 3, :], t.s4[:, 2, :], neg_half[:], ALU.pow).then_inc(chain[4], 1)

            def bcast(ap):
                return ap.unsqueeze(1).to_broadcast([128, TILES, C])

            def add_bias(t, col, chain, done, v, w):
                pool.wait_ge(chain[5], v)
                pool.tensor_tensor(t.x[:], t.x[:], bcast(w[:, col:col + C]), ALU.add).then_inc(done, 1)

            def slot(x, y):
                if x:
                    rstd(x.t, ln1, x.v)
                    pool.wait_ge(ld_w[x.par], x.wv)
                    add_bias(x.t, W_PB, ln1, pb_added, x.v, wts[x.par])
                if y:
                    rstd(y.t, ln2, y.v)
                    add_bias(y.t, W_B2, ln2, b2_added, y.v, wts[y.par])

            def last(s, v):
                rstd(st[s], fin, v)
                pool.wait_ge(y_ready, pool.snap(v + 1))
                imgs = bass.ds(v * CHUNK_B - CHUNK_B, CHUNK_B)
                pool.tensor_copy(ypad[64:64 + C, imgs, 0:PADW - 1, :], ypad[0:C, imgs, 1:PADW, :]).then_inc(y_copied, 1)
                pool.wait_ge(y_copied, v)

            pool.wait_ge(setup, 4 * STREAMS)
            pool.wait_ge(ld_sed, 32)
            sw = sed_w[0:96, :].rearrange("p (k e) -> p k e", e=C)
            pool.tensor_tensor(sw, sw, signs[:].unsqueeze(2).to_broadcast([96, 128, C]), ALU.mult).then_inc(sed_ready, 1)
            pool.wait_ge(sed_ready, 1)
            pipeline(pool, slot, lambda s, v: rstd(st[s], en, v), last)

            pool.wait_ge(y_ready, 9)
            pool.wait_ge(fin[5], 8)
            pool.wait_ge(pe_fin, 9)
            for k in range(2):
                pool.wait_ge(ld_w[k], 16 * (GROUPS * 3 + 1))
                pool.wait_ge(ld_x[k], 16 * (GROUPS + 1))
            pool.wait_ge(ld_late, 16 * 7)
            pool.memset(neg_half8[:], -0.5).then_inc(late_set, 1)
            pool.memset(half8[:], 0.5).then_inc(late_set, 1)
            pool.memset(x2[:], 0.0).then_inc(late_set, 1)
            pool.memset(a2[:], 0.0).then_inc(late_set, 1)
            pool.wait_ge(late_set, 4)

            def bcast8(ap):
                return ap.unsqueeze(1).to_broadcast([128, 8, C])

            for k, col in enumerate((V_PB, V_B2)):
                for n in range(4):
                    pool.wait_ge(var_ready, 4 * k + n + 1)
                    pool.tensor_tensor(st1[:, n, 3], st1[:, n, 2], neg_half8[:, 0:8], ALU.pow).then_inc(rstd_ready, 1)
                    pool.tensor_tensor(chunk(x1, n), chunk(x1, n), bcast8(l1w[:, col:col + C]), ALU.add).then_inc(bias_added, 1)

            bn_var = l2w[0:64, U_BN + 3:U_BN + 4]
            pool.tensor_scalar(bn_var, bn_var, EPS, None, ALU.add).then_inc(bn_ready, 1)
            pool.wait_ge(bn_ready, 1)
            pool.tensor_tensor(bn_var, bn_var, neg_half8[0:64, 0:1],
                               ALU.pow).then_inc(bn_ready, 1)

            pool.wait_ge(a_ready, 32)
            pool.memset(hst[:], 0.0).then_inc(late_set, 1)
            for u in range(8):
                pool.wait_ge(gate_taken[1], 4 * u + 4)
                pool.wait_ge(gate_taken[2], 4 * u + 4)
                pool.tensor_tensor(mag[0][:], mag[0][:], mag[1][:], ALU.add).then_inc(sum_ready, 1)
                y, d = ysum[u // 4], u % 4
                pool.wait_ge(d_taken, 4 * u + 4)
                if d:
                    pool.wait_ge(y_added, 2 * u)
                    pool.tensor_tensor(y[:], y[:], xd[:], ALU.add).then_inc(y_added, 1)
                    pool.wait_ge(y_added, 2 * u + 1)
                    pool.wait_ge(u_taken, 4 * u + 4)
                    pool.tensor_tensor(y[:], y[:], gsum[u % 2][:], ALU.add).then_inc(y_added, 1)
                else:
                    pool.wait_ge(u_taken, 4 * u + 4)
                    pool.tensor_tensor(y[:], xd[:], gsum[u % 2][:], ALU.add).then_inc(y_added, 2)
                if u in (4, 7):
                    hb = u // 7
                    pool.wait_ge(tail_dve, D_ALL * hb + D_VAR + 1)
                    pool.tensor_tensor(tvar[:, 1], tvar[:, 0], neg_half8[:], ALU.pow).then_inc(trstd_ready, 1)
                    pool.wait_ge(gx2_ready, 8 * hb + 8)
                    pool.tensor_tensor(gx[:, 1], gx[:, 0], half8[0:DIN], ALU.pow).then_inc(gx_ready, 1)

        @block.vector
        def _(dve):
            dve.wait_ge(ld_const, 16 * 7)
            hi = bias_hm
            rest = rpb_sb
            dve.tensor_copy(hi[:], rpb_sb[:]).then_inc(split, 1)
            dve.wait_ge(split, 1)
            dve.tensor_tensor(rest[:], rpb_sb[:], hi[:], ALU.subtract).then_inc(split, 1)
            dve.wait_ge(split, 2)
            dve.tensor_copy(bias_hm[64:128], rest[64:128]).then_inc(split, 1)
            dve.tensor_copy(bias_lm[0:64], rest[0:64]).then_inc(split, 1)
            dve.wait_ge(split, 4)
            dve.tensor_tensor(bias_lm[0:64], rest[0:64], bias_lm[0:64], ALU.subtract).then_inc(split, 1)

            dve.wait_ge(ld_late, 16 * 7)
            dve.tensor_tensor(conv_w[64:64 + C, 1, :], conv_w[64:64 + C, 1, :], ident[64:64 + C, 64:64 + C], ALU.add).then_inc(conv_ready, 1)

            def norm(t, src, dst, chain, v):
                dve.tensor_reduce(t.s4[:, 0, :], src[:], AX.X, ALU.add).then_inc(chain[0], 1)
                dve.wait_ge(chain[0], v)
                dve.scalar_tensor_tensor(t.xc[:], t.s4[:, 0, :].unsqueeze(2).to_broadcast([128, TILES, C]), -1.0 / C,
                                         src[:], ALU.mult, ALU.add).then_inc(chain[1], 1)
                dve.wait_ge(chain[1], v)
                dve.tensor_tensor(t.sq[:], t.xc[:], t.xc[:], ALU.mult).then_inc(chain[2], 1)
                dve.wait_ge(chain[2], v)
                dve.tensor_reduce(t.s4[:, 1, :], t.sq[:], AX.X, ALU.add).then_inc(chain[6], 1)
                dve.wait_ge(chain[6], v)
                dve.tensor_scalar(t.s4[:, 2, :], t.s4[:, 1, :], 1.0 / C, EPS, ALU.mult, ALU.add).then_inc(chain[3], 1)
                dve.wait_ge(chain[4], v)
                dve.tensor_tensor(dst[:, :, 0:C], t.xc[:], t.s4[:, 3, :].unsqueeze(2).to_broadcast([128, TILES, C]),
                                  ALU.mult).then_inc(chain[5], 1)

            def take_v(t, v):
                dve.wait_ge(pe_v, v)
                src = t.bank[1][:, 0:PAIRS * C].rearrange("p (q h c) -> p q h c", q=PAIRS, h=3)
                dst = t.v[:].rearrange("p (q w) (h c) -> p q w h c", q=PAIRS, h=3)
                for w in range(2):
                    for r in range(2):
                        op = dve.tensor_copy(dst[64 * r:64 * r + 64, :, w, :, 8 * r:8 * r + 8],
                                             src[64 * w:64 * w + 64, :, :, 8 * r:8 * r + 8])
                op.then_inc(v_ready, 1)

            def center(t, j, v):
                hs = 2 if j < 2 else 1
                dve.wait_ge(pe_S[j], v)
                s = t.bank[j][:, 0:hs * 4 * N].rearrange("p (h q m) -> p h q m", h=hs, q=PAIRS)
                mx = t.mx[:, j, 0:hs, :]
                dve.tensor_reduce(mx, s, AX.X, ALU.max).then_inc(mx_ready[j], 1)
                dve.wait_ge(mx_ready[j], v)
                d = t.d[:, min(j, 2)].rearrange("p q (h m) -> p h q m", h=2)
                r = 0 if j < 3 else 1
                dve.tensor_tensor(d[:, r:r + hs], s, mx.unsqueeze(3).to_broadcast([128, hs, PAIRS, N]),
                                  ALU.subtract).then_inc(d_ready[j], 1)

            def take_o(t, shifted, v):
                dve.wait_ge(pe_O, v)
                dve.reciprocal(t.rd[:], t.bank[3][64:64 + C, :]).then_inc(rd_ready, 1)
                dve.wait_ge(rd_ready, v)
                for cols, b, ys, xs in window_pieces(shifted):
                    dst = window_view(t.oT[:], b, ys, xs)
                    like = "p (b y i) -> p b y i" if xs.step is None else "p (b y x i) -> p b y x i"
                    dims = dict(y=2, i=32) if xs.step is None else dict(y=2, x=2, i=16)
                    op = dve.tensor_tensor(dst, t.bank[3][0:C, cols].rearrange(like, **dims),
                                           t.rd[:, cols].rearrange(like, **dims), ALU.mult)
                op.then_inc(o_ready, 1)

            def add_res(t, bk, pe_done, bias_done, ready, v):
                dve.wait_ge(pe_done, v)
                dve.wait_ge(bias_done, v)
                dve.tensor_tensor(t.x[:], bk[:, 0:TILES * C].rearrange("p (t c) -> p t c", t=TILES), t.x[:],
                                  ALU.add).then_inc(ready, 1)
                dve.wait_ge(ready, v)

            def first(s, v):
                t = st[s]
                dve.wait_ge(ld_x[s], group_value(dve, v, s, 16))
                norm(t, t.xin, t.x, en, v)
                dve.wait_ge(en[5], v)
                gb = en_gb[:].unsqueeze(2).to_broadcast([128, 2, TILES, C])
                dve.tensor_tensor(t.x[:], t.x[:], gb[:, 0], ALU.mult).then_inc(x_used[s], 1)
                dve.wait_ge(x_used[s], group_value(dve, v, s, 1))
                dve.tensor_tensor(t.x[:], t.x[:], gb[:, 1], ALU.add).then_inc(en[7], 1)

            def last(s, v):
                norm(st[s], st[s].x, st[s].z, fin, v)

            def slot(x, y):
                if x:
                    if x.first is not None:
                        dve.wait_ge(en[7], x.first)
                        if x.before is not None:
                            dve.wait_ge(pe_fin, x.before)
                    norm(x.t, x.t.x, x.t.z, ln1, x.v)
                if y:
                    take_o(y.t, y.par == 1, y.v)
                if x:
                    take_v(x.t, x.v)
                if y:
                    add_res(y.t, y.t.bank[0], pe_proj, pb_added, x1_ready, y.v)
                    norm(y.t, y.t.x, y.t.z, ln2, y.v)
                if x:
                    for j in (2, 3, 0, 1):
                        center(x.t, j, x.v)
                if y:
                    add_res(y.t, y.t.bank[0], pe_fc2, b2_added, x2_ready, y.v)

            dve.wait_ge(setup, 4 * STREAMS)
            pipeline(dve, slot, first, last)

            dve.wait_ge(y_ready, 9)
            dve.wait_ge(pe_fin, 9)
            for k in range(2):
                dve.wait_ge(ld_w[k], 16 * (GROUPS * 3 + 1))
                dve.wait_ge(ld_x[k], 16 * (GROUPS + 1))
            dve.wait_ge(y_copied, 8)
            chain = [0]

            def step(op):
                chain[0] += 1
                op.then_inc(dve_step, 1)
                dve.wait_ge(dve_step, chain[0])

            step(dve.tensor_tensor(taps_w[:], taps_w[:], front_w[:].unsqueeze(1).to_broadcast([64 + C, 9, DIN]), ALU.mult))
            dve.wait_ge(ld_gates, 16)
            for g in (4, 5):
                cols = graw[:, g * 4 * DIN:(g + 1) * 4 * DIN].rearrange("p (d c) -> p d c", d=4)
                step(dve.tensor_tensor(cols, cols, l3w[:, Q_WM:Q_WM + 4].unsqueeze(2).to_broadcast([128, 4, DIN]), ALU.mult))
            for k in range(3):
                step(dve.tensor_copy(gpart[k][:], graw[:]))
                if k < 2:
                    step(dve.tensor_tensor(graw[:], graw[:], gpart[k][:], ALU.subtract))
            step(dve.tensor_scalar(gates_w[:], gpart[0][:], l3w[:, Q_MASK:Q_MASK + 1], None, ALU.mult))
            for k in (1, 2):
                step(dve.scalar_tensor_tensor(gates_w[:], gpart[k][:], l3w[:, Q_MASK + k:Q_MASK + k + 1], gates_w[:],
                                              ALU.mult, ALU.add))
            for t in (1, 3, 5, 7):
                dve.wait_ge(conv_done, t + 1)
                dve.tensor_copy(y2[:, 2 * t:2 * t + 2, :].rearrange("p i w -> p (i w)"), B8[t][0:C, :]).then_inc(conv_d, 1)

            def b8(ap):
                return ap.unsqueeze(2).to_broadcast([128, 8, C])

            def half_norms(k, source):
                for n in range(4):
                    source(n)
                    x, xc, sq = chunk(x1, n), chunk(xc1, n), chunk(sq1, n)
                    step(dve.tensor_reduce(st1[:, n, 0], x, AX.X, ALU.add))
                    step(dve.scalar_tensor_tensor(xc, b8(st1[:, n, 0]), -1.0 / C, x, ALU.mult, ALU.add))
                    step(dve.tensor_tensor(sq, xc, xc, ALU.mult))
                    step(dve.tensor_reduce(st1[:, n, 1], sq, AX.X, ALU.add))
                    dve.tensor_scalar(st1[:, n, 2], st1[:, n, 1], 1.0 / C, EPS, ALU.mult, ALU.add).then_inc(var_ready, 1)
                for n in range(4):
                    dve.wait_ge(rstd_ready, 4 * k + n + 1)
                    dve.tensor_tensor(chunk(z1, n), chunk(xc1, n), b8(st1[:, n, 3]), ALU.mult).then_inc(norm_ready, 1)

            def take_conv(n):
                dve.wait_ge(back_done, n + 1)
                step(dve.tensor_copy(chunk(x1, n), B8[n][:, 0:8 * C].rearrange("p (i c) -> p i c", c=C)))

            def add_back(n, bk, done, k, final=None):
                dve.wait_ge(done, 1 + n // 2)
                dve.wait_ge(bias_added, 4 * k + n + 1)
                op = dve.tensor_tensor(chunk(x1, n), B8[bk + n][:, 0:8 * C].rearrange("p (i c) -> p i c", c=C),
                                       chunk(x1, n), ALU.add)
                op.then_inc(final, 1) if final else step(op)

            half_norms(0, take_conv)
            half_norms(1, lambda n: add_back(n, 4, proj1_done, 0))
            for n in range(4):
                add_back(n, 0, fc2_done, 1, x1_final)

            for k in (1, 3, 5, 7):
                dve.wait_ge(x2T_done, k + 1)
                dve.tensor_copy(x2_rows(k), B8[(4 + k) % 8][0:C, :].rearrange("p (i y x) -> p y x i", i=4, x=4)).then_inc(x2_d, 1)
            dve.wait_ge(x2_a, 4)
            dve.wait_ge(x2_d, 4)
            dve.tensor_reduce(pooled[:], x2[:, :, :, 1:1 + IMG], AX.XY, ALU.add).then_inc(pooled_ready, 1)
            dve.wait_ge(bn_ready, 2)
            bn = [l2w[0:64, U_BN + k:U_BN + k + 1] for k in range(4)]
            step(dve.tensor_tensor(bn[0], bn[0], bn[3], ALU.mult))
            dve.wait_ge(t_done, 1)
            step(dve.tensor_scalar(t2[:, 0], B8[4][0:64, 0:8], 1.0 / 256, bn[2], ALU.mult, ALU.subtract))
            step(dve.tensor_scalar(t2[:, 1], t2[:, 0], bn[0], bn[1], ALU.mult, ALU.add))
            dve.tensor_scalar(t2[:, 2], t2[:, 1], 0.0, None, ALU.max).then_inc(t_ready, 1)
            dve.wait_ge(wt_done, 1)
            step(dve.tensor_tensor(wt2[:], B8[5][0:112, 0:32].rearrange("p (t b) -> p t b", t=4),
                                   l2w[0:112, U_B2:U_B2 + 4].unsqueeze(2).to_broadcast([112, 4, 8]), ALU.add))
            for n, tap in enumerate((3, 0, 1, 2)):
                for j in range(8):
                    if tap == 3:
                        dve.tensor_scalar(a2[:, j, 1:17, 1:17], x2[:, j, :, 0:16], wt2[:, 3, j:j + 1],
                                          l2w[0:112, U_BIAS:U_BIAS + 1], ALU.mult, ALU.add).then_inc(a_ready, 1)
                    else:
                        if j == 0:
                            dve.wait_ge(a_ready, 8 * n)
                        dve.scalar_tensor_tensor(a2[:, j, 2:17, 1:17], x2[:, j, 0:15, tap:tap + 16], wt2[:, tap, j:j + 1],
                                                 a2[:, j, 2:17, 1:17], ALU.mult, ALU.add).then_inc(a_ready, 1)
            dve.wait_ge(a_ready, 32)

            for e in range(8):
                px, r = B8[4 + e % 4], rest3[e % 2]
                dve.wait_ge(px_hi, e + 1)
                dve.tensor_tensor(r[:], px[:], xb[:, e, :], ALU.subtract).then_inc(px_left, 1)
                dve.wait_ge(px_left, e + 1)
                dve.tensor_copy(xb[32:64, e, :], r[32:64]).then_inc(xb_ready, 1)
                step(dve.tensor_copy(mid3[96:128], r[96:128]))
                dve.tensor_tensor(xb[96:128, e, :], r[96:128], mid3[96:128], ALU.subtract).then_inc(xb_ready, 1)

            def seen(imgs, d):
                v = x3[:, imgs, :].rearrange("p b (y x) -> p b y x", x=IMG)
                if d == 0:
                    return v
                if d == 1:
                    return v.rearrange("p b y x -> p b x y")
                if d == 2:
                    return v[:, :, :, ::-1]
                return v[:, :, ::-1, :].rearrange("p b y x -> p b x y")

            def rows(t, s):
                return t[:].rearrange("p (b k s) -> p b k s", b=8, s=8)[:, :, :, s]

            def state(shift, s):
                v = hst[:, :, 1 + shift:1 + shift + IMG, :]
                return v.rearrange("p b y (n s) -> p b (y n) s", s=8)[:, :, :, s]

            def t8(i):
                return tmp[i][:].rearrange("p (b k) -> p b k", b=8)

            def unit(u):
                hb, d = u // 4, u % 4
                gl, gm, gr = gate[u % 2]
                dve.wait_ge(gate_taken[0], 4 * u + 4)
                if u >= 2:
                    dve.wait_ge(y_added, 2 * u - 2)
                dve.scalar_tensor_tensor(gsum[u % 2][:], gl[:], -1.0, gl[:], ALU.mult, ALU.max).then_inc(low_ready, 1)
                for e in range(4):
                    for bk, dst, done, taken in ((3, lx, l_done, l_taken), (4, xd, d_done, d_taken)):
                        if bk == 4 and e == 0 and u:
                            dve.wait_ge(y_added, 2 * u - 1)
                        dve.wait_ge(done, 4 * u + e + 1)
                        imgs = slice(8 * hb + 2 * e, 8 * hb + 2 * e + 2)
                        dve.tensor_tensor(dst[:, 512 * e:512 * (e + 1)].rearrange("p (b y x) -> p b y x", b=2, y=IMG),
                                          B8[bk][0:DIN, :].rearrange("p (b y x) -> p b y x", b=2, y=IMG),
                                          seen(imgs, d), ALU.mult).then_inc(taken, 1)
                dve.wait_ge(sum_ready, u + 1)
                dve.wait_ge(low_ready, u + 1)
                rgate = gsum[u % 2]
                dve.scalar_tensor_tensor(rgate[:], rgate[:], 1e-7, mag[0][:], ALU.add, ALU.add).then_inc(all_ready, 1)
                dve.wait_ge(all_ready, u + 1)
                dve.reciprocal(rgate[:], rgate[:]).then_inc(recip_done, 1)
                dve.wait_ge(recip_done, u + 1)
                dve.wait_ge(l_taken, 4 * u + 4)
                if u == 0:
                    dve.wait_ge(late_set, 5)
                step(dve.tensor_copy(state(0, 0), rows(lx, 0)))
                for s in range(1, 8):
                    dve.tensor_tensor(t8(0), rows(gl, s), state(-1, s - 1), ALU.mult).then_inc(dve_step, 1)
                    dve.tensor_tensor(t8(1), rows(gm, s), state(0, s - 1), ALU.mult).then_inc(dve_step, 1)
                    dve.tensor_tensor(t8(2), rows(gr, s), state(1, s - 1), ALU.mult).then_inc(dve_step, 1)
                    dve.wait_ge(dve_step, chain[0] + 2)
                    chain[0] += 3
                    step(dve.tensor_tensor(t8(0), t8(0), t8(1), ALU.add))
                    step(dve.tensor_tensor(t8(0), t8(0), t8(2), ALU.add))
                    step(dve.tensor_tensor(t8(0), t8(0), rows(rgate, s), ALU.mult))
                    op = dve.tensor_tensor(state(0, s), t8(0), rows(lx, s), ALU.add)
                    if s < 7:
                        step(op)
                    else:
                        op.then_inc(scan_done, 1)
                dve.wait_ge(scan_done, u + 1)
                for e in range(4):
                    dve.wait_ge(u_done, 4 * u + e + 1)
                    dve.tensor_tensor(gsum[u % 2][:, 512 * e:512 * (e + 1)].rearrange("p (b k) -> p b k", b=2),
                                      B8[5][0:DIN, :].rearrange("p (b k) -> p b k", b=2),
                                      hst[:, 2 * e:2 * e + 2, 1:1 + IMG, :].rearrange("p b y x -> p b (y x)"),
                                      ALU.mult).then_inc(u_taken, 1)
                dve.wait_ge(u_taken, 4 * u + 4)

            def tail(hb):
                dve.wait_ge(y_added, 8 * hb + 8)
                for e in range(4):
                    cols = slice(512 * e, 512 * (e + 1))
                    dve.wait_ge(tail_pe, M_ALL * hb + M_MEAN + e + 1)
                    dve.scalar_tensor_tensor(yc[:, cols], B8[6 + e % 2][0:DIN, :], -1.0 / DIN, ysum[hb][:, cols],
                                             ALU.mult, ALU.add).then_inc(tail_dve, 1)
                dve.wait_ge(tail_pe, M_ALL * hb + M_VAR + 1)
                dve.tensor_scalar(tvar[:, 0], B8[6][:, 0:16], 1.0 / DIN, EPS, ALU.mult, ALU.add).then_inc(tail_dve, 1)
                dve.wait_ge(tail_pe, M_ALL * hb + M_RT + 1)
                dve.tensor_copy(rT[:], B8[7][0:16, 0:128]).then_inc(tail_dve, 1)
                for e in range(4):
                    cols = slice(512 * e, 512 * (e + 1))
                    dve.wait_ge(tail_pe, M_ALL * hb + M_SPREAD + e + 1)
                    dve.tensor_tensor(yq[:, cols], B8[6 + e % 2][0:DIN, :], yc[:, cols], ALU.mult).then_inc(tail_dve, 1)
                dve.wait_ge(tail_pe, M_ALL * hb + M_GM + 1)
                step(dve.tensor_scalar(gx[:, 2], B8[6][0:DIN, 0:8], 1.0 / DIN, 1e-6, ALU.mult, ALU.add))
                step(dve.reciprocal(gx[:, 3], gx[:, 2]))
                step(dve.tensor_tensor(gx[:, 4], gx[:, 1], gx[:, 3], ALU.mult))
                step(dve.tensor_scalar(gx[:, 5], gx[:, 4], l3w[0:DIN, Q_GRN:Q_GRN + 1], 1.0, ALU.mult, ALU.add))
                for b in range(8):
                    cols = slice(256 * b, 256 * (b + 1))
                    dve.tensor_scalar(yq[:, cols], yc[:, cols], gx[:, 5, b:b + 1], l3w[0:DIN, Q_GRN + 1:Q_GRN + 2],
                                      ALU.mult, ALU.add).then_inc(tail_dve, 1)

            for u in range(8):
                unit(u)
                if u == 4:
                    tail(0)
            tail(1)

        @block.scalar
        def _(act):
            def affine_windows(t, shifted, v, w):
                act.wait_ge(pe_zT, v)
                for cols, b, ys, xs in window_pieces(shifted):
                    op = act.activation(t.xT[:, cols], window_view(t.bank[1][0:KA, :], b, ys, xs), ACT.Identity,
                                        scale=w[0:KA, W_GB:W_GB + 1], bias=w[0:KA, W_GB + 1:W_GB + 2])
                op.then_inc(xT_ready, 1)

            def affine_T(t, v, w):
                act.wait_ge(pe_z2T, v)
                act.activation(t.xT[:], t.bank[1][0:KA, :], ACT.Identity, scale=w[0:KA, W_GB + 2:W_GB + 3],
                               bias=w[0:KA, W_GB + 3:W_GB + 4]).then_inc(xT2_ready, 1)

            def slot(x, y):
                if y:
                    for h in (2, 0, 1):
                        act.wait_ge(pe_PT[h], y.v)
                        act.activation(y.t.pt[:, h].rearrange("p q n -> p (q n)"), y.t.bank[h][:], ACT.Copy).then_inc(pt_ready[h], 1)
                if x:
                    t, v = x.t, x.v
                    act.wait_ge(ld_w[x.par], x.wv)
                    affine_windows(t, x.par == 1, v, wts[x.par])
                    act.wait_ge(pe_qk[0], v)
                    act.activation(t.q0[:], t.bank[0][:], ACT.Copy, scale=HD ** -0.5).then_inc(qk_ready[0], 1)
                    act.wait_ge(pe_qk[1], v)
                    act.activation(t.k0[:], t.bank[2][:], ACT.Copy).then_inc(qk_ready[1], 1)
                    act.wait_ge(pe_qk[2], v)
                    act.activation(t.q1[:], t.bank[3][0:64], ACT.Copy, scale=HD ** -0.5)
                    act.activation(t.k1[:], t.bank[3][64:128], ACT.Copy).then_inc(qk_ready[2], 1)
                if y:
                    affine_T(y.t, y.v, wts[y.par])
                    for h in range(2):
                        act.wait_ge(pe_fc1[h], y.v)
                        act.activation(y.t.g[:, h, :], y.t.bank[2 + h][0:96, :], ACT.Gelu).then_inc(g_ready[h], 1)
                if x:
                    for h in (2, 0, 1):
                        act.wait_ge(d_ready[h], x.v)
                        if h == 2:
                            act.wait_ge(d_ready[3], x.v)
                        act.activation(x.t.d[:, h], x.t.d[:, h], ACT.Exp).then_inc(p_ready[h], 1)

            def last(s, v):
                act.wait_ge(pe_fin, act.snap(v + 1))
                src = tokens(st[s].bank[1][0:C, :]).rearrange("p b y (x) (j i) -> p b y x j i", j=4)
                for b in range(CHUNK_B):
                    for y in range(4):
                        dst = ypad[0:C, bass.ds(v * CHUNK_B + (b - CHUNK_B), 1), 1 + 4 * y:5 + 4 * y,
                                   1:1 + IMG].rearrange("p o j (x i) -> p (o x) j i", i=4)
                        op = act.activation(dst, src[:, b, y], ACT.Identity, scale=fn_gb[0:C, 0:1], bias=fn_gb[0:C, 1:2])
                op.then_inc(y_ready, 1)

            pipeline(act, slot, None, last)

            act.wait_ge(fin[5], 8)
            for k in range(2):
                act.wait_ge(ld_w[k], 16 * (GROUPS * 3 + 1))
                act.wait_ge(ld_x[k], 16 * (GROUPS + 1))
            act.wait_ge(pe_fin, 9)
            act.wait_ge(y_copied, 8)
            act.wait_ge(ld_late, 16 * 7)
            for t in (0, 2, 4, 6):
                act.wait_ge(conv_done, t + 1)
                act.activation(y2[:, 2 * t:2 * t + 2, :].rearrange("p i w -> p (i w)"), B8[t][0:C, :], ACT.Copy).then_inc(conv_a, 1)

            def affine(k, bk, col):
                for n in range(4):
                    act.wait_ge(zT_done, 4 * k + n + 1)
                    act.activation(xs[:, 4 * (n // 2):4 * (n // 2) + 4, 128 * (n % 2):128 * (n % 2) + 128],
                                   B8[bk + n][0:96, :].rearrange("p (a w) -> p a w", a=4), ACT.Identity,
                                   scale=l1w[0:96, col:col + 1], bias=l1w[0:96, col + 1:col + 2]).then_inc(xs_ready, 1)

            affine(0, 4, V_GB)
            for t in range(4):
                act.wait_ge(sed_done, t + 1)
                act.activation(hs[:, 2 * t:2 * t + 2, :].rearrange("p c w -> p (c w)"), B8[t][0:96, :], ACT.Gelu).then_inc(h_ready, 1)
            affine(1, 0, V_GB + 2)
            for t in range(4):
                for u in range(4):
                    act.wait_ge(fc1_done, 4 * t + u + 1)
                    act.activation(g1[:, u, 512 * t:512 * (t + 1)], B8[4 + u][0:96, :], ACT.Gelu,
                                   bias=l1w[0:96, V_F1B + u % 2:V_F1B + u % 2 + 1]).then_inc(g1_ready, 1)
            act.wait_ge(late_set, 4)
            for k in (0, 2, 4, 6):
                act.wait_ge(x2T_done, k + 1)
                act.activation(x2_rows(k), B8[(4 + k) % 8][0:C, :].rearrange("p (i y x) -> p y x i", i=4, x=4), ACT.Copy).then_inc(x2_a, 1)

            act.wait_ge(a_ready, 32)
            for e in range(9):
                if e < 8:
                    act.wait_ge(x3_done, e + 1)
                    act.activation(x3[:, 2 * e:2 * e + 2, :].rearrange("p b k -> p (b k)"), B8[e % 4][0:DIN, :], ACT.Identity,
                                   bias=l3w[0:DIN, Q_BDW:Q_BDW + 1]).then_inc(x3_ready, 1)
                if e:
                    act.wait_ge(px_done, e)
                    act.activation(xb[:, e - 1, :], B8[4 + (e - 1) % 4][:], ACT.Copy).then_inc(px_hi, 1)

            def tail(hb):
                act.wait_ge(tail_dve, D_ALL * hb + D_YC + 4)
                act.activation(yq[:], yc[:], ACT.Square).then_inc(yq_ready, 1)
                act.wait_ge(tail_dve, D_ALL * hb + D_YN + 4)
                act.activation(yc[:], yq[:], ACT.Identity, scale=l3w[0:DIN, Q_LN:Q_LN + 1],
                               bias=l3w[0:DIN, Q_LN + 1:Q_LN + 2]).then_inc(v_norm, 1)
                act.wait_ge(v_norm, hb + 1)
                for b in range(8):
                    cols = slice(256 * b, 256 * (b + 1))
                    act.activation(yq[:, cols], yc[:, cols], ACT.Square, accum_out=gx[:, 0, b:b + 1]).then_inc(gx2_ready, 1)
                for e in range(4):
                    act.wait_ge(tail_pe, M_ALL * hb + M_OUT + e + 1)
                    if hb and e == 0:
                        act.wait_ge(stored, 16 * 4)
                    act.activation(ob[:, 2 * e:2 * e + 2, :].rearrange("p b k -> p (b k)"), B8[6 + e % 2][0:C, :],
                                   ACT.Copy).then_inc(out_ready, 1)

            for u in range(8):
                if u >= 2:
                    act.wait_ge(scan_done, u - 1)
                    act.wait_ge(low_ready, u - 1)
                for e in range(4):
                    cols = slice(512 * e, 512 * (e + 1))
                    for k in range(3):
                        act.wait_ge(gate_done[k], 4 * u + e + 1)
                        if k:
                            if u:
                                act.wait_ge(all_ready, u)
                            act.activation(mag[k - 1][:, cols], B8[k][0:DIN, :], ACT.Abs)
                        act.activation(gate[u % 2][k][:, cols], B8[k][0:DIN, :], ACT.Copy).then_inc(gate_taken[k], 1)
                if u == 5:
                    tail(0)
            tail(1)

        @block.tensor
        def _(pe):
            def transpose_z(t, chain, done, v):
                pe.wait_ge(chain[5], v)
                for i in range(TILES):
                    op = pe.transpose(t.bank[1][0:ZW, i * 128:(i + 1) * 128], t.z[:, i, :], ident[:])
                op.then_inc(done, 1)

            def project(t, w, v):
                pe.wait_ge(xT_ready, v)
                for j in range(3):
                    pe.matmul(t.bank[(0, 2, 3)[j]][:], w[0:KA, W_QK + 128 * j:W_QK + 128 * (j + 1)], t.xT[:],
                              start=True, stop=True).then_inc(pe_qk[j], 1)
                for p in range(PAIRS):
                    op = pe.matmul(t.bank[1][:, p * C:(p + 1) * C], t.xT[:, 128 * p:128 * (p + 1)],
                                   w[0:KA, W_V:W_V + C], start=True, stop=True)
                op.then_inc(pe_v, 1)

            def scores(t, shifted, lp, v, half):
                if half == 0:
                    for j in range(3):
                        pe.wait_ge(qk_ready[j], v)
                    pe.wait_ge(v_ready, v)
                    for j in range(4):
                        h0, hs = ((0, 2), (2, 2), (4, 1), (5, 1))[j]
                        for part, table in enumerate((bias_hm, bias_lm)):
                            cols = slice(h0 * N, (h0 + hs) * N)
                            if shifted:
                                rhs = table[:, bass.ds(lp * 4 + 3, PAIRS), cols].rearrange("p q (h m) -> p h q m", h=hs)
                            else:
                                rhs = table[:, bass.ds(lp, 1), cols].rearrange(
                                    "p q (h m) -> p h q m", h=hs).to_broadcast([128, hs, PAIRS, N])
                            pe.matmul(t.bank[j][:, 0:hs * 4 * N], ident2[:], rhs, start=(part == 0), stop=(part == 1))
                q, k, heads = ((t.q0, t.k0, 4), (t.q1, t.k1, 2))[half]
                for p in range(PAIRS):
                    for b in range(2):
                        cols = slice(128 * p + 64 * b, 128 * p + 64 * b + 64)
                        for j in range(heads):
                            rows = slice(32 * j, 32 * j + HD)
                            c = half * 4 * N + p * N
                            op = pe.matmul(t.bank[j][64 * b:64 * b + 64, c:c + N], q[rows, cols], k[rows, cols],
                                           start=False, stop=True, skip_group_check=True)
                            if p == 3 and b == 1 and (half == 1 or j > 1):
                                op.then_inc(pe_S[j], 1)

            def probs_T(t, v):
                for h in (2, 0, 1):
                    pe.wait_ge(p_ready[h], v)
                    for p in range(PAIRS):
                        op = pe.transpose(t.bank[h][:, 128 * p:128 * (p + 1)], t.d[:, h, p], ident[:])
                    op.then_inc(pe_PT[h], 1)

            def values(t, v):
                for h in range(HP):
                    pe.wait_ge(pt_ready[h], v)
                for w in range(2 * PAIRS):
                    for h in range(HP):
                        op = pe.matmul(t.bank[3][0:112, w * N:(w + 1) * N], t.v[:, w, 128 * h:128 * h + 112],
                                       t.pt[:, h, w // 2, N * (w % 2):N * (w % 2) + N], start=(h == 0), stop=(h == 2))
                op.then_inc(pe_O, 1)

            def proj(t, w, v):
                pe.wait_ge(o_ready, v)
                for i in range(TILES):
                    op = pe.matmul(t.bank[0][:, i * C:(i + 1) * C], t.oT[:, i * 128:(i + 1) * 128],
                                   w[0:C, W_PROJ:W_PROJ + C], start=True, stop=True)
                op.then_inc(pe_proj, 1)

            def fc1(t, w, v):
                pe.wait_ge(xT2_ready, v)
                for h in range(2):
                    pe.matmul(t.bank[2 + h][0:96, :], w[0:KA, W_FC1 + 96 * h:W_FC1 + 96 * (h + 1)], t.xT[:],
                              start=True, stop=True).then_inc(pe_fc1[h], 1)

            def fc2(t, w, v):
                pe.wait_ge(g_ready[0], v)
                pe.wait_ge(g_ready[1], v)
                for i in range(TILES):
                    for h in range(2):
                        op = pe.matmul(t.bank[0][:, i * C:(i + 1) * C], t.g[:, h, i * 128:(i + 1) * 128],
                                       w[0:96, W_FC2 + C * h:W_FC2 + C * (h + 1)], start=(h == 0), stop=(h == 1))
                op.then_inc(pe_fc2, 1)

            def slot(x, y):
                if y:
                    probs_T(y.t, y.v)
                if x:
                    if x.before is not None:
                        pe.wait_ge(y_ready, x.before)
                    transpose_z(x.t, ln1, pe_zT, x.v)
                if y:
                    values(y.t, y.v)
                if x:
                    pe.wait_ge(ld_w[x.par], x.wv)
                    project(x.t, wts[x.par], x.v)
                if y:
                    proj(y.t, wts[y.par], y.v)
                if x:
                    scores(x.t, x.par == 1, x.lp, x.v, 0)
                if y:
                    transpose_z(y.t, ln2, pe_z2T, y.v)
                if x:
                    scores(x.t, x.par == 1, x.lp, x.v, 1)
                if y:
                    fc1(y.t, wts[y.par], y.v)
                    fc2(y.t, wts[y.par], y.v)

            pe.wait_ge(ld_const, 16 * 7)
            pe.wait_ge(split, 5)
            pe.wait_ge(setup, 4 * STREAMS)
            pipeline(pe, slot, None, lambda s, v: transpose_z(st[s], fin, pe_fin, v))

            pe.wait_ge(y_ready, 9)
            pe.wait_ge(y_copied, 8)
            pe.wait_ge(conv_ready, 1)
            for i in range(16):
                y, x = i // 4, i % 4
                for kx in range(3):
                    for ky in (0, 2):
                        rows = 64 + C if ky == 0 else C
                        op = pe.matmul(B8[i // 2][0:C, 256 * (i % 2):256 * (i % 2) + 256],
                                       conv_w[0:rows, kx + 3 * (ky // 2), :],
                                       ypad[0:rows, :, y + ky:y + ky + 13:4, x + kx:x + kx + 13:4],
                                       start=(kx == 0 and ky == 0), stop=(kx == 2 and ky == 2))
                if i % 2:
                    op.then_inc(conv_done, 1)
            for n in range(4):
                pe.wait_ge(conv_a, 2 + 2 * (n // 2))
                pe.wait_ge(conv_d, 2 + 2 * (n // 2))
                for i in range(8):
                    op = pe.transpose(B8[n][:, C * i:C * (i + 1)], y2[:, 8 * (n // 2) + i, 128 * (n % 2):128 * (n % 2) + 128],
                                      ident[0:C, 0:C])
                op.then_inc(back_done, 1)

            def pairs_T(k, bk):
                for n in range(4):
                    pe.wait_ge(norm_ready, 4 * k + n + 1)
                    z = z1[:, n % 2, 8 * (n // 2):8 * (n // 2) + 8, :].rearrange("p i c -> p (i c)")
                    for a in range(4):
                        op = pe.transpose(B8[bk + n][0:96, 128 * a:128 * (a + 1)], z[:, 96 * a:96 * (a + 1)], ident[:])
                    op.then_inc(zT_done, 1)

            pairs_T(0, 4)
            pe.wait_ge(xs_ready, 4)
            pe.wait_ge(sed_ready, 1)
            sw = sed_w[0:96, :].rearrange("p (a c m) -> p a c m", a=8, c=8)
            for c in range(8):
                for a in range(8):
                    op = pe.matmul(B8[c // 2][0:96, 256 * (c % 2):256 * (c % 2) + 256], sw[:, a, c, :], xs[:, a, :],
                                   start=(a == 0), stop=(a == 7))
                if c % 2:
                    op.then_inc(sed_done, 1)
            for c in range(8):
                pe.wait_ge(h_ready, c // 2 + 1)
                for h in range(2):
                    op = pe.matmul(B8[4 + h + 2 * (c // 4)][:, 96 * (c % 4):96 * (c % 4) + 96], hs[:, c, 128 * h:128 * h + 128],
                                   l1w[0:96, V_PROJ:V_PROJ + 96], start=True, stop=True)
                if c % 4 == 3:
                    op.then_inc(proj1_done, 1)
            pairs_T(1, 0)

            def fc2_late(t):
                pe.wait_ge(g1_ready, 4 * t + 4)
                pe.wait_ge(xs_ready, 8)
                for c in (2 * t, 2 * t + 1):
                    for h in range(2):
                        for r in range(2):
                            col = 96 * (c % 4) + C * r
                            for k in range(2):
                                op = pe.matmul(B8[h + 2 * (c // 4)][:, col:col + C], g1[:, 2 * r + k, 256 * c + 128 * h:256 * c + 128 * h + 128],
                                               l1w[0:96, V_FC2 + C * k:V_FC2 + C * (k + 1)], start=(k == 0), stop=(k == 1))
                if t % 2:
                    op.then_inc(fc2_done, 1)

            for t in range(4):
                pe.wait_ge(xs_ready, 6 + 2 * (t // 2))
                for u in range(4):
                    if t:
                        pe.wait_ge(g1_ready, 4 * (t - 1) + u + 1)
                    pe.matmul(B8[4 + u][0:96, :], l1w[0:96, V_FC1 + 96 * u:V_FC1 + 96 * (u + 1)],
                              xs[:, 2 * t:2 * t + 2, :].rearrange("p c w -> p (c w)"), start=True, stop=True).then_inc(fc1_done, 1)
                if t:
                    fc2_late(t - 1)
            fc2_late(3)

            for k in range(8):
                pe.wait_ge(x1_final, 2 if k < 4 else 4)
                if k == 4:
                    pe.wait_ge(x1_final, 4)
                for i in range(4):
                    op = pe.transpose(B8[(4 + k) % 8][0:C, 128 * i:128 * (i + 1)], x1[:, k % 2, 4 * (k // 2) + i, :], ident[:])
                op.then_inc(x2T_done, 1)
            pe.wait_ge(pooled_ready, 1)
            pe.matmul(B8[4][0:64, 0:8], l2w[0:112, U_W1:U_W1 + 64], pooled[:], start=True, stop=True).then_inc(t_done, 1)
            pe.wait_ge(t_ready, 1)
            for tap in range(4):
                op = pe.matmul(B8[5][0:112, 8 * tap:8 * tap + 8], l2w[0:64, U_W2 + 112 * tap:U_W2 + 112 * (tap + 1)], t2[:, 2],
                               start=True, stop=True)
            op.then_inc(wt_done, 1)

            pe.wait_ge(a_ready, 32)
            pe.wait_ge(ld_late, 16 * 7)
            for e in range(9):
                if e < 8:
                    h, j = e // 4, 2 * (e % 4)
                    if e >= 4:
                        pe.wait_ge(x3_ready, e - 3)
                    for k in range(9):
                        rows = slice(64 * h, 64 * h + C)
                        op = pe.matmul(B8[e % 4][0:DIN, :], taps_w[rows, k, :], a2[rows, j:j + 2, k // 3:k // 3 + 16, k % 3:k % 3 + 16],
                                       start=(k == 0), stop=(k == 8))
                    op.then_inc(x3_done, 1)
                if e:
                    pe.wait_ge(x3_ready, e)
                    if e >= 5:
                        pe.wait_ge(px_left, e - 4)
                    pe.matmul(B8[4 + (e - 1) % 4][:], l3w[0:DIN, Q_XD:Q_XD + 128], x3[:, 2 * e - 2:2 * e, :].rearrange("p b k -> p (b k)"),
                              start=True, stop=True).then_inc(px_done, 1)

            gw = gates_w[:].rearrange("p (g d c) -> p g d c", g=6, d=4)

            def gate_mm(u, e, g, bk, done):
                pe.matmul(B8[bk][0:DIN, :], gw[:, g, u % 4, :], xb[:, 4 * (u // 4) + e, :], start=True, stop=True).then_inc(done, 1)

            def gates(u):
                for e in range(4):
                    for k in range(3):
                        n = 4 * u + e
                        if n:
                            pe.wait_ge(gate_taken[k], n)
                        gate_mm(u, e, k, k, gate_done[k])

            def in_gates(u):
                for e in range(4):
                    for g, bk, done, taken in ((3, 3, l_done, l_taken), (5, 4, d_done, d_taken)):
                        if 4 * u + e:
                            if bk == 3 or e:
                                pe.wait_ge(taken, 4 * u + e)
                            else:
                                pe.wait_ge(taken, 4 * u)
                        gate_mm(u, e, g, bk, done)

            def out_gates(u):
                for e in range(4):
                    if 4 * u + e:
                        pe.wait_ge(u_taken, 4 * u + e)
                    gate_mm(u, e, 4, 5, u_done)

            def tail(hb):
                ones = l3w[0:DIN, Q_ONE:Q_ONE + DIN]
                pe.wait_ge(y_added, 8 * hb + 8)
                for e in range(4):
                    if e >= 2:
                        pe.wait_ge(tail_dve, D_ALL * hb + D_YC + e - 1)
                    pe.matmul(B8[6 + e % 2][0:DIN, :], ones, ysum[hb][:, 512 * e:512 * (e + 1)],
                              start=True, stop=True).then_inc(tail_pe, 1)
                pe.wait_ge(yq_ready, hb + 1)
                for t in range(16):
                    op = pe.matmul(B8[6][:, t:t + 1], yq[:, 128 * t:128 * (t + 1)], ones[:, 0:1], start=True, stop=True)
                op.then_inc(tail_pe, 1)
                pe.wait_ge(trstd_ready, hb + 1)
                pe.transpose(B8[7][0:16, 0:128], tvar[:, 1, :], ident[:]).then_inc(tail_pe, 1)
                pe.wait_ge(tail_dve, D_ALL * hb + D_RT + 1)
                for e in range(4):
                    if e >= 2:
                        pe.wait_ge(tail_dve, D_ALL * hb + D_YN + e - 1)
                    for t in range(4):
                        op = pe.matmul(B8[6 + e % 2][0:DIN, 128 * t:128 * (t + 1)], spread[:, 4 * e + t, :], rT[:],
                                       start=True, stop=True)
                    op.then_inc(tail_pe, 1)
                pe.wait_ge(gx_ready, hb + 1)
                pe.matmul(B8[6][0:DIN, 0:8], ones, gx[:, 1], start=True, stop=True).then_inc(tail_pe, 1)
                for e in range(4):
                    pe.wait_ge(tail_dve, D_ALL * hb + D_V2 + 2 * e + 2)
                    if e >= 2:
                        pe.wait_ge(out_ready, 4 * hb + e - 1)
                    pe.matmul(B8[6 + e % 2][0:C, :], l3w[0:DIN, Q_OUT:Q_OUT + C], yq[:, 512 * e:512 * (e + 1)],
                              start=True, stop=True).then_inc(tail_pe, 1)

            pe.wait_ge(xb_ready, 16)
            gates(0)
            for u in range(8):
                in_gates(u)
                if u < 7:
                    gates(u + 1)
                out_gates(u)
                if u == 4:
                    tail(0)
            tail(1)


def rel_pos_index():
    ws = 8
    coords = np.stack(np.meshgrid(np.arange(ws), np.arange(ws), indexing="ij")).reshape(2, -1)
    rel = (coords[:, :, None] - coords[:, None, :]).transpose(1, 2, 0)
    rel[:, :, 0] += ws - 1
    rel[:, :, 1] += ws - 1
    rel[:, :, 0] *= 2 * ws - 1
    return rel.sum(-1)


def window_order(shifted, u, v):
    order = []
    swap_y, swap_x = shifted and u == 1, shifted and v == 1
    for sy in range(2):
        for sx in range(2):
            y0, x0 = (1 - sy if swap_y else sy), (1 - sx if swap_x else sx)
            for iy in range(4):
                for ix in range(4):
                    order.append((4 * y0 + iy) * 8 + 4 * x0 + ix)
    return np.array(order)


def attn_mask(u, v):
    ids = np.zeros((8, 8))
    if u == 1:
        ids[4:, :] += 2
    if v == 1:
        ids[:, 4:] += 1
    ids = ids.reshape(-1)
    return np.where(ids[None, :] != ids[:, None], -100.0, 0.0)


def bias_layout(rpb):
    rpi = rel_pos_index()
    gathered, masks = [None] * 15, [None] * 15
    for l in range(3):
        for shifted in (False, True):
            for u in range(2):
                for v in range(2):
                    if not shifted and (u, v) != (0, 0):
                        continue
                    o = window_order(shifted, u, v)
                    idx = 3 + 4 * l + 2 * u + v if shifted else l
                    gathered[idx] = rpb[2 * l + shifted][rpi[o][:, o]].transpose(0, 2, 1)
                    m = attn_mask(u, v)[o][:, o] if shifted else np.zeros((64, 64))
                    masks[idx] = np.repeat(m[:, None, :], HEADS, 1)
    return np.stack(gathered, 1).reshape(64, 15, SC), np.stack(masks, 1).reshape(64, 15, SC)


def pack_l0(qkv_w, qkv_b, proj_w, proj_b, n1_g, n1_b, n2_g, n2_b, fc1_w, fc1_b, fc2_w, fc2_b):
    wp = np.zeros((8, 128, W_COLS), np.float32)
    for i in range(8):
        l = i % 6
        qk = np.zeros((KA, 384), np.float32)
        for h in range(HEADS):
            for j in range(2):
                rows = slice(j * 48 + h * 8, j * 48 + h * 8 + 8)
                row, second = ((0, 0), (0, 1), (1, 0), (1, 1), (2, 0), (3, 0))[h]
                col = 256 + 64 * j + 32 * row if second else 128 * j + 32 * row
                qk[:C, col:col + 8] = qkv_w[l][rows].T
                qk[C, col:col + 8] = qkv_b[l][rows]
        wp[i, :KA, W_QK:W_QK + 384] = qk
        wp[i, :C, W_V:W_V + C] = qkv_w[l][96:144].T
        wp[i, C, W_V:W_V + C] = qkv_b[l][96:144]
        wp[i, :C, W_PROJ:W_PROJ + C] = proj_w[l].T
        wp[i, :C, W_FC1:W_FC1 + MLP] = fc1_w[l].T
        wp[i, C, W_FC1:W_FC1 + MLP] = fc1_b[l]
        wp[i, :96, W_FC2:W_FC2 + 96] = fc2_w[l].T.reshape(2, 96, C).transpose(1, 0, 2).reshape(96, 96)
        for j, a in enumerate((n1_g, n1_b, n2_g, n2_b)):
            wp[i, :C, W_GB + j] = a[l]
            wp[i, C, W_GB + j] = 1.0 - j % 2
        wp[i, :, W_PB:W_PB + C] = proj_b[l]
        wp[i, :, W_B2:W_B2 + C] = fc2_b[l]
    return wp


def sedenion_signs():
    def conj(x):
        return x if len(x) == 1 else np.concatenate([conj(x[:len(x) // 2]), -x[len(x) // 2:]])

    def mult(a, b):
        if len(a) == 1:
            return a * b
        h = len(a) // 2
        a1, a2, b1, b2 = a[:h], a[h:], b[:h], b[h:]
        return np.concatenate([mult(a1, b1) - mult(conj(b2), a2), mult(b2, a1) + mult(a2, conj(b1))])

    eye = np.eye(16, dtype=np.float32)
    return np.array([[mult(eye[i], eye[i ^ k])[k] for k in range(16)] for i in range(16)], np.float32)


def late_arrays(inp):
    l0 = {k[8:]: v for k, v in inp.items() if k.startswith("L0_conv_")}
    l1 = {k[8:]: v for k, v in inp.items() if k.startswith("L1_conv_")}
    l2 = {k[8:]: v for k, v in inp.items() if k.startswith("L2_conv_")}
    cw = np.zeros((112, 6, C), np.float32)
    w = l0["conv_w"].transpose(1, 2, 3, 0)
    cw[:C, 0:3], cw[64:, 0:3], cw[:C, 3:6] = w[:, 0], w[:, 1], w[:, 2]
    i, k = np.arange(16)[:, None], np.arange(16)[None, :]
    sed = l1["w_sed"][i ^ k]
    sed = sed.reshape(8, 2, 16, C, C).transpose(1, 3, 0, 2, 4).reshape(96, 16 * SC)
    signs = sedenion_signs().reshape(8, 2, 16).transpose(1, 0, 2)
    signs = np.repeat(signs.reshape(2, 1, 128), C, 1).reshape(96, 128)
    lw = np.zeros((128, L1_COLS), np.float32)
    for r in range(2):
        rows = slice(C * r, C * r + C)
        lw[rows, V_PROJ + C * r:V_PROJ + C * (r + 1)] = l1["proj_w"]
        lw[rows, V_FC1 + 192 * r:V_FC1 + 192 * (r + 1)] = l1["fc1_w"]
        for j, a in enumerate(("norm1_g", "norm1_b", "norm2_g", "norm2_b")):
            lw[rows, V_GB + j] = l1[a]
    lw[:96, V_FC2:V_FC2 + 96] = l1["fc2_w"].reshape(2, 96, C).transpose(1, 0, 2).reshape(96, 96)
    lw[:96, V_F1B:V_F1B + 2] = l1["fc1_b"].reshape(2, 96).T
    lw[:, V_PB:V_PB + C], lw[:, V_B2:V_B2 + C] = l1["proj_b"], l1["fc2_b"]
    mw = np.zeros((128, L2_COLS), np.float32)
    mw[:64, U_BN + 3] = 1.0
    for h in range(2):
        ch, hid = slice(64 * h, 64 * h + C), slice(32 * h, 32 * h + 12)
        mw[ch, U_W1 + 32 * h:U_W1 + 32 * h + 12] = l2["w1"].T
        w2, b2 = l2["w2"].reshape(C, 9, 12), l2["b2"].reshape(C, 9)
        for t in range(4):
            c0 = U_W2 + 112 * t + 64 * h
            mw[hid, c0:c0 + C] = w2[:, t].T
            mw[ch, U_B2 + t] = b2[:, t]
        mw[ch, U_BIAS] = l2["bias"]
        for j, a in enumerate(("gamma", "beta", "running_mean", "running_var")):
            mw[hid, U_BN + j] = l2[a]
    l3 = {k[8:]: v for k, v in inp.items() if k.startswith("L3_conv_")}
    front = np.zeros((112, 96), np.float32)
    taps = np.zeros((112, 9, 96), np.float32)
    for h in range(2):
        front[64 * h:64 * h + C] = l3["W_in"].T
        taps[64 * h:64 * h + C] = l3["W_dw"].reshape(96, 9).T
    raw = np.concatenate([l3["W_w"], l3["W_l"], l3["W_u"], l3["W_d"]]).T
    raw = np.tile(raw, (8, 1))
    qw = np.zeros((128, L3_COLS), np.float32)
    qw[:96, Q_XD:Q_XD + 128] = np.tile(l3["W_xd"].T, (1, 8))
    qw[:96, Q_OUT:Q_OUT + 48] = l3["W_out"].T
    qw[:, Q_ONE:Q_ONE + 96] = 1.0
    for c, a in ((Q_BDW, "b_dw"), (Q_LN, "ln_w"), (Q_LN + 1, "ln_b"), (Q_GRN, "grn_gamma"), (Q_GRN + 1, "grn_beta")):
        qw[:96, c] = l3[a]
    qw[:, Q_WM:Q_WM + 4] = l3["w_m"]
    for blk, part in enumerate((0, 1, 0, 1, 2, None, 0, 1)):
        if part is not None:
            qw[16 * blk:16 * blk + 16, Q_MASK + part] = 1.0
    spread = np.zeros((16, 16, 96), np.float32)
    spread[np.arange(16), np.arange(16)] = 1.0
    return {"conv_in": cw, "sed_in": sed, "sign_in": signs, "l1_in": lw, "l2_in": mw,
            "front_in": front, "taps_in": taps, "gates_in": raw, "l3_in": qw, "spread_in": spread}


def first_layer_arrays(inp):
    x = inp["x"].reshape(8, 2, C, 2, 2, 4, 4, 4)
    x = x.transpose(0, 4, 6, 5, 7, 1, 3, 2).reshape(8, 128, TILES, C)
    x = np.concatenate([x, x[-2:]], 0)
    l0 = {k[8:]: v for k, v in inp.items() if k.startswith("L0_conv_")}
    bias, mask = bias_layout(l0["rpb"])
    fn = np.zeros((KA, 2), np.float32)
    fn[:C, 0], fn[:C, 1] = l0["fn_g"], l0["fn_b"]
    fn[C, 0] = 1.0
    return {
        "x_tok": np.ascontiguousarray(x),
        "wpack": pack_l0(*[l0[k] for k in ("qkv_w", "qkv_b", "proj_w", "proj_b", "n1_g", "n1_b", "n2_g", "n2_b",
                                         "fc1_w", "fc1_b", "fc2_w", "fc2_b")]),
        "rpb_raw": np.ascontiguousarray(bias),
        "mask_in": mask.astype(np.dtype("bfloat16")),
        "ident_in": np.eye(128, dtype=np.float32),
        "ident2_in": np.tile(np.eye(64), (2, 2)).astype(np.dtype("bfloat16")),
        "en_in": np.broadcast_to(np.stack([l0["en_g"], l0["en_b"]]), (128, 2, C)).copy(),
        "fn_in": fn,
    }


_ARGS = ["x_tok", "wpack", "rpb_raw", "mask_in", "ident_in", "ident2_in", "en_in", "fn_in", "conv_in", "sed_in", "sign_in",
         "l1_in", "l2_in", "front_in", "taps_in", "gates_in", "l3_in", "spread_in"]


def kernel(**inputs):
    import concourse.bacc as bacc
    from concourse.bass_utils import run_bass_kernel_spmd as run

    inp = {name: np.asarray(a) for name, a in inputs.items()}
    laid = {**first_layer_arrays(inp), **late_arrays(inp)}
    nc = bacc.Bacc("TRN2", target_bir_lowering=False, num_devices=1)
    arrays, args = {}, []
    for name in _ARGS:
        a = np.ascontiguousarray(laid[name])
        arrays[f"in_{name}"] = a
        args.append(nc.dram_tensor(f"in_{name}", a.shape, mybir.dt.from_np(a.dtype), kind="ExternalInput").ap())
    args.append(nc.dram_tensor("out_0", (B, C, IMG, IMG), F32, kind="ExternalOutput").ap())
    build(nc, *args)
    r = run(nc, [arrays], core_ids=[0])
    return r.results[0]["out_0"]
```

```python
import numpy as np
from contextlib import ExitStack

import concourse.bass as bass
from concourse import mybir
from concourse.alu_op_type import AluOpType as ALU

F32 = mybir.dt.float32
BF16 = mybir.dt.bfloat16
ACT = mybir.ActivationFunctionType
AX = mybir.AxisListType

B, C, IMG = 16, 48, 16
HEADS, HD, BLOCKS, MLP = 6, 8, 6, 192
N = 64
STREAMS = 2
CHUNK_B = 2
GROUPS = B // (STREAMS * CHUNK_B)
TOK = CHUNK_B * IMG * IMG
TILES = TOK // 128
PAIRS = 4
SC = HEADS * N
KA = C + 1
ZW = 65
HP = HEADS // 2
VW = 2 * HD + 2
PADW = IMG + 2
EPS = 1e-5

W_QK, W_V, W_PROJ, W_FC1, W_FC2, W_GB, W_PB, W_B2 = np.cumsum([0, 128, 48, 48, 192, 96, 4, 48])
W_COLS = int(W_B2) + 48

V_PROJ, V_FC1, V_FC2, V_GB, V_F1B, V_PB, V_B2 = (int(n) for n in np.cumsum([0, 96, 2 * 192, 96, 4, 2, 48]))
L1_COLS = V_B2 + 48
DIN, HB = 96, 8 * 256
Q_XD, Q_OUT, Q_ONE, Q_BDW, Q_LN, Q_GRN, Q_WM, Q_MASK = (int(n) for n in np.cumsum([0, 128, 48, 96, 1, 2, 2, 4]))
L3_COLS = Q_MASK + 3
U_W1, U_W2, U_BN, U_B2, U_BIAS = (int(n) for n in np.cumsum([0, 64, 4 * 112, 4, 4]))
L2_COLS = U_BIAS + 1


M_MEAN, M_VAR, M_RT, M_SPREAD, M_GM, M_OUT, M_ALL = (int(n) for n in np.cumsum([0, 4, 1, 1, 4, 1, 4]))
D_YC, D_VAR, D_RT, D_YN, D_V2, D_ALL = (int(n) for n in np.cumsum([0, 4, 1, 1, 4, 8]))


class Step:
    pass


def blocks_of(shifted, u):
    if not shifted:
        return slice(2 * u, 2 * u + 2)
    return slice(1, 3) if u == 0 else slice(0, 4, 3)


def window_pieces(shifted):
    for p in range(PAIRS):
        ys, xs = blocks_of(shifted, p // 2), blocks_of(shifted, p % 2)
        wide = xs.step is None
        for b in ((slice(0, CHUNK_B),) if wide else (slice(0, 1), slice(1, 2))):
            yield slice(128 * p + N * b.start, 128 * p + N * b.stop), b, ys, xs


def build(nc, x_tok, wpack, rpb_raw, mask_in, ident_in, ident2_in, en_in, fn_in,
          conv_in, sed_in, sign_in, l1_in, l2_in,
          front_in, taps_in, gates_in, l3_in, spread_in, out):
    with ExitStack() as ctx:

        def sb(name, shape, dt=F32):
            return ctx.enter_context(nc.sbuf_tensor(name, shape, dt))

        l01_memory, l0_memory, l1_memory = (ctx.enter_context(ExitStack()) for _ in range(3))

        def l01(name, shape, dt=F32):
            return l01_memory.enter_context(nc.sbuf_tensor(name, shape, dt))

        def l1(name, shape, dt=F32):
            return l1_memory.enter_context(nc.sbuf_tensor(name, shape, dt))

        def l0(name, shape, dt=F32):
            return l0_memory.enter_context(nc.sbuf_tensor(name, shape, dt))

        def sem(name):
            return ctx.enter_context(nc.semaphore(name))

        def sems(name, n):
            return [sem(f"{name}{i}") for i in range(n)]

        bank = [[ctx.enter_context(nc.psum_tensor(f"bank{s}{i}", [128, 512], F32)) for i in range(4)]
                for s in range(STREAMS)]
        ident = sb("ident", [128, 128])
        ident2 = sb("ident2", [128, 128], BF16)
        a2 = sb("a2", [64 + C, 8, PADW, PADW])
        front_w = sb("front_w", [64 + C, DIN])
        taps_w = sb("taps_w", [64 + C, 2, 9, DIN])
        gates_w = sb("gates_w", [128, 6 * 4 * DIN], BF16)
        l3w = sb("l3w", [128, L3_COLS])
        spread = sb("spread", [16, 16, DIN])
        l2w = sb("l2w", [128, L2_COLS])
        neg_half8 = sb("neg_half8", [128, 16])
        half8 = sb("half8", [128, 8])

        sed_w = l01("sed_w", [128, 16 * SC])
        rpb_sb = sed_w[:, 0:15 * SC].rearrange("p (t c) -> p t c", c=SC)
        ypad = l01("ypad", [64 + C, B, PADW, PADW])
        conv_w = l01("conv_w", [64 + C, 6, C])
        signs = l01("signs", [96, 128])
        l1w = l01("l1w", [128, L1_COLS])

        en_gb = l0("en_gb", [128, 2, C])
        fn_gb = l0("fn_gb", [KA, 2 + HEADS])
        neg_half = l0("neg_half", [128, 4])
        wts = [l0(f"wts{i}", [128, W_COLS]) for i in range(2)]
        bias_hm = l0("bias_hm", [128, 15, SC], BF16)
        bias_lm = l0("bias_lm", [128, 15, SC], BF16)
        st = []
        for s in range(STREAMS):
            t = Step()
            t.bank = bank[s]
            t.xin = l0(f"xin{s}", [128, TILES, C])
            t.x = l0(f"x{s}", [128, TILES, C])
            t.xc = l0(f"xc{s}", [128, TILES, C])
            t.sq = l0(f"sq{s}", [128, TILES, C])
            t.z = l0(f"z{s}", [128, TILES, ZW])
            t.s4 = l0(f"s4{s}", [128, 4, TILES])
            t.xT = l0(f"xT{s}", [128, TOK])
            t.q = l0(f"q{s}", [128, TOK])
            t.kraw = l0(f"kraw{s}", [C, TOK])
            t.k = l0(f"k{s}", [128, HEADS, TOK])
            t.mx = l0(f"mx{s}", [128, PAIRS, HEADS])
            t.d = l0(f"d{s}", [128, PAIRS, HEADS, N])
            t.pt = l0(f"pt{s}", [128, PAIRS, HP, 128])
            t.v = l0(f"v{s}", [128, 2 * PAIRS, HP, VW])
            t.rd = l0(f"rd{s}", [128, PAIRS * HP, 2])
            t.on = l0(f"on{s}", [128, PAIRS * C + ZW - C])
            t.oT = l0(f"oT{s}", [128, TOK])
            t.g = l0(f"g{s}", [96, 2, TOK])
            st.append(t)
        l0_memory.close()

        y2 = l1("y2", [C, 16, 256])
        x1 = l1("wx", [128, 2, 16, C])
        xc1, sq1, z1 = l1("wxc", [128, 2, 16, C]), l1("wsq", [128, 2, 16, C]), l1("wz", [128, 2, 16, C])
        st1 = l1("st1", [128, 4, 4, 8])
        xs = l1("xs", [96, 8, 256])
        hs = l1("sed_h", [96, 8, 256])
        g1 = l1("hid1", [96, 4, 2048])
        x2 = l1("x2", [64 + C, 8, IMG, PADW])
        pooled = l1("pooled", [64 + C, 8])
        t2 = l1("t2", [64, 4, 8])
        wt2 = l1("wt2", [64 + C, 4, 8])
        graw = l1("graw", [128, 6 * 4 * DIN])
        gpart = [l1(f"gpart{i}", [128, 6 * 4 * DIN], BF16) for i in range(3)]
        l1_memory.close()
        l01_memory.close()

        x3 = sb("x3", [DIN, B, 256])
        xb = sb("xb", [128, 8, 512], BF16)
        rest3 = [sb(f"rest3{i}", [128, 512]) for i in range(2)]
        mid3 = sb("mid3", [128, 512], BF16)
        gate = [[sb(f"gate{i}{k}", [DIN, HB]) for k in range(3)] for i in range(2)]
        mag = [sb(f"mag{k}", [DIN, HB]) for k in range(2)]
        gsum = [sb(f"gsum{i}", [DIN, HB]) for i in range(2)]
        lx = sb("lx", [DIN, HB])
        xd = sb("xd", [DIN, HB])
        hst = sb("hst", [DIN, 8, PADW, IMG])
        tmp = [sb(f"tmp{i}", [DIN, 256]) for i in range(3)]
        ysum = [sb(f"ysum{i}", [DIN, HB]) for i in range(2)]
        yc, yq = sb("yc", [DIN, HB]), sb("yq", [DIN, HB])
        tvar = sb("tvar", [128, 2, 16])
        rT = sb("rT", [16, 128])
        gx = sb("gx", [DIN, 6, 8])
        ob = yc[0:C].rearrange("p (b k) -> p b k", b=8)

        ld_const, ld_x, ld_w = sem("ld_const"), sems("ld_x", 2), sems("ld_w", 2)
        setup = sem("setup")
        split = sem("split")
        x_used = sems("x_used", 2)
        en = sems("en", 8)
        fin = sems("fin", 7)
        ln1, ln2 = sems("ln1_", 7), sems("ln2_", 7)
        pe_zT, pe_qk, pe_v, pe_S, pe_PT = sem("pe_zT"), sem("pe_qk"), sem("pe_v"), sems("pe_S", 4), sems("pe_PT", 4)
        pe_OT, on_ready = sem("pe_OT"), sem("on_ready")
        pe_O, pe_proj, pe_z2T, pe_fc1, pe_fc2 = sem("pe_O"), sem("pe_proj"), sem("pe_z2T"), sems("pe_fc1", 2), sem("pe_fc2")
        pe_fin = sem("pe_fin")
        xT_ready, xT2_ready, qk_ready, v_ready = sem("xT_ready"), sem("xT2_ready"), sems("qk_ready", 3), sem("v_ready")
        mx_ready, d_ready, p_ready, pt_ready = sems("mx_ready", 4), sems("d_ready", 4), sems("p_ready", 4), sems("pt_ready", 4)
        rd_ready, o_ready, x1_ready, x2_ready, g_ready = sem("rd_ready"), sem("o_ready"), sem("x1_ready"), sem("x2_ready"), sems("g_ready", 2)
        pb_added, b2_added, y_ready = sem("pb_added"), sem("b2_added"), sem("y_ready")
        stored = sem("stored")
        ld_sed, sed_ready, ld_late, conv_ready, y_copied, late_set = (sem(n) for n in (
            "ld_sed", "sed_ready", "ld_late", "conv_ready", "y_copied", "late_set"))
        conv_done, conv_a, conv_d, back_done = sem("conv_done"), sem("conv_a"), sem("conv_d"), sem("back_done")
        var_ready, rstd_ready, norm_ready, zT_done, xs_ready, bias_added = (sem(n) for n in (
            "var_ready", "rstd_ready", "norm_ready", "zT_done", "xs_ready", "bias_added"))
        dve_step, sed_done, h_ready, proj1_done, fc1_done, g1_ready, fc2_done, x1_final = (sem(n) for n in (
            "dve_step", "sed_done", "h_ready", "proj1_done", "fc1_done", "g1_ready", "fc2_done", "x1_final"))
        x2T_done, x2_a, x2_d, pooled_ready, t_done, t_ready, wt_done, bn_ready, a_ready = (sem(n) for n in (
            "x2T_done", "x2_a", "x2_d", "pooled_ready", "t_done", "t_ready", "wt_done", "bn_ready", "a_ready"))
        ld_gates = sem("ld_gates")
        x3_done, x3_ready, px_done, px_hi, px_left, xb_ready = (sem(n) for n in (
            "x3_done", "x3_ready", "px_done", "px_hi", "px_left", "xb_ready"))
        gate_done, gate_taken = sems("gate_done", 3), sems("gate_taken", 3)
        l_done, l_taken, d_done, d_taken, u_done, u_taken = (sem(n) for n in (
            "l_done", "l_taken", "d_done", "d_taken", "u_done", "u_taken"))
        low_ready, sum_ready, scan_done, y_added, recip_done, all_ready = (sem(n) for n in (
            "low_ready", "sum_ready", "scan_done", "y_added", "recip_done", "all_ready"))
        tail_pe, tail_dve = sem("tail_pe"), sem("tail_dve")
        yq_ready, trstd_ready, v_norm, gx2_ready, gx_ready, out_ready = (
            sem(n) for n in ("yq_ready", "trstd_ready", "v_norm", "gx2_ready", "gx_ready", "out_ready"))

        block = ctx.enter_context(nc.Block())

        def group_value(eng, v, s, k):
            return k * ((v - s + 1) // 2) if isinstance(v, int) else eng.snap((v + (1 - s)) // 2 * k)

        def pipeline(eng, slot, first, last):
            def step(n, v, lp, wv, **kw):
                o = Step()
                o.t, o.par, o.v, o.lp, o.wv = st[n % 2], n // 2 % 2, v, lp, wv
                o.first, o.before = kw.get("first"), kw.get("before")
                return o

            if first:
                first(0, 1)
            slot(step(0, 1, 0, 16, first=1 if first else None), None)
            with eng.Fori(0, GROUPS) as g:
                ga = [eng.snap(g * 2 + k) for k in (1, 2, 3)]
                start = dict(first=ga[1], before=ga[0])
                if first:
                    first(1, ga[1])
                wg = eng.snap(g * 48 + 16)
                with eng.Fori(0, 2) as lp:
                    vs = [eng.snap(g * 12 + lp * 4 + (k + 1)) for k in range(5)]
                    wv = eng.snap(g * 48 + lp * 16 + 16)
                    wn = eng.snap(g * 48 + lp * 16 + 32)
                    for k in range(1, 5):
                        x = step(k % 4, vs[k], lp if k < 4 else lp + 1, wv if k < 4 else wn, **start if k == 1 else {})
                        slot(x, step(k - 1, vs[k - 1], lp, wv))
                vs = [eng.snap(g * 12 + (8 + k + 1)) for k in range(5)]
                wv, wn = eng.snap(g * 48 + 48), eng.snap(g * 48 + 64)
                for k in range(1, 4):
                    slot(step(k, vs[k], 2, wv), step(k - 1, vs[k - 1], 2, wv))
                last(0, ga[0])
                if first:
                    first(0, ga[2])
                slot(step(0, vs[4], 0, wn, first=ga[2], before=ga[1]), step(3, vs[3], 2, wv))
                last(1, ga[1])

        def tokens(ap):
            return ap.rearrange("p (b y x i) -> p b y x i", b=CHUNK_B, y=4, x=4)

        def chunk(t, n):
            return t[:, n % 2, 8 * (n // 2):8 * (n // 2) + 8, :]

        B8 = bank[0] + bank[1]

        def x2_rows(k):
            h, iy = k % 2, k // 2
            v = x2[64 * h:64 * h + C].rearrange("p b (y j) x -> p (b y) j x", j=4)
            return v[:, :, iy, 1:1 + IMG].rearrange("p y (x i) -> p y x i", i=4)

        def window_view(ap, b, ys, xs):
            if xs.step is None:
                v = ap.rearrange("p (b y i) -> p b y i", b=CHUNK_B, y=4)
                return v[:, b, ys, 16 * xs.start:16 * xs.stop]
            return tokens(ap)[:, b, ys, xs, :]

        @block.sync
        def _(sp):
            for dst, src in ((ident[:], ident_in), (ident2[:], ident2_in), (rpb_sb[0:64], rpb_raw),
                             (rpb_sb[64:128], rpb_raw), (bias_lm[64:128], mask_in), (en_gb[:], en_in),
                             (fn_gb[:], fn_in)):
                sp.dma_start(dst, src).then_inc(ld_const, 16)
            for s in range(STREAMS):
                sp.dma_start(st[s].xin[:], x_tok[s]).then_inc(ld_x[s], 16)
            for dst, src in ((conv_w[:], conv_in), (l1w[:], l1_in), (l2w[:], l2_in), (front_w[:], front_in),
                             (taps_w[:], taps_in), (l3w[:], l3_in), (spread[:], spread_in)):
                sp.dma_start(dst, src).then_inc(ld_late, 16)
            for par in range(2):
                sp.dma_start(wts[par][:], wpack[par]).then_inc(ld_w[par], 16)
            def reload(par, nxt, done):
                sp.wait_ge(pe_fc2, done)
                sp.wait_ge(b2_added, done)
                sp.dma_start(wts[par][:], nxt).then_inc(ld_w[par], 16)

            sp.wait_ge(split, 5)
            sp.dma_start(sed_w[0:96, :], sed_in).then_inc(ld_sed, 16)
            sp.dma_start(signs[:], sign_in).then_inc(ld_sed, 16)
            with sp.Fori(0, GROUPS) as g:
                sp.wait_ge(x_used[0], g + 1)
                sp.dma_start(st[0].xin[:], x_tok[bass.ds(g * STREAMS + 2, 1)].rearrange("a p t c -> (a p) t c")).then_inc(ld_x[0], 16)
                sp.wait_ge(x_used[1], g + 1)
                sp.dma_start(st[1].xin[:], x_tok[bass.ds(g * STREAMS + 3, 1)].rearrange("a p t c -> (a p) t c")).then_inc(ld_x[1], 16)
                with sp.Fori(0, BLOCKS // 2) as lp:
                    for par in range(2):
                        reload(par, wpack[bass.ds(lp * 2 + (2 + par), 1)].rearrange("a p c -> (a p) c"),
                               sp.snap(g * 12 + lp * 4 + (2 * par + 2)))
            for s in range(STREAMS):
                sp.wait_ge(ld_x[s], 16 * (GROUPS + 1))
            for par in range(2):
                sp.wait_ge(ld_w[par], 16 * (GROUPS * 3 + 1))
            sp.wait_ge(y_copied, 8)
            sp.wait_ge(fin[5], 8)
            sp.dma_start(graw[:], gates_in).then_inc(ld_gates, 16)
            for hb in range(2):
                for e in range(4):
                    sp.wait_ge(out_ready, 4 * hb + e + 1)
                    sp.dma_start(out[8 * hb + 2 * e:8 * hb + 2 * e + 2].rearrange("b c y x -> c b (y x)"),
                                 ob[:, 2 * e:2 * e + 2, :]).then_inc(stored, 16)
            sp.wait_ge(stored, 16 * 8)

        @block.gpsimd
        def _(pool):
            pool.memset(neg_half[:], -0.5).then_inc(setup, 1)
            pool.memset(ypad[:], 0.0).then_inc(y_ready, 1)
            for s in range(STREAMS):
                pool.memset(st[s].z[:, :, C:ZW], 1.0).then_inc(setup if s else pe_fin, 1)
                for zeroed in (st[s].v, st[s].xT, st[s].q, st[s].k, st[s].oT, st[s].on):
                    pool.memset(zeroed[:], 0.0).then_inc(setup, 1)
            pool.wait_ge(setup, 7 * STREAMS)
            for s in range(STREAMS):
                for r in range(2):
                    pool.memset(st[s].v[64 * r:64 * r + 64, :, :, 2 * HD + r:2 * HD + r + 1], 1.0).then_inc(setup, 1)

            def rstd(t, chain, v):
                pool.wait_ge(chain[3], v)
                pool.tensor_tensor(t.s4[:, 3, :], t.s4[:, 2, :], neg_half[:], ALU.pow).then_inc(chain[4], 1)

            def bcast(ap):
                return ap.unsqueeze(1).to_broadcast([128, TILES, C])

            def add_bias(t, col, chain, done, v, w):
                pool.wait_ge(chain[5], v)
                pool.tensor_tensor(t.x[:], t.x[:], bcast(w[:, col:col + C]), ALU.add).then_inc(done, 1)

            def slot(x, y):
                if x:
                    rstd(x.t, ln1, x.v)
                    pool.wait_ge(ld_w[x.par], x.wv)
                    add_bias(x.t, W_PB, ln1, pb_added, x.v, wts[x.par])
                if y:
                    rstd(y.t, ln2, y.v)
                    add_bias(y.t, W_B2, ln2, b2_added, y.v, wts[y.par])

            def last(s, v):
                rstd(st[s], fin, v)
                pool.wait_ge(y_ready, pool.snap(v + 1))
                imgs = bass.ds(v * CHUNK_B - CHUNK_B, CHUNK_B)
                pool.tensor_copy(ypad[64:64 + C, imgs, 0:PADW - 1, :], ypad[0:C, imgs, 1:PADW, :]).then_inc(y_copied, 1)
                pool.wait_ge(y_copied, v)

            pool.wait_ge(setup, 9 * STREAMS)
            pool.wait_ge(ld_sed, 32)
            sw = sed_w[0:96, :].rearrange("p (k e) -> p k e", e=C)
            pool.tensor_tensor(sw, sw, signs[:].unsqueeze(2).to_broadcast([96, 128, C]), ALU.mult).then_inc(sed_ready, 1)
            pool.wait_ge(sed_ready, 1)
            pipeline(pool, slot, lambda s, v: rstd(st[s], en, v), last)

            pool.wait_ge(y_ready, 9)
            pool.wait_ge(fin[5], 8)
            pool.wait_ge(pe_fin, 9)
            for k in range(2):
                pool.wait_ge(ld_w[k], 16 * (GROUPS * 3 + 1))
                pool.wait_ge(ld_x[k], 16 * (GROUPS + 1))
            pool.wait_ge(ld_late, 16 * 7)
            pool.memset(neg_half8[:], -0.5).then_inc(late_set, 1)
            pool.memset(half8[:], 0.5).then_inc(late_set, 1)
            pool.memset(x2[:], 0.0).then_inc(late_set, 1)
            pool.memset(a2[:], 0.0).then_inc(late_set, 1)
            pool.wait_ge(late_set, 4)

            def bcast8(ap):
                return ap.unsqueeze(1).to_broadcast([128, 8, C])

            for k, col in enumerate((V_PB, V_B2)):
                for n in range(4):
                    pool.wait_ge(var_ready, 4 * k + n + 1)
                    pool.tensor_tensor(st1[:, n, 3], st1[:, n, 2], neg_half8[:, 0:8], ALU.pow).then_inc(rstd_ready, 1)
                    pool.tensor_tensor(chunk(x1, n), chunk(x1, n), bcast8(l1w[:, col:col + C]), ALU.add).then_inc(bias_added, 1)

            bn_var = l2w[0:64, U_BN + 3:U_BN + 4]
            pool.tensor_scalar(bn_var, bn_var, EPS, None, ALU.add).then_inc(bn_ready, 1)
            pool.wait_ge(bn_ready, 1)
            pool.tensor_tensor(bn_var, bn_var, neg_half8[0:64, 0:1],
                               ALU.pow).then_inc(bn_ready, 1)

            pool.wait_ge(a_ready, 32)
            pool.memset(hst[:], 0.0).then_inc(late_set, 1)
            for u in range(8):
                pool.wait_ge(gate_taken[1], 4 * u + 4)
                pool.wait_ge(gate_taken[2], 4 * u + 4)
                pool.tensor_tensor(mag[0][:], mag[0][:], mag[1][:], ALU.add).then_inc(sum_ready, 1)
                y, d = ysum[u // 4], u % 4
                pool.wait_ge(d_taken, 4 * u + 4)
                if d:
                    pool.wait_ge(y_added, 2 * u)
                    pool.tensor_tensor(y[:], y[:], xd[:], ALU.add).then_inc(y_added, 1)
                    pool.wait_ge(y_added, 2 * u + 1)
                    pool.wait_ge(u_taken, 4 * u + 4)
                    pool.tensor_tensor(y[:], y[:], gsum[u % 2][:], ALU.add).then_inc(y_added, 1)
                else:
                    pool.wait_ge(u_taken, 4 * u + 4)
                    pool.tensor_tensor(y[:], xd[:], gsum[u % 2][:], ALU.add).then_inc(y_added, 2)
                if u in (4, 7):
                    hb = u // 7
                    pool.wait_ge(tail_dve, D_ALL * hb + D_VAR + 1)
                    pool.tensor_tensor(tvar[:, 1], tvar[:, 0], neg_half8[:], ALU.pow).then_inc(trstd_ready, 1)
                    pool.wait_ge(gx2_ready, 8 * hb + 8)
                    pool.tensor_tensor(gx[:, 1], gx[:, 0], half8[0:DIN], ALU.pow).then_inc(gx_ready, 1)

        @block.vector
        def _(dve):
            dve.wait_ge(ld_const, 16 * 7)
            hi = bias_hm
            rest = rpb_sb
            dve.tensor_copy(hi[:], rpb_sb[:]).then_inc(split, 1)
            dve.wait_ge(split, 1)
            dve.tensor_tensor(rest[:], rpb_sb[:], hi[:], ALU.subtract).then_inc(split, 1)
            dve.wait_ge(split, 2)
            dve.tensor_copy(bias_hm[64:128], rest[64:128]).then_inc(split, 1)
            dve.tensor_copy(bias_lm[0:64], rest[0:64]).then_inc(split, 1)
            dve.wait_ge(split, 4)
            dve.tensor_tensor(bias_lm[0:64], rest[0:64], bias_lm[0:64], ALU.subtract).then_inc(split, 1)

            dve.wait_ge(ld_late, 16 * 7)
            dve.tensor_tensor(conv_w[64:64 + C, 1, :], conv_w[64:64 + C, 1, :], ident[64:64 + C, 64:64 + C], ALU.add).then_inc(conv_ready, 1)

            def variance(t, src, chain, v):
                dve.tensor_reduce(t.s4[:, 0, :], src[:], AX.X, ALU.add).then_inc(chain[0], 1)
                dve.wait_ge(chain[0], v)
                dve.scalar_tensor_tensor(t.xc[:], t.s4[:, 0, :].unsqueeze(2).to_broadcast([128, TILES, C]), -1.0 / C,
                                         src[:], ALU.mult, ALU.add).then_inc(chain[1], 1)
                dve.wait_ge(chain[1], v)
                dve.tensor_tensor(t.sq[:], t.xc[:], t.xc[:], ALU.mult).then_inc(chain[2], 1)
                dve.wait_ge(chain[2], v)
                dve.tensor_reduce(t.s4[:, 1, :], t.sq[:], AX.X, ALU.add).then_inc(chain[6], 1)
                dve.wait_ge(chain[6], v)
                dve.tensor_scalar(t.s4[:, 2, :], t.s4[:, 1, :], 1.0 / C, EPS, ALU.mult, ALU.add).then_inc(chain[3], 1)

            def normalise(t, dst, chain, v):
                dve.wait_ge(chain[4], v)
                dve.tensor_tensor(dst[:, :, 0:C], t.xc[:], t.s4[:, 3, :].unsqueeze(2).to_broadcast([128, TILES, C]),
                                  ALU.mult).then_inc(chain[5], 1)

            def norm(t, src, dst, chain, v):
                variance(t, src, chain, v)
                normalise(t, dst, chain, v)

            def take_k(t, v):
                dve.wait_ge(qk_ready[0], v)
                for h in range(HEADS):
                    op = dve.tensor_scalar(t.k[0:C, h], t.kraw[:], fn_gb[0:C, 2 + h:3 + h], None, ALU.mult)
                op.then_inc(qk_ready[2], 1)

            def take_v(t, v):
                dve.wait_ge(pe_v, v)
                src = t.bank[2][:, 0:PAIRS * C].rearrange("p (q h c) -> p q h c", q=PAIRS, h=HP)
                dst = t.v[:].rearrange("p (q w) h c -> p q w h c", q=PAIRS)
                for w in range(2):
                    for r in range(2):
                        op = dve.tensor_copy(dst[64 * r:64 * r + 64, :, w, :, HD * r:HD * r + HD],
                                             src[64 * w:64 * w + 64, :, :, HD * r:HD * r + HD])
                op.then_inc(v_ready, 1)

            def center(t, p, v):
                dve.wait_ge(pe_S[p], v)
                s = t.bank[p][:, 0:SC].rearrange("p (h m) -> p h m", h=HEADS)
                dve.tensor_reduce(t.mx[:, p], s, AX.X, ALU.max).then_inc(mx_ready[p], 1)
                dve.wait_ge(mx_ready[p], v)
                dve.tensor_tensor(t.d[:, p], s, t.mx[:, p].unsqueeze(2).to_broadcast([128, HEADS, N]),
                                  ALU.subtract).then_inc(d_ready[p], 1)

            def divide_o(t, v):
                dve.wait_ge(pe_O, v)
                o = t.bank[0][:, 0:PAIRS * HP * VW].rearrange("p (q c) -> p q c", c=VW)
                dve.reciprocal(t.rd[:], o[:, :, 2 * HD:VW]).then_inc(rd_ready, 1)
                dve.wait_ge(rd_ready, v)
                dve.tensor_tensor(t.on[:, 0:PAIRS * C].rearrange("p (q r c) -> p q r c", r=2, c=HD), o[:, :, 0:2 * HD].rearrange("p q (r c) -> p q r c", r=2),
                                  t.rd[:].unsqueeze(3).to_broadcast([128, PAIRS * HP, 2, HD]), ALU.mult).then_inc(on_ready, 1)

            def take_o(t, shifted, v):
                dve.wait_ge(pe_OT, v)
                for cols, b, ys, xs in window_pieces(shifted):
                    dst = window_view(t.oT[0:C], b, ys, xs)
                    like = "p (b y i) -> p b y i" if xs.step is None else "p (b y x i) -> p b y x i"
                    dims = dict(y=2, i=32) if xs.step is None else dict(y=2, x=2, i=16)
                    op = dve.tensor_copy(dst, t.bank[1][0:C, cols].rearrange(like, **dims))
                op.then_inc(o_ready, 1)

            def add_res(t, bk, pe_done, bias_done, ready, v):
                dve.wait_ge(pe_done, v)
                dve.wait_ge(bias_done, v)
                dve.tensor_tensor(t.x[:], bk[:, 0:TILES * C].rearrange("p (t c) -> p t c", t=TILES), t.x[:],
                                  ALU.add).then_inc(ready, 1)
                dve.wait_ge(ready, v)

            def first(s, v):
                t = st[s]
                dve.wait_ge(ld_x[s], group_value(dve, v, s, 16))
                norm(t, t.xin, t.x, en, v)
                dve.wait_ge(en[5], v)
                gb = en_gb[:].unsqueeze(2).to_broadcast([128, 2, TILES, C])
                dve.tensor_tensor(t.x[:], t.x[:], gb[:, 0], ALU.mult).then_inc(x_used[s], 1)
                dve.wait_ge(x_used[s], group_value(dve, v, s, 1))
                dve.tensor_tensor(t.x[:], t.x[:], gb[:, 1], ALU.add).then_inc(en[7], 1)

            def last(s, v):
                norm(st[s], st[s].x, st[s].z, fin, v)

            def slot(x, y):
                if x:
                    if x.first is not None:
                        dve.wait_ge(en[7], x.first)
                        if x.before is not None:
                            dve.wait_ge(pe_fin, x.before)
                    norm(x.t, x.t.x, x.t.z, ln1, x.v)
                if y:
                    divide_o(y.t, y.v)
                    take_o(y.t, y.par == 1, y.v)
                if x:
                    take_k(x.t, x.v)
                    take_v(x.t, x.v)
                if y:
                    add_res(y.t, y.t.bank[2], pe_proj, pb_added, x1_ready, y.v)
                    variance(y.t, y.t.x, ln2, y.v)
                if x:
                    center(x.t, 0, x.v)
                if y:
                    normalise(y.t, y.t.z, ln2, y.v)
                if x:
                    for p in range(1, PAIRS):
                        center(x.t, p, x.v)
                if y:
                    add_res(y.t, y.t.bank[0], pe_fc2, b2_added, x2_ready, y.v)

            dve.wait_ge(setup, 9 * STREAMS)
            pipeline(dve, slot, first, last)

            dve.wait_ge(y_ready, 9)
            dve.wait_ge(pe_fin, 9)
            for k in range(2):
                dve.wait_ge(ld_w[k], 16 * (GROUPS * 3 + 1))
                dve.wait_ge(ld_x[k], 16 * (GROUPS + 1))
            dve.wait_ge(y_copied, 8)
            chain = [0]

            def step(op):
                chain[0] += 1
                op.then_inc(dve_step, 1)
                dve.wait_ge(dve_step, chain[0])

            taps = taps_w[:].rearrange("p h k c -> p (h k) c")
            step(dve.tensor_tensor(taps, taps, front_w[:].unsqueeze(1).to_broadcast([64 + C, 18, DIN]), ALU.mult))
            dve.wait_ge(ld_gates, 16)
            for g in (4, 5):
                cols = graw[:, g * 4 * DIN:(g + 1) * 4 * DIN].rearrange("p (d c) -> p d c", d=4)
                step(dve.tensor_tensor(cols, cols, l3w[:, Q_WM:Q_WM + 4].unsqueeze(2).to_broadcast([128, 4, DIN]), ALU.mult))
            for k in range(3):
                step(dve.tensor_copy(gpart[k][:], graw[:]))
                if k < 2:
                    step(dve.tensor_tensor(graw[:], graw[:], gpart[k][:], ALU.subtract))
            step(dve.tensor_scalar(gates_w[:], gpart[0][:], l3w[:, Q_MASK:Q_MASK + 1], None, ALU.mult))
            for k in (1, 2):
                step(dve.scalar_tensor_tensor(gates_w[:], gpart[k][:], l3w[:, Q_MASK + k:Q_MASK + k + 1], gates_w[:],
                                              ALU.mult, ALU.add))
            for t in (1, 3, 5, 7):
                dve.wait_ge(conv_done, t + 1)
                dve.tensor_copy(y2[:, 2 * t:2 * t + 2, :].rearrange("p i w -> p (i w)"), B8[t][0:C, :]).then_inc(conv_d, 1)

            def b8(ap):
                return ap.unsqueeze(2).to_broadcast([128, 8, C])

            def half_norms(k, source):
                for n in range(4):
                    source(n)
                    x, xc, sq = chunk(x1, n), chunk(xc1, n), chunk(sq1, n)
                    step(dve.tensor_reduce(st1[:, n, 0], x, AX.X, ALU.add))
                    step(dve.scalar_tensor_tensor(xc, b8(st1[:, n, 0]), -1.0 / C, x, ALU.mult, ALU.add))
                    step(dve.tensor_tensor(sq, xc, xc, ALU.mult))
                    step(dve.tensor_reduce(st1[:, n, 1], sq, AX.X, ALU.add))
                    dve.tensor_scalar(st1[:, n, 2], st1[:, n, 1], 1.0 / C, EPS, ALU.mult, ALU.add).then_inc(var_ready, 1)
                for n in range(4):
                    dve.wait_ge(rstd_ready, 4 * k + n + 1)
                    dve.tensor_tensor(chunk(z1, n), chunk(xc1, n), b8(st1[:, n, 3]), ALU.mult).then_inc(norm_ready, 1)

            def take_conv(n):
                dve.wait_ge(back_done, n + 1)
                step(dve.tensor_copy(chunk(x1, n), B8[n][:, 0:8 * C].rearrange("p (i c) -> p i c", c=C)))

            def add_back(n, bk, done, k, final=None):
                dve.wait_ge(done, 1 + n // 2)
                dve.wait_ge(bias_added, 4 * k + n + 1)
                op = dve.tensor_tensor(chunk(x1, n), B8[bk + n][:, 0:8 * C].rearrange("p (i c) -> p i c", c=C),
                                       chunk(x1, n), ALU.add)
                op.then_inc(final, 1) if final else step(op)

            half_norms(0, take_conv)
            half_norms(1, lambda n: add_back(n, 4, proj1_done, 0))
            for n in range(4):
                add_back(n, 0, fc2_done, 1, x1_final)

            for k in (1, 3, 5, 7):
                dve.wait_ge(x2T_done, k + 1)
                dve.tensor_copy(x2_rows(k), B8[(4 + k) % 8][0:C, :].rearrange("p (i y x) -> p y x i", i=4, x=4)).then_inc(x2_d, 1)
            dve.wait_ge(x2_a, 4)
            dve.wait_ge(x2_d, 4)
            dve.tensor_reduce(pooled[:], x2[:, :, :, 1:1 + IMG], AX.XY, ALU.add).then_inc(pooled_ready, 1)
            dve.wait_ge(bn_ready, 2)
            bn = [l2w[0:64, U_BN + k:U_BN + k + 1] for k in range(4)]
            step(dve.tensor_tensor(bn[0], bn[0], bn[3], ALU.mult))
            dve.wait_ge(t_done, 1)
            step(dve.tensor_scalar(t2[:, 0], B8[4][0:64, 0:8], 1.0 / 256, bn[2], ALU.mult, ALU.subtract))
            step(dve.tensor_scalar(t2[:, 1], t2[:, 0], bn[0], bn[1], ALU.mult, ALU.add))
            dve.tensor_scalar(t2[:, 2], t2[:, 1], 0.0, None, ALU.max).then_inc(t_ready, 1)
            dve.wait_ge(wt_done, 1)
            step(dve.tensor_tensor(wt2[:], B8[5][0:112, 0:32].rearrange("p (t b) -> p t b", t=4),
                                   l2w[0:112, U_B2:U_B2 + 4].unsqueeze(2).to_broadcast([112, 4, 8]), ALU.add))
            for n, tap in enumerate((3, 0, 1, 2)):
                for j in range(8):
                    if tap == 3:
                        dve.tensor_scalar(a2[:, j, 1:17, 1:17], x2[:, j, :, 0:16], wt2[:, 3, j:j + 1],
                                          l2w[0:112, U_BIAS:U_BIAS + 1], ALU.mult, ALU.add).then_inc(a_ready, 1)
                    else:
                        if j == 0:
                            dve.wait_ge(a_ready, 8 * n)
                        dve.scalar_tensor_tensor(a2[:, j, 2:17, 1:17], x2[:, j, 0:15, tap:tap + 16], wt2[:, tap, j:j + 1],
                                                 a2[:, j, 2:17, 1:17], ALU.mult, ALU.add).then_inc(a_ready, 1)
            dve.wait_ge(a_ready, 32)

            for e in range(8):
                px, r = B8[4 + e % 4], rest3[e % 2]
                dve.wait_ge(px_hi, e + 1)
                dve.tensor_tensor(r[:], px[:], xb[:, e, :], ALU.subtract).then_inc(px_left, 1)
                dve.wait_ge(px_left, e + 1)
                dve.tensor_copy(xb[32:64, e, :], r[32:64]).then_inc(xb_ready, 1)
                step(dve.tensor_copy(mid3[96:128], r[96:128]))
                dve.tensor_tensor(xb[96:128, e, :], r[96:128], mid3[96:128], ALU.subtract).then_inc(xb_ready, 1)

            def seen(imgs, d):
                v = x3[:, imgs, :].rearrange("p b (y x) -> p b y x", x=IMG)
                if d == 0:
                    return v
                if d == 1:
                    return v.rearrange("p b y x -> p b x y")
                if d == 2:
                    return v[:, :, :, ::-1]
                return v[:, :, ::-1, :].rearrange("p b y x -> p b x y")

            def rows(t, s):
                return t[:].rearrange("p (b k s) -> p b k s", b=8, s=8)[:, :, :, s]

            def state(shift, s):
                v = hst[:, :, 1 + shift:1 + shift + IMG, :]
                return v.rearrange("p b y (n s) -> p b (y n) s", s=8)[:, :, :, s]

            def t8(i):
                return tmp[i][:].rearrange("p (b k) -> p b k", b=8)

            def unit(u):
                hb, d = u // 4, u % 4
                gl, gm, gr = gate[u % 2]
                dve.wait_ge(gate_taken[0], 4 * u + 4)
                if u >= 2:
                    dve.wait_ge(y_added, 2 * u - 2)
                dve.scalar_tensor_tensor(gsum[u % 2][:], gl[:], -1.0, gl[:], ALU.mult, ALU.max).then_inc(low_ready, 1)
                for e in range(4):
                    for bk, dst, done, taken in ((3, lx, l_done, l_taken), (4, xd, d_done, d_taken)):
                        if bk == 4 and e == 0 and u:
                            dve.wait_ge(y_added, 2 * u - 1)
                        dve.wait_ge(done, 4 * u + e + 1)
                        imgs = slice(8 * hb + 2 * e, 8 * hb + 2 * e + 2)
                        dve.tensor_tensor(dst[:, 512 * e:512 * (e + 1)].rearrange("p (b y x) -> p b y x", b=2, y=IMG),
                                          B8[bk][0:DIN, :].rearrange("p (b y x) -> p b y x", b=2, y=IMG),
                                          seen(imgs, d), ALU.mult).then_inc(taken, 1)
                dve.wait_ge(sum_ready, u + 1)
                dve.wait_ge(low_ready, u + 1)
                rgate = gsum[u % 2]
                dve.scalar_tensor_tensor(rgate[:], rgate[:], 1e-7, mag[0][:], ALU.add, ALU.add).then_inc(all_ready, 1)
                dve.wait_ge(all_ready, u + 1)
                dve.reciprocal(rgate[:], rgate[:]).then_inc(recip_done, 1)
                dve.wait_ge(recip_done, u + 1)
                dve.wait_ge(l_taken, 4 * u + 4)
                if u == 0:
                    dve.wait_ge(late_set, 5)
                step(dve.tensor_copy(state(0, 0), rows(lx, 0)))
                for s in range(1, 8):
                    dve.tensor_tensor(t8(0), rows(gl, s), state(-1, s - 1), ALU.mult).then_inc(dve_step, 1)
                    dve.tensor_tensor(t8(1), rows(gm, s), state(0, s - 1), ALU.mult).then_inc(dve_step, 1)
                    dve.tensor_tensor(t8(2), rows(gr, s), state(1, s - 1), ALU.mult).then_inc(dve_step, 1)
                    dve.wait_ge(dve_step, chain[0] + 2)
                    chain[0] += 3
                    step(dve.tensor_tensor(t8(0), t8(0), t8(1), ALU.add))
                    step(dve.tensor_tensor(t8(0), t8(0), t8(2), ALU.add))
                    step(dve.tensor_tensor(t8(0), t8(0), rows(rgate, s), ALU.mult))
                    op = dve.tensor_tensor(state(0, s), t8(0), rows(lx, s), ALU.add)
                    if s < 7:
                        step(op)
                    else:
                        op.then_inc(scan_done, 1)
                dve.wait_ge(scan_done, u + 1)
                for e in range(4):
                    dve.wait_ge(u_done, 4 * u + e + 1)
                    dve.tensor_tensor(gsum[u % 2][:, 512 * e:512 * (e + 1)].rearrange("p (b k) -> p b k", b=2),
                                      B8[5][0:DIN, :].rearrange("p (b k) -> p b k", b=2),
                                      hst[:, 2 * e:2 * e + 2, 1:1 + IMG, :].rearrange("p b y x -> p b (y x)"),
                                      ALU.mult).then_inc(u_taken, 1)
                dve.wait_ge(u_taken, 4 * u + 4)

            def tail(hb):
                dve.wait_ge(y_added, 8 * hb + 8)
                if hb:
                    dve.wait_ge(stored, 16 * 4)
                for e in range(4):
                    cols = slice(512 * e, 512 * (e + 1))
                    dve.wait_ge(tail_pe, M_ALL * hb + M_MEAN + e + 1)
                    dve.scalar_tensor_tensor(yc[:, cols], B8[6 + e % 2][0:DIN, :], -1.0 / DIN, ysum[hb][:, cols],
                                             ALU.mult, ALU.add).then_inc(tail_dve, 1)
                dve.wait_ge(tail_pe, M_ALL * hb + M_VAR + 1)
                dve.tensor_scalar(tvar[:, 0], B8[6][:, 0:16], 1.0 / DIN, EPS, ALU.mult, ALU.add).then_inc(tail_dve, 1)
                dve.wait_ge(tail_pe, M_ALL * hb + M_RT + 1)
                dve.tensor_copy(rT[:], B8[7][0:16, 0:128]).then_inc(tail_dve, 1)
                for e in range(4):
                    cols = slice(512 * e, 512 * (e + 1))
                    dve.wait_ge(tail_pe, M_ALL * hb + M_SPREAD + e + 1)
                    dve.tensor_tensor(yq[:, cols], B8[6 + e % 2][0:DIN, :], yc[:, cols], ALU.mult).then_inc(tail_dve, 1)
                dve.wait_ge(tail_pe, M_ALL * hb + M_GM + 1)
                step(dve.tensor_scalar(gx[:, 2], B8[6][0:DIN, 0:8], 1.0 / DIN, 1e-6, ALU.mult, ALU.add))
                step(dve.reciprocal(gx[:, 3], gx[:, 2]))
                step(dve.tensor_tensor(gx[:, 4], gx[:, 1], gx[:, 3], ALU.mult))
                step(dve.tensor_scalar(gx[:, 5], gx[:, 4], l3w[0:DIN, Q_GRN:Q_GRN + 1], 1.0, ALU.mult, ALU.add))
                for b in range(8):
                    cols = slice(256 * b, 256 * (b + 1))
                    dve.tensor_scalar(yq[:, cols], yc[:, cols], gx[:, 5, b:b + 1], l3w[0:DIN, Q_GRN + 1:Q_GRN + 2],
                                      ALU.mult, ALU.add).then_inc(tail_dve, 1)

            for u in range(8):
                unit(u)
                if u == 4:
                    tail(0)
            tail(1)

        @block.scalar
        def _(act):
            def affine_windows(t, shifted, v, w):
                act.wait_ge(pe_zT, v)
                for cols, b, ys, xs in window_pieces(shifted):
                    op = act.activation(t.xT[0:KA, cols], window_view(t.bank[1][0:KA, :], b, ys, xs), ACT.Identity,
                                        scale=w[0:KA, W_GB:W_GB + 1], bias=w[0:KA, W_GB + 1:W_GB + 2])
                op.then_inc(xT_ready, 1)

            def affine_T(t, v, w):
                act.wait_ge(pe_z2T, v)
                act.activation(t.xT[0:KA], t.bank[1][0:KA, :], ACT.Identity, scale=w[0:KA, W_GB + 2:W_GB + 3],
                               bias=w[0:KA, W_GB + 3:W_GB + 4]).then_inc(xT2_ready, 1)

            def exponential(t, p, v):
                act.wait_ge(d_ready[p], v)
                act.activation(t.d[:, p], t.d[:, p], ACT.Exp).then_inc(p_ready[p], 1)

            def slot(x, y):
                if y:
                    for p in range(PAIRS):
                        act.wait_ge(pe_PT[p], y.v)
                        act.activation(y.t.pt[:, p].rearrange("p h n -> p (h n)"), y.t.bank[p][:, 0:SC], ACT.Copy).then_inc(pt_ready[p], 1)
                if x:
                    t, v = x.t, x.v
                    act.wait_ge(ld_w[x.par], x.wv)
                    affine_windows(t, x.par == 1, v, wts[x.par])
                    act.wait_ge(pe_qk, v)
                    act.activation(t.kraw[:], t.bank[0][64:64 + C, :], ACT.Copy).then_inc(qk_ready[0], 1)
                    act.activation(t.q[0:C], t.bank[0][0:C], ACT.Copy, scale=HD ** -0.5).then_inc(qk_ready[1], 1)
                    for p in range(2):
                        exponential(t, p, v)
                if y:
                    affine_T(y.t, y.v, wts[y.par])
                if x:
                    for p in range(2, PAIRS):
                        exponential(t, p, v)
                if y:
                    for h in range(2):
                        act.wait_ge(pe_fc1[h], y.v)
                        act.activation(y.t.g[:, h, :], y.t.bank[2 + h][0:96, :], ACT.Gelu).then_inc(g_ready[h], 1)

            def last(s, v):
                act.wait_ge(pe_fin, act.snap(v + 1))
                src = tokens(st[s].bank[1][0:C, :]).rearrange("p b y (x) (j i) -> p b y x j i", j=4)
                for b in range(CHUNK_B):
                    for y in range(4):
                        dst = ypad[0:C, bass.ds(v * CHUNK_B + (b - CHUNK_B), 1), 1 + 4 * y:5 + 4 * y,
                                   1:1 + IMG].rearrange("p o j (x i) -> p (o x) j i", i=4)
                        op = act.activation(dst, src[:, b, y], ACT.Identity, scale=fn_gb[0:C, 0:1], bias=fn_gb[0:C, 1:2])
                op.then_inc(y_ready, 1)

            pipeline(act, slot, None, last)

            act.wait_ge(fin[5], 8)
            for k in range(2):
                act.wait_ge(ld_w[k], 16 * (GROUPS * 3 + 1))
                act.wait_ge(ld_x[k], 16 * (GROUPS + 1))
            act.wait_ge(pe_fin, 9)
            act.wait_ge(y_copied, 8)
            act.wait_ge(ld_late, 16 * 7)
            for t in (0, 2, 4, 6):
                act.wait_ge(conv_done, t + 1)
                act.activation(y2[:, 2 * t:2 * t + 2, :].rearrange("p i w -> p (i w)"), B8[t][0:C, :], ACT.Copy).then_inc(conv_a, 1)

            def affine(k, bk, col):
                for n in range(4):
                    act.wait_ge(zT_done, 4 * k + n + 1)
                    act.activation(xs[:, 4 * (n // 2):4 * (n // 2) + 4, 128 * (n % 2):128 * (n % 2) + 128],
                                   B8[bk + n][0:96, :].rearrange("p (a w) -> p a w", a=4), ACT.Identity,
                                   scale=l1w[0:96, col:col + 1], bias=l1w[0:96, col + 1:col + 2]).then_inc(xs_ready, 1)

            affine(0, 4, V_GB)
            for t in range(4):
                act.wait_ge(sed_done, t + 1)
                act.activation(hs[:, 2 * t:2 * t + 2, :].rearrange("p c w -> p (c w)"), B8[t][0:96, :], ACT.Gelu).then_inc(h_ready, 1)
            affine(1, 0, V_GB + 2)
            for t in range(4):
                for u in range(4):
                    act.wait_ge(fc1_done, 4 * t + u + 1)
                    act.activation(g1[:, u, 512 * t:512 * (t + 1)], B8[4 + u][0:96, :], ACT.Gelu,
                                   bias=l1w[0:96, V_F1B + u % 2:V_F1B + u % 2 + 1]).then_inc(g1_ready, 1)
            act.wait_ge(late_set, 4)
            for k in (0, 2, 4, 6):
                act.wait_ge(x2T_done, k + 1)
                act.activation(x2_rows(k), B8[(4 + k) % 8][0:C, :].rearrange("p (i y x) -> p y x i", i=4, x=4), ACT.Copy).then_inc(x2_a, 1)

            act.wait_ge(a_ready, 32)
            for e in range(9):
                if e < 8:
                    act.wait_ge(x3_done, e + 1)
                    act.activation(x3[:, 2 * e:2 * e + 2, :].rearrange("p b k -> p (b k)"), B8[e % 4][0:DIN, :], ACT.Identity,
                                   bias=l3w[0:DIN, Q_BDW:Q_BDW + 1]).then_inc(x3_ready, 1)
                if e:
                    act.wait_ge(px_done, e)
                    act.activation(xb[:, e - 1, :], B8[4 + (e - 1) % 4][:], ACT.Copy).then_inc(px_hi, 1)

            def tail(hb):
                act.wait_ge(tail_dve, D_ALL * hb + D_YC + 4)
                act.activation(yq[:], yc[:], ACT.Square).then_inc(yq_ready, 1)
                act.wait_ge(tail_dve, D_ALL * hb + D_YN + 4)
                act.activation(yc[:], yq[:], ACT.Identity, scale=l3w[0:DIN, Q_LN:Q_LN + 1],
                               bias=l3w[0:DIN, Q_LN + 1:Q_LN + 2]).then_inc(v_norm, 1)
                act.wait_ge(v_norm, hb + 1)
                for b in range(8):
                    cols = slice(256 * b, 256 * (b + 1))
                    act.activation(yq[:, cols], yc[:, cols], ACT.Square, accum_out=gx[:, 0, b:b + 1]).then_inc(gx2_ready, 1)
                for e in range(4):
                    act.wait_ge(tail_pe, M_ALL * hb + M_OUT + e + 1)
                    act.activation(ob[:, 2 * e:2 * e + 2, :].rearrange("p b k -> p (b k)"), B8[6 + e % 2][0:C, :],
                                   ACT.Copy).then_inc(out_ready, 1)

            for u in range(8):
                if u >= 2:
                    act.wait_ge(scan_done, u - 1)
                    act.wait_ge(low_ready, u - 1)
                for e in range(4):
                    cols = slice(512 * e, 512 * (e + 1))
                    for k in range(3):
                        act.wait_ge(gate_done[k], 4 * u + e + 1)
                        if k:
                            if u:
                                act.wait_ge(all_ready, u)
                            act.activation(mag[k - 1][:, cols], B8[k][0:DIN, :], ACT.Abs)
                        act.activation(gate[u % 2][k][:, cols], B8[k][0:DIN, :], ACT.Copy).then_inc(gate_taken[k], 1)
                if u == 5:
                    tail(0)
            tail(1)

        @block.tensor
        def _(pe):
            def transpose_z(t, chain, done, v):
                pe.wait_ge(chain[5], v)
                for i in range(TILES):
                    op = pe.transpose(t.bank[1][0:ZW, i * 128:(i + 1) * 128], t.z[:, i, :], ident[:])
                op.then_inc(done, 1)

            def project(t, w, v):
                pe.wait_ge(xT_ready, v)
                pe.matmul(t.bank[0][:], w[:, W_QK:W_QK + 128], t.xT[:], start=True, stop=True).then_inc(pe_qk, 1)
                for p in range(PAIRS):
                    op = pe.matmul(t.bank[2][:, p * C:(p + 1) * C], t.xT[:, 128 * p:128 * (p + 1)],
                                   w[:, W_V:W_V + C], start=True, stop=True)
                op.then_inc(pe_v, 1)

            def scores(t, shifted, lp, v, p):
                if p == 0:
                    for half in (1, 2):
                        pe.wait_ge(qk_ready[half], v)
                if p == 2:
                    pe.wait_ge(v_ready, v)
                for part, table in enumerate((bias_hm, bias_lm)):
                    if shifted:
                        rhs = table[:, bass.ds(lp * 4 + (3 + p), 1), :]
                    else:
                        rhs = table[:, bass.ds(lp, 1), :]
                    pe.matmul(t.bank[p][:, 0:SC], ident2[:], rhs.rearrange("p o c -> p (o c)"), start=(part == 0), stop=(part == 1))
                for b in range(2):
                    cols = slice(128 * p + 64 * b, 128 * p + 64 * b + 64)
                    op = pe.matmul(t.bank[p][64 * b:64 * b + 64, 0:SC], t.q[:, cols], t.k[:, :, cols],
                                   start=False, stop=True, skip_group_check=True)
                op.then_inc(pe_S[p], 1)

            def probs_T(t, v):
                for p in range(PAIRS):
                    pe.wait_ge(p_ready[p], v)
                    for h in range(HP):
                        op = pe.transpose(t.bank[p][:, 128 * h:128 * (h + 1)],
                                          t.d[:, p, 2 * h:2 * h + 2].rearrange("p h m -> p (h m)"), ident[:])
                    op.then_inc(pe_PT[p], 1)

            def values(t, v):
                for p in range(PAIRS):
                    pe.wait_ge(pt_ready[p], v)
                    for b in range(2):
                        for h in range(HP):
                            col = (p * HP + h) * VW
                            op = pe.matmul(t.bank[0][64 * b:64 * b + 64, col:col + VW], t.pt[:, p, h, 64 * b:64 * b + 64],
                                           t.v[:, 2 * p + b, h, :], start=True, stop=True)
                op.then_inc(pe_O, 1)

            def values_T(t, v):
                pe.wait_ge(on_ready, v)
                for p in range(PAIRS):
                    op = pe.transpose(t.bank[1][0:ZW, 128 * p:128 * (p + 1)], t.on[:, p * C:p * C + ZW], ident[:])
                op.then_inc(pe_OT, 1)

            def proj(t, w, v):
                pe.wait_ge(o_ready, v)
                for i in range(TILES):
                    op = pe.matmul(t.bank[2][:, i * C:(i + 1) * C], t.oT[:, i * 128:(i + 1) * 128],
                                   w[:, W_PROJ:W_PROJ + C], start=True, stop=True)
                op.then_inc(pe_proj, 1)

            def fc1(t, w, v):
                pe.wait_ge(xT2_ready, v)
                for h in range(2):
                    pe.matmul(t.bank[2 + h][0:96, :], w[:, W_FC1 + 96 * h:W_FC1 + 96 * (h + 1)], t.xT[:],
                              start=True, stop=True).then_inc(pe_fc1[h], 1)

            def fc2(t, w, v):
                pe.wait_ge(g_ready[0], v)
                pe.wait_ge(g_ready[1], v)
                for i in range(TILES):
                    for h in range(2):
                        op = pe.matmul(t.bank[0][:, i * C:(i + 1) * C], t.g[:, h, i * 128:(i + 1) * 128],
                                       w[0:96, W_FC2 + C * h:W_FC2 + C * (h + 1)], start=(h == 0), stop=(h == 1))
                op.then_inc(pe_fc2, 1)

            def slot(x, y):
                if y:
                    probs_T(y.t, y.v)
                    values(y.t, y.v)
                if x:
                    if x.before is not None:
                        pe.wait_ge(y_ready, x.before)
                    transpose_z(x.t, ln1, pe_zT, x.v)
                if y:
                    values_T(y.t, y.v)
                if x:
                    pe.wait_ge(ld_w[x.par], x.wv)
                    project(x.t, wts[x.par], x.v)
                if y:
                    proj(y.t, wts[y.par], y.v)
                if x:
                    for p in range(3):
                        scores(x.t, x.par == 1, x.lp, x.v, p)
                if y:
                    transpose_z(y.t, ln2, pe_z2T, y.v)
                if x:
                    scores(x.t, x.par == 1, x.lp, x.v, 3)
                if y:
                    fc1(y.t, wts[y.par], y.v)
                    fc2(y.t, wts[y.par], y.v)

            pe.wait_ge(ld_const, 16 * 7)
            pe.wait_ge(split, 5)
            pe.wait_ge(setup, 9 * STREAMS)
            pipeline(pe, slot, None, lambda s, v: transpose_z(st[s], fin, pe_fin, v))

            pe.wait_ge(y_ready, 9)
            pe.wait_ge(y_copied, 8)
            pe.wait_ge(conv_ready, 1)
            for i in range(16):
                y, x = i // 4, i % 4
                for kx in range(3):
                    for ky in (0, 2):
                        op = pe.matmul(B8[i // 2][0:C, 256 * (i % 2):256 * (i % 2) + 256],
                                       conv_w[:, kx + 3 * (ky // 2), :],
                                       ypad[:, :, y + ky:y + ky + 13:4, x + kx:x + kx + 13:4],
                                       start=(kx == 0 and ky == 0), stop=(kx == 2 and ky == 2))
                if i % 2:
                    op.then_inc(conv_done, 1)
            for n in range(4):
                pe.wait_ge(conv_a, 2 + 2 * (n // 2))
                pe.wait_ge(conv_d, 2 + 2 * (n // 2))
                for i in range(8):
                    op = pe.transpose(B8[n][:, C * i:C * (i + 1)], y2[:, 8 * (n // 2) + i, 128 * (n % 2):128 * (n % 2) + 128],
                                      ident[0:C, 0:C])
                op.then_inc(back_done, 1)

            def pairs_T(k, bk):
                for n in range(4):
                    pe.wait_ge(norm_ready, 4 * k + n + 1)
                    z = z1[:, n % 2, 8 * (n // 2):8 * (n // 2) + 8, :].rearrange("p i c -> p (i c)")
                    for a in range(4):
                        op = pe.transpose(B8[bk + n][0:96, 128 * a:128 * (a + 1)], z[:, 96 * a:96 * (a + 1)], ident[:])
                    op.then_inc(zT_done, 1)

            pairs_T(0, 4)
            pe.wait_ge(xs_ready, 4)
            pe.wait_ge(sed_ready, 1)
            sw = sed_w[0:96, :].rearrange("p (a c m) -> p a c m", a=8, c=8)
            for c in range(8):
                for a in range(8):
                    op = pe.matmul(B8[c // 2][0:96, 256 * (c % 2):256 * (c % 2) + 256], sw[:, a, c, :], xs[:, a, :],
                                   start=(a == 0), stop=(a == 7))
                if c % 2:
                    op.then_inc(sed_done, 1)
            for c in range(8):
                pe.wait_ge(h_ready, c // 2 + 1)
                for h in range(2):
                    op = pe.matmul(B8[4 + h + 2 * (c // 4)][:, 96 * (c % 4):96 * (c % 4) + 96], hs[:, c, 128 * h:128 * h + 128],
                                   l1w[0:96, V_PROJ:V_PROJ + 96], start=True, stop=True)
                if c % 4 == 3:
                    op.then_inc(proj1_done, 1)
            pairs_T(1, 0)

            def fc2_late(t):
                pe.wait_ge(g1_ready, 4 * t + 4)
                pe.wait_ge(xs_ready, 8)
                for c in (2 * t, 2 * t + 1):
                    for h in range(2):
                        for r in range(2):
                            col = 96 * (c % 4) + C * r
                            for k in range(2):
                                op = pe.matmul(B8[h + 2 * (c // 4)][:, col:col + C], g1[:, 2 * r + k, 256 * c + 128 * h:256 * c + 128 * h + 128],
                                               l1w[0:96, V_FC2 + C * k:V_FC2 + C * (k + 1)], start=(k == 0), stop=(k == 1))
                if t % 2:
                    op.then_inc(fc2_done, 1)

            for t in range(4):
                pe.wait_ge(xs_ready, 6 + 2 * (t // 2))
                for u in range(4):
                    if t:
                        pe.wait_ge(g1_ready, 4 * (t - 1) + u + 1)
                    pe.matmul(B8[4 + u][0:96, :], l1w[0:96, V_FC1 + 96 * u:V_FC1 + 96 * (u + 1)],
                              xs[:, 2 * t:2 * t + 2, :].rearrange("p c w -> p (c w)"), start=True, stop=True).then_inc(fc1_done, 1)
                if t:
                    fc2_late(t - 1)
            fc2_late(3)

            for k in range(8):
                pe.wait_ge(x1_final, 2 if k < 4 else 4)
                if k == 4:
                    pe.wait_ge(x1_final, 4)
                for i in range(4):
                    op = pe.transpose(B8[(4 + k) % 8][0:C, 128 * i:128 * (i + 1)], x1[:, k % 2, 4 * (k // 2) + i, :], ident[:])
                op.then_inc(x2T_done, 1)
            pe.wait_ge(pooled_ready, 1)
            pe.matmul(B8[4][0:64, 0:8], l2w[0:112, U_W1:U_W1 + 64], pooled[:], start=True, stop=True).then_inc(t_done, 1)
            pe.wait_ge(t_ready, 1)
            for tap in range(4):
                op = pe.matmul(B8[5][0:112, 8 * tap:8 * tap + 8], l2w[0:64, U_W2 + 112 * tap:U_W2 + 112 * (tap + 1)], t2[:, 2],
                               start=True, stop=True)
            op.then_inc(wt_done, 1)

            pe.wait_ge(a_ready, 32)
            pe.wait_ge(ld_late, 16 * 7)
            for e in range(9):
                if e < 8:
                    h, j = e // 4, 2 * (e % 4)
                    if e >= 4:
                        pe.wait_ge(x3_ready, e - 3)
                    for k in range(9):
                        op = pe.matmul(B8[e % 4][0:DIN, :], taps_w[:, h, k, :], a2[:, j:j + 2, k // 3:k // 3 + 16, k % 3:k % 3 + 16],
                                       start=(k == 0), stop=(k == 8))
                    op.then_inc(x3_done, 1)
                if e:
                    pe.wait_ge(x3_ready, e)
                    if e >= 5:
                        pe.wait_ge(px_left, e - 4)
                    pe.matmul(B8[4 + (e - 1) % 4][:], l3w[0:DIN, Q_XD:Q_XD + 128], x3[:, 2 * e - 2:2 * e, :].rearrange("p b k -> p (b k)"),
                              start=True, stop=True).then_inc(px_done, 1)

            gw = gates_w[:].rearrange("p (g d c) -> p g d c", g=6, d=4)

            def gate_mm(u, e, g, bk, done):
                pe.matmul(B8[bk][0:DIN, :], gw[:, g, u % 4, :], xb[:, 4 * (u // 4) + e, :], start=True, stop=True).then_inc(done, 1)

            def gates(u):
                for e in range(4):
                    for k in range(3):
                        n = 4 * u + e
                        if n:
                            pe.wait_ge(gate_taken[k], n)
                        gate_mm(u, e, k, k, gate_done[k])

            def in_gates(u):
                for e in range(4):
                    for g, bk, done, taken in ((3, 3, l_done, l_taken), (5, 4, d_done, d_taken)):
                        if 4 * u + e:
                            if bk == 3 or e:
                                pe.wait_ge(taken, 4 * u + e)
                            else:
                                pe.wait_ge(taken, 4 * u)
                        gate_mm(u, e, g, bk, done)

            def out_gates(u):
                for e in range(4):
                    if 4 * u + e:
                        pe.wait_ge(u_taken, 4 * u + e)
                    gate_mm(u, e, 4, 5, u_done)

            def tail(hb):
                ones = l3w[0:DIN, Q_ONE:Q_ONE + DIN]
                pe.wait_ge(y_added, 8 * hb + 8)
                for e in range(4):
                    if e >= 2:
                        pe.wait_ge(tail_dve, D_ALL * hb + D_YC + e - 1)
                    pe.matmul(B8[6 + e % 2][0:DIN, :], ones, ysum[hb][:, 512 * e:512 * (e + 1)],
                              start=True, stop=True).then_inc(tail_pe, 1)
                pe.wait_ge(yq_ready, hb + 1)
                for t in range(16):
                    op = pe.matmul(B8[6][:, t:t + 1], yq[:, 128 * t:128 * (t + 1)], ones[:, 0:1], start=True, stop=True)
                op.then_inc(tail_pe, 1)
                pe.wait_ge(trstd_ready, hb + 1)
                pe.transpose(B8[7][0:16, 0:128], tvar[:, 1, :], ident[:]).then_inc(tail_pe, 1)
                pe.wait_ge(tail_dve, D_ALL * hb + D_RT + 1)
                for e in range(4):
                    if e >= 2:
                        pe.wait_ge(tail_dve, D_ALL * hb + D_YN + e - 1)
                    for t in range(4):
                        op = pe.matmul(B8[6 + e % 2][0:DIN, 128 * t:128 * (t + 1)], spread[:, 4 * e + t, :], rT[:],
                                       start=True, stop=True)
                    op.then_inc(tail_pe, 1)
                pe.wait_ge(gx_ready, hb + 1)
                pe.matmul(B8[6][0:DIN, 0:8], ones, gx[:, 1], start=True, stop=True).then_inc(tail_pe, 1)
                for e in range(4):
                    pe.wait_ge(tail_dve, D_ALL * hb + D_V2 + 2 * e + 2)
                    if e >= 2:
                        pe.wait_ge(out_ready, 4 * hb + e - 1)
                    pe.matmul(B8[6 + e % 2][0:C, :], l3w[0:DIN, Q_OUT:Q_OUT + C], yq[:, 512 * e:512 * (e + 1)],
                              start=True, stop=True).then_inc(tail_pe, 1)

            pe.wait_ge(xb_ready, 16)
            gates(0)
            for u in range(8):
                in_gates(u)
                if u < 7:
                    gates(u + 1)
                out_gates(u)
                if u == 4:
                    tail(0)
            tail(1)


def rel_pos_index():
    ws = 8
    coords = np.stack(np.meshgrid(np.arange(ws), np.arange(ws), indexing="ij")).reshape(2, -1)
    rel = (coords[:, :, None] - coords[:, None, :]).transpose(1, 2, 0)
    rel[:, :, 0] += ws - 1
    rel[:, :, 1] += ws - 1
    rel[:, :, 0] *= 2 * ws - 1
    return rel.sum(-1)


def window_order(shifted, u, v):
    order = []
    swap_y, swap_x = shifted and u == 1, shifted and v == 1
    for sy in range(2):
        for sx in range(2):
            y0, x0 = (1 - sy if swap_y else sy), (1 - sx if swap_x else sx)
            for iy in range(4):
                for ix in range(4):
                    order.append((4 * y0 + iy) * 8 + 4 * x0 + ix)
    return np.array(order)


def attn_mask(u, v):
    ids = np.zeros((8, 8))
    if u == 1:
        ids[4:, :] += 2
    if v == 1:
        ids[:, 4:] += 1
    ids = ids.reshape(-1)
    return np.where(ids[None, :] != ids[:, None], -100.0, 0.0)


def bias_layout(rpb):
    rpi = rel_pos_index()
    gathered, masks = [None] * 15, [None] * 15
    for l in range(3):
        for shifted in (False, True):
            for u in range(2):
                for v in range(2):
                    if not shifted and (u, v) != (0, 0):
                        continue
                    o = window_order(shifted, u, v)
                    idx = 3 + 4 * l + 2 * u + v if shifted else l
                    gathered[idx] = rpb[2 * l + shifted][rpi[o][:, o]].transpose(0, 2, 1)
                    m = attn_mask(u, v)[o][:, o] if shifted else np.zeros((64, 64))
                    masks[idx] = np.repeat(m[:, None, :], HEADS, 1)
    return np.stack(gathered, 1).reshape(64, 15, SC), np.stack(masks, 1).reshape(64, 15, SC)


def pack_l0(qkv_w, qkv_b, proj_w, proj_b, n1_g, n1_b, n2_g, n2_b, fc1_w, fc1_b, fc2_w, fc2_b):
    wp = np.zeros((8, 128, W_COLS), np.float32)
    for i in range(8):
        l = i % 6
        for j in range(2):
            wp[i, :C, W_QK + 64 * j:W_QK + 64 * j + C] = qkv_w[l][C * j:C * (j + 1)].T
            wp[i, C, W_QK + 64 * j:W_QK + 64 * j + C] = qkv_b[l][C * j:C * (j + 1)]
        wp[i, :C, W_V:W_V + C] = qkv_w[l][96:144].T
        wp[i, C, W_V:W_V + C] = qkv_b[l][96:144]
        wp[i, :C, W_PROJ:W_PROJ + C] = proj_w[l].T
        wp[i, :C, W_FC1:W_FC1 + MLP] = fc1_w[l].T
        wp[i, C, W_FC1:W_FC1 + MLP] = fc1_b[l]
        wp[i, :96, W_FC2:W_FC2 + 96] = fc2_w[l].T.reshape(2, 96, C).transpose(1, 0, 2).reshape(96, 96)
        for j, a in enumerate((n1_g, n1_b, n2_g, n2_b)):
            wp[i, :C, W_GB + j] = a[l]
            wp[i, C, W_GB + j] = 1.0 - j % 2
        wp[i, :, W_PB:W_PB + C] = proj_b[l]
        wp[i, :, W_B2:W_B2 + C] = fc2_b[l]
    return wp


def sedenion_signs():
    def conj(x):
        return x if len(x) == 1 else np.concatenate([conj(x[:len(x) // 2]), -x[len(x) // 2:]])

    def mult(a, b):
        if len(a) == 1:
            return a * b
        h = len(a) // 2
        a1, a2, b1, b2 = a[:h], a[h:], b[:h], b[h:]
        return np.concatenate([mult(a1, b1) - mult(conj(b2), a2), mult(b2, a1) + mult(a2, conj(b1))])

    eye = np.eye(16, dtype=np.float32)
    return np.array([[mult(eye[i], eye[i ^ k])[k] for k in range(16)] for i in range(16)], np.float32)


def late_arrays(inp):
    l0 = {k[8:]: v for k, v in inp.items() if k.startswith("L0_conv_")}
    l1 = {k[8:]: v for k, v in inp.items() if k.startswith("L1_conv_")}
    l2 = {k[8:]: v for k, v in inp.items() if k.startswith("L2_conv_")}
    cw = np.zeros((112, 6, C), np.float32)
    w = l0["conv_w"].transpose(1, 2, 3, 0)
    cw[:C, 0:3], cw[64:, 0:3], cw[:C, 3:6] = w[:, 0], w[:, 1], w[:, 2]
    i, k = np.arange(16)[:, None], np.arange(16)[None, :]
    sed = l1["w_sed"][i ^ k]
    sed = sed.reshape(8, 2, 16, C, C).transpose(1, 3, 0, 2, 4).reshape(96, 16 * SC)
    signs = sedenion_signs().reshape(8, 2, 16).transpose(1, 0, 2)
    signs = np.repeat(signs.reshape(2, 1, 128), C, 1).reshape(96, 128)
    lw = np.zeros((128, L1_COLS), np.float32)
    for r in range(2):
        rows = slice(C * r, C * r + C)
        lw[rows, V_PROJ + C * r:V_PROJ + C * (r + 1)] = l1["proj_w"]
        lw[rows, V_FC1 + 192 * r:V_FC1 + 192 * (r + 1)] = l1["fc1_w"]
        for j, a in enumerate(("norm1_g", "norm1_b", "norm2_g", "norm2_b")):
            lw[rows, V_GB + j] = l1[a]
    lw[:96, V_FC2:V_FC2 + 96] = l1["fc2_w"].reshape(2, 96, C).transpose(1, 0, 2).reshape(96, 96)
    lw[:96, V_F1B:V_F1B + 2] = l1["fc1_b"].reshape(2, 96).T
    lw[:, V_PB:V_PB + C], lw[:, V_B2:V_B2 + C] = l1["proj_b"], l1["fc2_b"]
    mw = np.zeros((128, L2_COLS), np.float32)
    mw[:64, U_BN + 3] = 1.0
    for h in range(2):
        ch, hid = slice(64 * h, 64 * h + C), slice(32 * h, 32 * h + 12)
        mw[ch, U_W1 + 32 * h:U_W1 + 32 * h + 12] = l2["w1"].T
        w2, b2 = l2["w2"].reshape(C, 9, 12), l2["b2"].reshape(C, 9)
        for t in range(4):
            c0 = U_W2 + 112 * t + 64 * h
            mw[hid, c0:c0 + C] = w2[:, t].T
            mw[ch, U_B2 + t] = b2[:, t]
        mw[ch, U_BIAS] = l2["bias"]
        for j, a in enumerate(("gamma", "beta", "running_mean", "running_var")):
            mw[hid, U_BN + j] = l2[a]
    l3 = {k[8:]: v for k, v in inp.items() if k.startswith("L3_conv_")}
    front = np.zeros((112, 96), np.float32)
    taps = np.zeros((112, 2, 9, 96), np.float32)
    for h in range(2):
        front[64 * h:64 * h + C] = l3["W_in"].T
        taps[64 * h:64 * h + C, h] = l3["W_dw"].reshape(96, 9).T
    raw = np.concatenate([l3["W_w"], l3["W_l"], l3["W_u"], l3["W_d"]]).T
    raw = np.tile(raw, (8, 1))
    qw = np.zeros((128, L3_COLS), np.float32)
    qw[:96, Q_XD:Q_XD + 128] = np.tile(l3["W_xd"].T, (1, 8))
    qw[:96, Q_OUT:Q_OUT + 48] = l3["W_out"].T
    qw[:, Q_ONE:Q_ONE + 96] = 1.0
    for c, a in ((Q_BDW, "b_dw"), (Q_LN, "ln_w"), (Q_LN + 1, "ln_b"), (Q_GRN, "grn_gamma"), (Q_GRN + 1, "grn_beta")):
        qw[:96, c] = l3[a]
    qw[:, Q_WM:Q_WM + 4] = l3["w_m"]
    for blk, part in enumerate((0, 1, 0, 1, 2, None, 0, 1)):
        if part is not None:
            qw[16 * blk:16 * blk + 16, Q_MASK + part] = 1.0
    spread = np.zeros((16, 16, 96), np.float32)
    spread[np.arange(16), np.arange(16)] = 1.0
    return {"conv_in": cw, "sed_in": sed, "sign_in": signs, "l1_in": lw, "l2_in": mw,
            "front_in": front, "taps_in": taps, "gates_in": raw, "l3_in": qw, "spread_in": spread}


def first_layer_arrays(inp):
    x = inp["x"].reshape(8, 2, C, 2, 2, 4, 4, 4)
    x = x.transpose(0, 4, 6, 5, 7, 1, 3, 2).reshape(8, 128, TILES, C)
    x = np.concatenate([x, x[-2:]], 0)
    l0 = {k[8:]: v for k, v in inp.items() if k.startswith("L0_conv_")}
    bias, mask = bias_layout(l0["rpb"])
    fn = np.zeros((KA, 2 + HEADS), np.float32)
    fn[np.arange(C), 2 + np.arange(C) // HD] = 1.0
    fn[:C, 0], fn[:C, 1] = l0["fn_g"], l0["fn_b"]
    fn[C, 0] = 1.0
    return {
        "x_tok": np.ascontiguousarray(x),
        "wpack": pack_l0(*[l0[k] for k in ("qkv_w", "qkv_b", "proj_w", "proj_b", "n1_g", "n1_b", "n2_g", "n2_b",
                                         "fc1_w", "fc1_b", "fc2_w", "fc2_b")]),
        "rpb_raw": np.ascontiguousarray(bias),
        "mask_in": mask.astype(np.dtype("bfloat16")),
        "ident_in": np.eye(128, dtype=np.float32),
        "ident2_in": np.tile(np.eye(64), (2, 2)).astype(np.dtype("bfloat16")),
        "en_in": np.broadcast_to(np.stack([l0["en_g"], l0["en_b"]]), (128, 2, C)).copy(),
        "fn_in": fn,
    }


_ARGS = ["x_tok", "wpack", "rpb_raw", "mask_in", "ident_in", "ident2_in", "en_in", "fn_in", "conv_in", "sed_in", "sign_in",
         "l1_in", "l2_in", "front_in", "taps_in", "gates_in", "l3_in", "spread_in"]


def kernel(**inputs):
    import concourse.bacc as bacc
    from concourse.bass_utils import run_bass_kernel_spmd as run

    inp = {name: np.asarray(a) for name, a in inputs.items()}
    laid = {**first_layer_arrays(inp), **late_arrays(inp)}
    nc = bacc.Bacc("TRN2", target_bir_lowering=False, num_devices=1)
    arrays, args = {}, []
    for name in _ARGS:
        a = np.ascontiguousarray(laid[name])
        arrays[f"in_{name}"] = a
        args.append(nc.dram_tensor(f"in_{name}", a.shape, mybir.dt.from_np(a.dtype), kind="ExternalInput").ap())
    args.append(nc.dram_tensor("out_0", (B, C, IMG, IMG), F32, kind="ExternalOutput").ap())
    build(nc, *args)
    r = run(nc, [arrays], core_ids=[0])
    return r.results[0]["out_0"]
```

```python
import numpy as np
from contextlib import ExitStack

import concourse.bass as bass
from concourse import mybir
from concourse.alu_op_type import AluOpType as ALU

F32 = mybir.dt.float32
BF16 = mybir.dt.bfloat16
ACT = mybir.ActivationFunctionType
AX = mybir.AxisListType

B, C, IMG = 16, 48, 16
HEADS, HD, BLOCKS, MLP = 6, 8, 6, 192
N = 64
STREAMS = 2
CHUNK_B = 2
GROUPS = B // (STREAMS * CHUNK_B)
TOK = CHUNK_B * IMG * IMG
TILES = TOK // 128
PAIRS = 4
SC = HEADS * N
KA = C + 1
ZW = 65
HP = HEADS // 2
VW = 2 * HD + 2
VO = HP * VW
PADW = IMG + 2
EPS, GATE_EPS = 1e-5, 1e-7

W_QK, W_V, W_PROJ, W_FC1, W_FC2, W_GB, W_PB, W_B2 = np.cumsum([0, 128, 48, 48, 192, 96, 4, 48])
W_COLS = int(W_B2) + 48

V_PROJ, V_FC1, V_FC2, V_GB, V_F1B, V_PB, V_B2 = (int(n) for n in np.cumsum([0, 96, 2 * 192, 96, 4, 2, 48]))
L1_COLS = V_B2 + 48
DIN, HB = 96, 8 * 256
Q_XD, Q_OUT, Q_ONE, Q_BDW, Q_LN, Q_GRN, Q_WM, Q_MASK = (int(n) for n in np.cumsum([0, 128, 48, 96, 1, 2, 2, 4]))
L3_COLS = Q_MASK + 3
U_W1, U_W2, U_BN, U_B2, U_BIAS = (int(n) for n in np.cumsum([0, 64, 4 * 112, 4, 4]))
L2_COLS = U_BIAS + 1


M_MEAN, M_VAR, M_RT, M_SPREAD, M_GM, M_OUT, M_ALL = (int(n) for n in np.cumsum([0, 4, 1, 1, 4, 1, 4]))
D_YC, D_VAR, D_RT, D_YN, D_V2, D_ALL = (int(n) for n in np.cumsum([0, 4, 1, 1, 4, 8]))


VAR_BANK = (6, 5)


K_ACT, K_POOL, K_DVE = (0, 1), (2,), (3, 4, 5)


class Step:
    pass


def blocks_of(shifted, u):
    if not shifted:
        return slice(2 * u, 2 * u + 2)
    return slice(1, 3) if u == 0 else slice(0, 4, 3)


def build(nc, x_tok, wpack, rpb_raw, mask_in, ident_in, ident2_in, en_in, fn_in,
          conv_in, sed_in, sign_in, l1_in, l2_in,
          front_in, taps_in, gates_in, l3_in, spread_in, out):
    with ExitStack() as ctx:

        def sb(name, shape, dt=F32):
            return ctx.enter_context(nc.sbuf_tensor(name, shape, dt))

        l01_memory, l0_memory, l1_memory = (ctx.enter_context(ExitStack()) for _ in range(3))

        def l01(name, shape, dt=F32):
            return l01_memory.enter_context(nc.sbuf_tensor(name, shape, dt))

        def l1(name, shape, dt=F32):
            return l1_memory.enter_context(nc.sbuf_tensor(name, shape, dt))

        def l0(name, shape, dt=F32):
            return l0_memory.enter_context(nc.sbuf_tensor(name, shape, dt))

        def sem(name):
            return ctx.enter_context(nc.semaphore(name))

        def sems(name, n):
            return [sem(f"{name}{i}") for i in range(n)]

        bank = [[ctx.enter_context(nc.psum_tensor(f"bank{s}{i}", [128, 512], F32)) for i in range(4)]
                for s in range(STREAMS)]
        ident = sb("ident", [128, 128])
        ident2 = sb("ident2", [128, 128], BF16)
        a2 = sb("a2", [64 + C, 8, PADW, PADW])
        front_w = sb("front_w", [64 + C, DIN])
        taps_w = sb("taps_w", [64 + C, 6, DIN])
        gates_w = sb("gates_w", [128, 6 * 4 * DIN], BF16)
        l3w = sb("l3w", [128, L3_COLS])
        spread = sb("spread", [16, 16, DIN])
        l2w = sb("l2w", [128, L2_COLS])
        neg_half8 = sb("neg_half8", [128, 16])
        half8 = sb("half8", [128, 8])
        gate_eps = sb("gate_eps", [128, 1])

        sed_w = l01("sed_w", [128, 16 * SC])
        rpb_sb = sed_w[0:N, 0:15 * SC].rearrange("p (t c) -> p t c", c=SC)
        ypad = l01("ypad", [64 + C, B, PADW, PADW])
        conv_w = l01("conv_w", [64 + C, 6, C])
        signs = l01("signs", [96, 128])
        l1w = l01("l1w", [128, L1_COLS])

        en_gb = l0("en_gb", [128, 2, C])
        fn_gb = l0("fn_gb", [KA, 2 + HEADS])
        neg_half = l0("neg_half", [128, 4])
        wts = [l0(f"wts{i}", [128, W_COLS]) for i in range(2)]
        bias_hm = l0("bias_hm", [128, 15, SC], BF16)
        bias_lm = l0("bias_lm", [128, 15, SC], BF16)
        st = []
        for s in range(STREAMS):
            t = Step()
            t.bank = bank[s]
            t.xin = l0(f"xin{s}", [128, TILES, C])
            t.x = l0(f"x{s}", [128, TILES, C])
            t.xc = l0(f"xc{s}", [128, TILES, C])
            t.sq = l0(f"sq{s}", [128, TILES, C + 1])
            t.z = l0(f"z{s}", [128, TILES, ZW])
            t.s4 = l0(f"s4{s}", [128, 4, TILES])
            t.xT = l0(f"xT{s}", [128, TOK])
            t.q = l0(f"q{s}", [128, TOK])
            t.kraw = l0(f"kraw{s}", [C, TOK])
            t.k = l0(f"k{s}", [128, HEADS, TOK])
            t.mx = l0(f"mx{s}", [128, PAIRS, HEADS])
            t.d = l0(f"d{s}", [128, PAIRS, HEADS, N])
            t.pt = l0(f"pt{s}", [128, PAIRS, HP, 128])
            t.v = l0(f"v{s}", [128, 2 * PAIRS, HP * (VO + VW)])
            t.rd = l0(f"rd{s}", [128, PAIRS * HP, 2])
            t.on = l0(f"on{s}", [128, PAIRS * C + ZW - C])
            t.oT = l0(f"oT{s}", [128, TOK])
            t.g = l0(f"g{s}", [96, 2, TOK])
            st.append(t)
        l0_memory.close()

        y2 = l1("y2", [C, 16, 256])
        x1 = l1("wx", [128, 2, 16, C])
        xc1, sq1, z1 = l1("wxc", [128, 2, 16, C]), l1("wsq", [128, 2, 16, C]), l1("wz", [128, 2, 16, C])
        st1 = l1("st1", [128, 4, 4, 8])
        xs = l1("xs", [96, 8, 256])
        hs = l1("sed_h", [96, 8, 256])
        x2 = l1("x2", [64 + C, 8, IMG, PADW])
        pooled = l1("pooled", [64 + C, 8])
        t2 = l1("t2", [64, 4, 8])
        wt2 = l1("wt2", [64 + C, 4, 8])
        graw = l1("graw", [128, 6 * 4 * DIN])
        gpart = [l1(f"gpart{i}", [128, 6 * 4 * DIN], BF16) for i in range(3)]
        g1_memory = l1_memory.enter_context(ExitStack())
        g1 = g1_memory.enter_context(nc.sbuf_tensor("hid1", [96, 4, 2048], F32))
        g1_memory.close()
        a3 = [l1(f"a3{i}", [64 + C, 8, PADW, PADW]) for i in range(2)]
        l1_memory.close()
        l01_memory.close()

        x3 = sb("x3", [DIN, B, 256])
        xb = sb("xb", [128, 8, 512], BF16)
        rest3 = [sb(f"rest3{i}", [128, 512]) for i in range(2)]
        mid3 = sb("mid3", [128, 512], BF16)
        gate = [[sb(f"gate{i}{k}", [DIN, HB]) for k in range(3)] for i in range(2)]
        mag = [sb(f"mag{k}", [DIN, HB]) for k in range(2)]
        gsum = [sb(f"gsum{i}", [DIN, HB]) for i in range(2)]
        lx = sb("lx", [DIN, HB])
        xd = sb("xd", [DIN, HB])
        hst = sb("hst", [DIN, 8, PADW, IMG])
        tmp = [sb(f"tmp{i}", [DIN, 256]) for i in range(3)]
        ysum = [sb(f"ysum{i}", [DIN, HB]) for i in range(2)]
        yc, yq = sb("yc", [DIN, HB]), sb("yq", [DIN, HB])
        tvar = sb("tvar", [128, 2, 16])
        rT = sb("rT", [16, 128])
        gx = sb("gx", [DIN, 6, 8])
        ob = yc[0:C].rearrange("p (b k) -> p b k", b=8)

        ld_const, ld_x, ld_w = sem("ld_const"), sems("ld_x", 2), sems("ld_w", 2)
        setup = sem("setup")
        ld_en, ld_rpb = sem("ld_en"), sems("ld_rpb", 3)
        split, rounded = sem("split"), sem("rounded")
        x_used = sems("x_used", 2)
        en = sems("en", 7)
        fin = sems("fin", 6)
        ln1, ln2 = sems("ln1_", 6), sems("ln2_", 6)
        pe_zT, pe_qk, pe_v, pe_S, pe_PT = sem("pe_zT"), sem("pe_qk"), sem("pe_v"), sems("pe_S", 4), sems("pe_PT", 4)
        pe_OT, on_ready = sem("pe_OT"), sem("on_ready")
        pe_O, pe_proj, pe_z2T, pe_fc1, pe_fc2 = sem("pe_O"), sem("pe_proj"), sem("pe_z2T"), sems("pe_fc1", 2), sem("pe_fc2")
        pe_fin = sem("pe_fin")
        xT_ready, xT2_ready, qk_ready, v_ready = sem("xT_ready"), sem("xT2_ready"), sems("qk_ready", 5), sem("v_ready")
        mx_ready, d_ready, p_ready, pt_ready = sems("mx_ready", 4), sems("d_ready", 4), sems("p_ready", 4), sems("pt_ready", 4)
        rd_ready, o_ready, x1_ready, x2_ready, g_ready = sem("rd_ready"), sem("o_ready"), sem("x1_ready"), sem("x2_ready"), sems("g_ready", 2)
        pb_added, b2_added, y_ready = sem("pb_added"), sem("b2_added"), sem("y_ready")
        stored = sem("stored")
        ld_sed, sed_ready, ld_late, conv_ready, y_copied, late_set = (sem(n) for n in (
            "ld_sed", "sed_ready", "ld_late", "conv_ready", "y_copied", "late_set"))
        conv_done, back_done = sem("conv_done"), sem("back_done")
        act_maps, dve_maps = sem("act_maps"), sem("dve_maps")
        var_ready, rstd_ready, norm_ready, zT_done, xs_ready, bias_added = (sem(n) for n in (
            "var_ready", "rstd_ready", "norm_ready", "zT_done", "xs_ready", "bias_added"))
        dve_step, sed_done, h_ready, proj1_done, fc1_done, g1_ready, fc2_done, x1_final = (sem(n) for n in (
            "dve_step", "sed_done", "h_ready", "proj1_done", "fc1_done", "g1_ready", "fc2_done", "x1_final"))
        x2T_done, pooled_ready, t_done, t_ready, wt_done, bn_ready, a_ready = (sem(n) for n in (
            "x2T_done", "pooled_ready", "t_done", "t_ready", "wt_done", "bn_ready", "a_ready"))
        ld_gates = sem("ld_gates")
        maps_copied = sems("maps_copied", 2)
        x3_done, x3_ready, px_done, px_hi, px_left, xb_ready = (sem(n) for n in (
            "x3_done", "x3_ready", "px_done", "px_hi", "px_left", "xb_ready"))
        gate_done, gate_taken = sems("gate_done", 3), sems("gate_taken", 3)
        lud_done, lud_taken = sem("lud_done"), sem("lud_taken")
        sum_ready, y_added, recip_done, guess_ready = (sem(n) for n in (
            "sum_ready", "y_added", "recip_done", "guess_ready"))
        tail_pe, tail_dve = sem("tail_pe"), sem("tail_dve")
        yq_ready, trstd_ready, v_norm, gx2_ready, gx_ready, out_ready = (
            sem(n) for n in ("yq_ready", "trstd_ready", "v_norm", "gx2_ready", "gx_ready", "out_ready"))

        block = ctx.enter_context(nc.Block())

        def group_value(eng, v, s, k):
            return k * ((v - s + 1) // 2) if isinstance(v, int) else eng.snap((v + (1 - s)) // 2 * k)

        def pipeline(eng, slot, first, last, begin=None, after=None):
            def step(n, v, lp, wv, **kw):
                o = Step()
                o.t, o.par, o.v, o.lp, o.wv = st[n % 2], n // 2 % 2, v, lp, wv
                o.first, o.before = kw.get("first"), kw.get("before")
                return o

            if first:
                first(0, 1)
            if begin:
                begin()
            slot(step(0, 1, 0, 16, first=1 if first else None), None)
            if after:
                after()
            with eng.Fori(0, GROUPS) as g:
                ga = [eng.snap(g * 2 + k) for k in (1, 2, 3)]
                start = dict(first=ga[1], before=ga[0])
                if first:
                    first(1, ga[1])
                with eng.Fori(0, 2) as lp:
                    vs = [eng.snap(g * 12 + lp * 4 + (k + 1)) for k in range(5)]
                    wv = eng.snap(g * 48 + lp * 16 + 16)
                    wn = eng.snap(g * 48 + lp * 16 + 32)
                    for k in range(1, 5):
                        x = step(k % 4, vs[k], lp if k < 4 else lp + 1, wv if k < 4 else wn, **start if k == 1 else {})
                        slot(x, step(k - 1, vs[k - 1], lp, wv))
                vs = [eng.snap(g * 12 + (8 + k + 1)) for k in range(5)]
                wv, wn = eng.snap(g * 48 + 48), eng.snap(g * 48 + 64)
                for k in range(1, 4):
                    slot(step(k, vs[k], 2, wv), step(k - 1, vs[k - 1], 2, wv))
                last(0, ga[0])
                if first:
                    first(0, ga[2])
                slot(step(0, vs[4], 0, wn, first=ga[2], before=ga[1]), step(3, vs[3], 2, wv))
                last(1, ga[1])

        def tokens(ap):
            return ap.rearrange("p (b y x i) -> p b y x i", b=CHUNK_B, y=4, x=4)

        def chunk(t, n):
            return t[:, n % 2, 8 * (n // 2):8 * (n // 2) + 8, :]

        B8 = bank[0] + bank[1]

        def x2_rows(k):
            h, iy = k % 2, k // 2
            v = x2[64 * h:64 * h + C].rearrange("p b (y j) x -> p (b y) j x", j=4)
            return v[:, :, iy, 1:1 + IMG].rearrange("p y (x i) -> p y x i", i=4)

        @block.sync
        def _(sp):
            sp.dma_start(st[0].xin[:], x_tok[0]).then_inc(ld_x[0], 16)
            sp.dma_start(en_gb[:], en_in).then_inc(ld_en, 16)
            for k in range(3):
                sp.dma_start(rpb_sb[:, 5 * k:5 * k + 5], rpb_raw[:, 5 * k:5 * k + 5]).then_inc(ld_rpb[k], 16)
            for dst, src in ((ident[:], ident_in), (ident2[:], ident2_in), (bias_lm[64:128], mask_in), (fn_gb[:], fn_in)):
                sp.dma_start(dst, src).then_inc(ld_const, 16)
            for par in range(2):
                sp.dma_start(wts[par][:], wpack[par]).then_inc(ld_w[par], 16)
            sp.dma_start(st[1].xin[:], x_tok[1]).then_inc(ld_x[1], 16)
            for dst, src in ((conv_w[:], conv_in), (l1w[:], l1_in), (l2w[:], l2_in), (front_w[:], front_in),
                             (taps_w[:], taps_in), (l3w[:], l3_in), (spread[:], spread_in)):
                sp.dma_start(dst, src).then_inc(ld_late, 16)

            def reload(par, nxt, done):
                sp.wait_ge(pe_fc2, done)
                sp.wait_ge(b2_added, done)
                sp.dma_start(wts[par][:], nxt).then_inc(ld_w[par], 16)

            sp.wait_ge(split, 6)
            sp.dma_start(sed_w[0:96, :], sed_in).then_inc(ld_sed, 16)
            sp.dma_start(signs[:], sign_in).then_inc(ld_sed, 16)
            with sp.Fori(0, GROUPS) as g:
                sp.wait_ge(x_used[0], g + 1)
                sp.dma_start(st[0].xin[:], x_tok[bass.ds(g * STREAMS + 2, 1)].rearrange("a p t c -> (a p) t c")).then_inc(ld_x[0], 16)
                sp.wait_ge(x_used[1], g + 1)
                sp.dma_start(st[1].xin[:], x_tok[bass.ds(g * STREAMS + 3, 1)].rearrange("a p t c -> (a p) t c")).then_inc(ld_x[1], 16)
                with sp.Fori(0, BLOCKS // 2) as lp:
                    for par in range(2):
                        reload(par, wpack[bass.ds(lp * 2 + (2 + par), 1)].rearrange("a p c -> (a p) c"),
                               sp.snap(g * 12 + lp * 4 + (2 * par + 2)))
            for s in range(STREAMS):
                sp.wait_ge(ld_x[s], 16 * (GROUPS + 1))
            for par in range(2):
                sp.wait_ge(ld_w[par], 16 * (GROUPS * 3 + 1))
            sp.wait_ge(y_copied, 8)
            sp.wait_ge(fin[5], 8)
            sp.dma_start(graw[:], gates_in).then_inc(ld_gates, 16)
            for hb in range(2):
                for e in range(4):
                    sp.wait_ge(out_ready, 4 * hb + e + 1)
                    sp.dma_start(out[8 * hb + 2 * e:8 * hb + 2 * e + 2].rearrange("b c y x -> c b (y x)"),
                                 ob[:, 2 * e:2 * e + 2, :]).then_inc(stored, 16)
            sp.wait_ge(stored, 16 * 8)

        @block.gpsimd
        def _(pool):
            pool.memset(neg_half[:], -0.5).then_inc(setup, 1)
            for s in range(STREAMS):
                pool.memset(st[s].sq[:, :, C:C + 1], C * EPS).then_inc(setup, 1)
                pool.memset(st[s].z[:, :, C:ZW], 1.0).then_inc(setup if s else pe_fin, 1)
            pool.wait_ge(setup, 2 * STREAMS)

            def begin():
                for s in range(STREAMS):
                    for zeroed in (st[s].v, st[s].xT, st[s].q, st[s].k, st[s].oT, st[s].on):
                        pool.memset(zeroed[:], 0.0).then_inc(setup, 1)
                pool.wait_ge(setup, 8 * STREAMS)
                for s in range(STREAMS):
                    for r in range(2):
                        pool.memset(st[s].v[64 * r:64 * r + 64].rearrange("p w (h c) -> p w h c", h=HP)[:, :, :, 2 * HD + r:2 * HD + r + 1],
                                    1.0).then_inc(setup, 1)
                pool.wait_ge(setup, 10 * STREAMS)
                pool.wait_ge(ld_const, 16 * 4)

            def rstd(t, chain, v):
                pool.wait_ge(chain[3], v)
                pool.tensor_tensor(t.s4[:, 3, :], t.s4[:, 2, :], neg_half[:], ALU.pow).then_inc(chain[4], 1)

            def bcast(ap):
                return ap.unsqueeze(1).to_broadcast([128, TILES, C])

            def add_bias(t, col, chain, done, v, w):
                pool.wait_ge(chain[5], v)
                pool.tensor_tensor(t.x[:], t.x[:], bcast(w[:, col:col + C]), ALU.add).then_inc(done, 1)

            def slot(x, y):
                if x:
                    rstd(x.t, ln1, x.v)
                    pool.wait_ge(ld_w[x.par], x.wv)
                    add_bias(x.t, W_PB, ln1, pb_added, x.v, wts[x.par])
                if y:
                    rstd(y.t, ln2, y.v)
                if x:
                    pool.wait_ge(qk_ready[0], x.v)
                    for h in K_POOL:
                        op = pool.tensor_tensor(x.t.k[0:C, h], x.t.kraw[:], fn_gb[0:C, 2 + h:3 + h].to_broadcast([C, TOK]), ALU.mult)
                    op.then_inc(qk_ready[3], 1)
                if y:
                    add_bias(y.t, W_B2, ln2, b2_added, y.v, wts[y.par])

            def last(s, v):
                rstd(st[s], fin, v)
                pool.wait_ge(y_ready, pool.snap(v + 1))
                imgs = bass.ds(v * CHUNK_B - CHUNK_B, CHUNK_B)
                pool.tensor_copy(ypad[64:64 + C, imgs, 0:PADW - 1, :], ypad[0:C, imgs, 1:PADW, :]).then_inc(y_copied, 1)
                pool.wait_ge(y_copied, v)

            pipeline(pool, slot, lambda s, v: rstd(st[s], en, v), last, begin,
                     lambda: pool.memset(ypad[:], 0.0).then_inc(y_ready, 1))

            pool.wait_ge(ld_sed, 32)
            sw = sed_w[0:96, :].rearrange("p (k e) -> p k e", e=C)
            pool.tensor_tensor(sw, sw, signs[:].unsqueeze(2).to_broadcast([96, 128, C]), ALU.mult).then_inc(sed_ready, 1)
            pool.wait_ge(y_ready, 9)
            pool.wait_ge(fin[5], 8)
            pool.wait_ge(pe_fin, 9)
            for k in range(2):
                pool.wait_ge(ld_w[k], 16 * (GROUPS * 3 + 1))
                pool.wait_ge(ld_x[k], 16 * (GROUPS + 1))
            pool.wait_ge(ld_late, 16 * 7)
            pool.memset(neg_half8[:], -0.5).then_inc(late_set, 1)
            pool.memset(half8[:], 0.5).then_inc(late_set, 1)
            pool.memset(gate_eps[:], GATE_EPS).then_inc(late_set, 1)
            pool.memset(x2[:], 0.0).then_inc(late_set, 1)
            pool.memset(a2[:], 0.0).then_inc(late_set, 1)
            pool.wait_ge(late_set, 5)

            def bcast8(ap):
                return ap.unsqueeze(1).to_broadcast([128, 8, C])

            for k, col in enumerate((V_PB, V_B2)):
                for n in range(4):
                    pool.wait_ge(var_ready, 4 * k + n + 1)
                    pool.tensor_tensor(st1[:, n, 3], st1[:, n, 2], neg_half8[:, 0:8], ALU.pow).then_inc(rstd_ready, 1)
                    pool.tensor_tensor(chunk(x1, n), chunk(x1, n), bcast8(l1w[:, col:col + C]), ALU.add).then_inc(bias_added, 1)

            bn_var = l2w[0:64, U_BN + 3:U_BN + 4]
            pool.tensor_scalar(bn_var, bn_var, EPS, None, ALU.add).then_inc(bn_ready, 1)
            pool.wait_ge(bn_ready, 1)
            pool.tensor_tensor(bn_var, bn_var, neg_half8[0:64, 0:1],
                               ALU.pow).then_inc(bn_ready, 1)

            pool.wait_ge(x1_final, 4)
            for half in a3:
                pool.memset(half[:], 0.0).then_inc(late_set, 1)
            pool.wait_ge(late_set, 7)
            for e in range(4):
                pool.wait_ge(a_ready, 8 * e + 8)
                for shift in range(2):
                    src = a2[64:64 + C, 2 * e:2 * e + 2, shift:PADW, :]
                    dst = a3[1][64 * shift:64 * shift + C, 2 * e:2 * e + 2, 0:PADW - shift, :]
                    if e or shift:
                        pool.wait_ge(maps_copied[1], 2 * e + shift)
                    pool.tensor_copy(dst, src).then_inc(maps_copied[1], 1)
            pool.wait_ge(maps_copied[1], 8)
            pool.wait_ge(a_ready, 32)
            pool.memset(hst[:], 0.0).then_inc(late_set, 1)
            def tail_rstd(hb):
                pool.wait_ge(tail_dve, D_ALL * hb + D_VAR + 1)
                pool.tensor_tensor(tvar[:, 1], tvar[:, 0], neg_half8[:], ALU.pow).then_inc(trstd_ready, 1)

            def tail_norms(hb):
                pool.wait_ge(gx2_ready, 8 * hb + 8)
                pool.tensor_tensor(gx[:, 1], gx[:, 0], half8[0:DIN], ALU.pow).then_inc(gx_ready, 1)

            def magnitudes(u):
                for k in range(3):
                    pool.wait_ge(gate_taken[k], 4 * u + 4)
                pool.tensor_tensor(mag[0][:], mag[0][:], mag[1][:], ALU.add).then_inc(sum_ready, 1)
                pool.wait_ge(sum_ready, 2 * u + 1)
                pool.tensor_tensor(gsum[u % 2][:], gsum[u % 2][:], mag[0][:], ALU.add).then_inc(sum_ready, 1)

            magnitudes(0)
            for u in range(8):
                y, d = ysum[u // 4], u % 4
                pool.wait_ge(lud_taken, 12 * u + 8)
                if d:
                    pool.wait_ge(y_added, 2 * u)
                    pool.tensor_tensor(y[:], y[:], xd[:], ALU.add).then_inc(y_added, 1)
                if u < 7:
                    magnitudes(u + 1)
                if u == 5:
                    tail_rstd(0)
                if u == 6:
                    tail_norms(0)
                pool.wait_ge(lud_taken, 12 * u + 12)
                if d:
                    pool.wait_ge(y_added, 2 * u + 1)
                    pool.tensor_tensor(y[:], y[:], gsum[u % 2][:], ALU.add).then_inc(y_added, 1)
                else:
                    pool.tensor_tensor(y[:], y[:], gsum[u % 2][:], ALU.add).then_inc(y_added, 2)
                if u == 7:
                    tail_rstd(1)
                    tail_norms(1)

        @block.vector
        def _(dve):
            def variance(t, src, chain, v):
                dve.tensor_reduce(t.s4[:, 0, :], src[:], AX.X, ALU.add).then_inc(chain[0], 1)
                dve.wait_ge(chain[0], v)
                dve.scalar_tensor_tensor(t.xc[:], t.s4[:, 0, :].unsqueeze(2).to_broadcast([128, TILES, C]), -1.0 / C,
                                         src[:], ALU.mult, ALU.add).then_inc(chain[1], 1)
                dve.wait_ge(chain[1], v)
                dve.tensor_tensor(t.sq[:, :, 0:C], t.xc[:], t.xc[:], ALU.mult).then_inc(chain[2], 1)
                dve.wait_ge(chain[2], v)
                dve.tensor_reduce(t.s4[:, 2, :], t.sq[:], AX.X, ALU.add).then_inc(chain[3], 1)

            def normalise(t, dst, chain, v):
                dve.wait_ge(chain[4], v)
                dve.scalar_tensor_tensor(dst[:, :, 0:C], t.xc[:], C ** 0.5, t.s4[:, 3, :].unsqueeze(2).to_broadcast([128, TILES, C]),
                                         ALU.mult, ALU.mult).then_inc(chain[5], 1)

            def norm(t, src, dst, chain, v):
                variance(t, src, chain, v)
                normalise(t, dst, chain, v)

            def take_k(t, v):
                dve.wait_ge(qk_ready[0], v)
                for h in K_DVE:
                    op = dve.tensor_scalar(t.k[0:C, h], t.kraw[:], fn_gb[0:C, 2 + h:3 + h], None, ALU.mult)
                op.then_inc(qk_ready[2], 1)

            def take_v(t, v):
                dve.wait_ge(pe_v, v)
                src = t.bank[2][:, 0:PAIRS * C].rearrange("p (q h c) -> p q h c", q=PAIRS, h=HP)
                dst = t.v[:].rearrange("p (q w) (h c) -> p q w h c", q=PAIRS, h=HP)
                for w in range(2):
                    for r in range(2):
                        op = dve.tensor_copy(dst[64 * r:64 * r + 64, :, w, :, HD * r:HD * r + HD],
                                             src[64 * w:64 * w + 64, :, :, HD * r:HD * r + HD])
                op.then_inc(v_ready, 1)

            def center(t, p, v):
                dve.wait_ge(pe_S[p], v)
                s = t.bank[p][:, 0:SC].rearrange("p (h m) -> p h m", h=HEADS)
                dve.tensor_reduce(t.mx[:, p], s, AX.X, ALU.max).then_inc(mx_ready[p], 1)
                dve.wait_ge(mx_ready[p], v)
                dve.tensor_tensor(t.d[:, p], s, t.mx[:, p].unsqueeze(2).to_broadcast([128, HEADS, N]),
                                  ALU.subtract).then_inc(d_ready[p], 1)

            def divide_o(t, v):
                dve.wait_ge(pe_O, v)
                o = t.bank[0][:, 0:PAIRS * HP * VW].rearrange("p (q c) -> p q c", c=VW)
                dve.reciprocal(t.rd[:], o[:, :, 2 * HD:VW]).then_inc(rd_ready, 1)
                dve.wait_ge(rd_ready, v)
                dve.tensor_tensor(t.on[:, 0:PAIRS * C].rearrange("p (q r c) -> p q r c", r=2, c=HD), o[:, :, 0:2 * HD].rearrange("p q (r c) -> p q r c", r=2),
                                  t.rd[:].unsqueeze(3).to_broadcast([128, PAIRS * HP, 2, HD]), ALU.mult).then_inc(on_ready, 1)

            def take_o(t, v):
                dve.wait_ge(pe_OT, v)
                dve.tensor_copy(t.oT[0:C], t.bank[1][0:C, :]).then_inc(o_ready, 1)

            def add_res(t, bk, pe_done, bias_done, ready, v):
                dve.wait_ge(pe_done, v)
                dve.wait_ge(bias_done, v)
                dve.tensor_tensor(t.x[:], bk[:, 0:TILES * C].rearrange("p (t c) -> p t c", t=TILES), t.x[:],
                                  ALU.add).then_inc(ready, 1)
                dve.wait_ge(ready, v)

            def first(s, v):
                t = st[s]
                dve.wait_ge(ld_x[s], group_value(dve, v, s, 16))
                norm(t, t.xin, t.x, en, v)
                dve.wait_ge(en[5], v)
                gb = en_gb[:].unsqueeze(2).to_broadcast([128, 2, TILES, C])
                dve.tensor_tensor(t.x[:], t.x[:], gb[:, 0], ALU.mult).then_inc(x_used[s], 1)
                dve.wait_ge(x_used[s], group_value(dve, v, s, 1))
                dve.tensor_tensor(t.x[:], t.x[:], gb[:, 1], ALU.add).then_inc(en[6], 1)

            def last(s, v):
                norm(st[s], st[s].x, st[s].z, fin, v)

            def slot(x, y):
                if x:
                    if x.first is not None:
                        dve.wait_ge(en[6], x.first)
                        if x.before is not None:
                            dve.wait_ge(pe_fin, x.before)
                    variance(x.t, x.t.x, ln1, x.v)
                if y:
                    divide_o(y.t, y.v)
                if x:
                    normalise(x.t, x.t.z, ln1, x.v)
                if y:
                    take_o(y.t, y.v)
                    add_res(y.t, y.t.bank[2], pe_proj, pb_added, x1_ready, y.v)
                    variance(y.t, y.t.x, ln2, y.v)
                if x:
                    take_k(x.t, x.v)
                if y:
                    normalise(y.t, y.t.z, ln2, y.v)
                if x:
                    take_v(x.t, x.v)
                    for p in range(PAIRS):
                        center(x.t, p, x.v)
                if y:
                    add_res(y.t, y.t.bank[0], pe_fc2, b2_added, x2_ready, y.v)

            def rest(k, first_parts):
                tables = slice(5 * k, 5 * k + 5)
                dve.wait_ge(rounded, first_parts)
                dve.tensor_tensor(rpb_sb[:, tables], rpb_sb[:, tables], bias_hm[0:64, tables], ALU.subtract).then_inc(split, 1)

            def third_parts(k, second_parts):
                tables = slice(5 * k, 5 * k + 5)
                dve.wait_ge(rounded, second_parts)
                dve.tensor_tensor(bias_lm[0:64, tables], rpb_sb[:, tables], bias_lm[0:64, tables], ALU.subtract).then_inc(split, 1)

            def begin():
                rest(0, 1)
                rest(1, 2)
                third_parts(0, 4)
                rest(2, 5)
                dve.wait_ge(setup, 10 * STREAMS)
                dve.wait_ge(ld_const, 16 * 4)

            def after():
                third_parts(1, 7)
                third_parts(2, 9)

            dve.wait_ge(pe_fin, 1)
            dve.wait_ge(ld_en, 16)
            pipeline(dve, slot, first, last, begin, after)

            dve.wait_ge(y_ready, 9)
            dve.wait_ge(pe_fin, 9)
            for k in range(2):
                dve.wait_ge(ld_w[k], 16 * (GROUPS * 3 + 1))
                dve.wait_ge(ld_x[k], 16 * (GROUPS + 1))
            dve.wait_ge(y_copied, 8)
            chain = [0]

            def step(op):
                chain[0] += 1
                op.then_inc(dve_step, 1)
                dve.wait_ge(dve_step, chain[0])

            dve.wait_ge(ld_late, 16 * 7)
            dve.tensor_tensor(conv_w[64:64 + C, 1, :], conv_w[64:64 + C, 1, :], ident[64:64 + C, 64:64 + C], ALU.add).then_inc(conv_ready, 1)

            step(dve.tensor_tensor(taps_w[:], taps_w[:], front_w[:].unsqueeze(1).to_broadcast([64 + C, 6, DIN]), ALU.mult))
            dve.wait_ge(ld_gates, 16)
            for g in (4, 5):
                cols = graw[:, g * 4 * DIN:(g + 1) * 4 * DIN].rearrange("p (d c) -> p d c", d=4)
                step(dve.tensor_tensor(cols, cols, l3w[:, Q_WM:Q_WM + 4].unsqueeze(2).to_broadcast([128, 4, DIN]), ALU.mult))
            for k in range(3):
                step(dve.tensor_copy(gpart[k][:], graw[:]))
                if k < 2:
                    step(dve.tensor_tensor(graw[:], graw[:], gpart[k][:], ALU.subtract))
            step(dve.tensor_scalar(gates_w[:], gpart[0][:], l3w[:, Q_MASK:Q_MASK + 1], None, ALU.mult))
            for k in (1, 2):
                step(dve.scalar_tensor_tensor(gates_w[:], gpart[k][:], l3w[:, Q_MASK + k:Q_MASK + k + 1], gates_w[:],
                                              ALU.mult, ALU.add))
            for t in (1, 3, 5, 7):
                dve.wait_ge(conv_done, t + 1)
                dve.tensor_copy(y2[:, 2 * t:2 * t + 2, :].rearrange("p i w -> p (i w)"), B8[t][0:C, :]).then_inc(dve_maps, 1)

            def b8(ap):
                return ap.unsqueeze(2).to_broadcast([128, 8, C])

            def half_norms(k, source):
                for n in range(4):
                    source(n)
                    x, xc, sq = chunk(x1, n), chunk(xc1, n), chunk(sq1, n)
                    step(dve.tensor_reduce(st1[:, n, 0], x, AX.X, ALU.add))
                    step(dve.scalar_tensor_tensor(xc, b8(st1[:, n, 0]), -1.0 / C, x, ALU.mult, ALU.add))
                    step(dve.tensor_tensor(sq, xc, xc, ALU.mult))
                    step(dve.tensor_reduce(st1[:, n, 1], sq, AX.X, ALU.add))
                    dve.tensor_scalar(st1[:, n, 2], st1[:, n, 1], 1.0 / C, EPS, ALU.mult, ALU.add).then_inc(var_ready, 1)
                for n in range(4):
                    dve.wait_ge(rstd_ready, 4 * k + n + 1)
                    dve.tensor_tensor(chunk(z1, n), chunk(xc1, n), b8(st1[:, n, 3]), ALU.mult).then_inc(norm_ready, 1)

            def take_conv(n):
                dve.wait_ge(back_done, n + 1)
                step(dve.tensor_copy(chunk(x1, n), B8[n][:, 0:8 * C].rearrange("p (i c) -> p i c", c=C)))

            def add_back(n, bk, done, k, final=None):
                dve.wait_ge(done, 1 + n // 2)
                dve.wait_ge(bias_added, 4 * k + n + 1)
                op = dve.tensor_tensor(chunk(x1, n), B8[bk + n][:, 0:8 * C].rearrange("p (i c) -> p i c", c=C),
                                       chunk(x1, n), ALU.add)
                op.then_inc(final, 1) if final else step(op)

            half_norms(0, take_conv)
            half_norms(1, lambda n: add_back(n, 4, proj1_done, 0))
            for n in range(4):
                add_back(n, 0, fc2_done, 1, x1_final)

            for k in (1, 3, 5, 7):
                dve.wait_ge(x2T_done, k + 1)
                dve.tensor_copy(x2_rows(k), B8[(4 + k) % 8][0:C, :].rearrange("p (i y x) -> p y x i", i=4, x=4)).then_inc(dve_maps, 1)
            dve.wait_ge(act_maps, 8)
            dve.wait_ge(dve_maps, 8)
            dve.tensor_reduce(pooled[:], x2[:, :, :, 1:1 + IMG], AX.XY, ALU.add).then_inc(pooled_ready, 1)
            dve.wait_ge(bn_ready, 2)
            bn = [l2w[0:64, U_BN + k:U_BN + k + 1] for k in range(4)]
            step(dve.tensor_tensor(bn[0], bn[0], bn[3], ALU.mult))
            dve.wait_ge(t_done, 1)
            step(dve.tensor_scalar(t2[:, 0], B8[4][0:64, 0:8], 1.0 / 256, bn[2], ALU.mult, ALU.subtract))
            step(dve.tensor_scalar(t2[:, 1], t2[:, 0], bn[0], bn[1], ALU.mult, ALU.add))
            dve.tensor_scalar(t2[:, 2], t2[:, 1], 0.0, None, ALU.max).then_inc(t_ready, 1)
            dve.wait_ge(wt_done, 1)
            step(dve.tensor_tensor(wt2[:], B8[5][0:112, 0:32].rearrange("p (t b) -> p t b", t=4),
                                   l2w[0:112, U_B2:U_B2 + 4].unsqueeze(2).to_broadcast([112, 4, 8]), ALU.add))
            for j0 in range(0, 8, 2):
                for n, tap in enumerate((3, 0, 1, 2)):
                    for j in (j0, j0 + 1):
                        if tap == 3:
                            dve.tensor_scalar(a2[:, j, 1:17, 1:17], x2[:, j, :, 0:16], wt2[:, 3, j:j + 1],
                                              l2w[0:112, U_BIAS:U_BIAS + 1], ALU.mult, ALU.add).then_inc(a_ready, 1)
                        else:
                            dve.wait_ge(a_ready, 4 * j0 + 2 * n - 1 + j - j0)
                            dve.scalar_tensor_tensor(a2[:, j, 2:17, 1:17], x2[:, j, 0:15, tap:tap + 16], wt2[:, tap, j:j + 1],
                                                     a2[:, j, 2:17, 1:17], ALU.mult, ALU.add).then_inc(a_ready, 1)
            dve.wait_ge(a_ready, 32)

            for e in range(8):
                px, r = B8[4 + e % 2], rest3[e % 2]
                dve.wait_ge(px_hi, e + 1)
                dve.tensor_tensor(r[:], px[:], xb[:, e, :], ALU.subtract).then_inc(px_left, 1)
                dve.wait_ge(px_left, e + 1)
                dve.tensor_copy(xb[32:64, e, :], r[32:64]).then_inc(xb_ready, 1)
                step(dve.tensor_copy(mid3[96:128], r[96:128]))
                dve.tensor_tensor(xb[96:128, e, :], r[96:128], mid3[96:128], ALU.subtract).then_inc(xb_ready, 1)

            def seen(imgs, d):
                v = x3[:, imgs, :].rearrange("p b (y x) -> p b y x", x=IMG)
                if d == 0:
                    return v
                if d == 1:
                    return v.rearrange("p b y x -> p b x y")
                if d == 2:
                    return v[:, :, :, ::-1]
                return v[:, :, ::-1, :].rearrange("p b y x -> p b x y")

            def rows(t, s):
                return t[:].rearrange("p (b k s) -> p b k s", b=8, s=8)[:, :, :, s]

            def state(shift, s):
                v = hst[:, :, 1 + shift:1 + shift + IMG, :]
                return v.rearrange("p b y (n s) -> p b (y n) s", s=8)[:, :, :, s]

            def t8(i):
                return tmp[i][:].rearrange("p (b k) -> p b k", b=8)

            def unit(u):
                hb, d = u // 4, u % 4
                gl, gm, gr = gate[u % 2]
                if u == 6:
                    tail(0, (2,))
                rgate = gsum[u % 2]
                for i in range(8):
                    e = i // 2
                    if i == 1 and d and u > 1:
                        dve.wait_ge(y_added, 2 * u - 1 if d > 1 else 2 * u - 3)
                    dve.wait_ge(lud_done, 12 * u + i + 1)
                    imgs = slice(8 * hb + 2 * e, 8 * hb + 2 * e + 2)
                    dve.tensor_tensor((lx, xd if d else ysum[hb])[i % 2][:, 512 * e:512 * (e + 1)].rearrange("p (b y x) -> p b y x", b=2, y=IMG),
                                      B8[3 + i % 3][0:DIN, :].rearrange("p (b y x) -> p b y x", b=2, y=IMG),
                                      seen(imgs, d), ALU.mult).then_inc(lud_taken, 1)
                if u in (5, 6):
                    tail(0, (0,) if u == 5 else (3,))
                dve.wait_ge(guess_ready, 2 * u + 2)
                dve.scalar_tensor_tensor(rgate[:], rgate[:], GATE_EPS, mag[1][:], ALU.add, ALU.mult).then_inc(recip_done, 1)
                dve.wait_ge(recip_done, 2 * u + 1)
                dve.scalar_tensor_tensor(rgate[:], rgate[:], -2.0, mag[1][:], ALU.add, ALU.mult).then_inc(recip_done, 1)
                dve.wait_ge(recip_done, 2 * u + 2)
                dve.wait_ge(lud_taken, 12 * u + 8)
                if u == 0:
                    dve.wait_ge(late_set, 8)
                step(dve.tensor_copy(state(0, 0), rows(lx, 0)))
                for s in range(1, 8):
                    for k, g in enumerate((gl, gm, gr)):
                        dve.tensor_tensor(t8(k), rows(g, s), state(k - 1, s - 1), ALU.mult).then_inc(dve_step, 1)
                    chain[0] += 3
                    dve.wait_ge(dve_step, chain[0] - 1)
                    for k in range(4):
                        for half in range(2):
                            b = slice(4 * half, 4 * half + 4)
                            if k:
                                dve.wait_ge(dve_step, chain[0] - 1)
                            t0 = t8(0)[:, b]
                            if k < 2:
                                op = dve.tensor_tensor(t0, t0, t8(k + 1)[:, b], ALU.add)
                            elif k == 2:
                                op = dve.tensor_tensor(t0, t0, rows(rgate, s)[:, b], ALU.mult)
                            else:
                                op = dve.tensor_tensor(state(0, s)[:, b], rows(lx, s)[:, b], t0, ALU.subtract)
                            op.then_inc(dve_step, 1)
                            chain[0] += 1
                    dve.wait_ge(dve_step, chain[0])
                if u in (5, 6):
                    tail(0, (1,) if u == 5 else (4,))
                for e in range(4):
                    if e == 0:
                        dve.wait_ge(dve_step, chain[0])
                    dve.wait_ge(lud_done, 12 * u + 8 + e + 1)
                    dve.tensor_tensor(gsum[u % 2][:, 512 * e:512 * (e + 1)].rearrange("p (b k) -> p b k", b=2),
                                      B8[3 + (8 + e) % 3][0:DIN, :].rearrange("p (b k) -> p b k", b=2),
                                      hst[:, 2 * e:2 * e + 2, 1:1 + IMG, :].rearrange("p b y x -> p b (y x)"),
                                      ALU.mult).then_inc(lud_taken, 1)
                dve.wait_ge(lud_taken, 12 * u + 12)

            def tail(hb, stages):
                if 0 in stages:
                    dve.wait_ge(y_added, 8 * hb + 8)
                    if hb:
                        dve.wait_ge(stored, 16 * 4)
                    for e in range(4):
                        cols = slice(512 * e, 512 * (e + 1))
                        dve.wait_ge(tail_pe, M_ALL * hb + M_MEAN + e + 1)
                        dve.scalar_tensor_tensor(yc[:, cols], B8[6 + e % 2][0:DIN, :], -1.0 / DIN, ysum[hb][:, cols],
                                                 ALU.mult, ALU.add).then_inc(tail_dve, 1)
                if 1 in stages:
                    dve.wait_ge(tail_pe, M_ALL * hb + M_VAR + 1)
                    dve.tensor_scalar(tvar[:, 0], B8[VAR_BANK[hb]][:, 0:16], 1.0 / DIN, EPS, ALU.mult, ALU.add).then_inc(tail_dve, 1)
                if 2 in stages:
                    dve.wait_ge(tail_pe, M_ALL * hb + M_RT + 1)
                    dve.tensor_copy(rT[:], B8[7][0:16, 0:128]).then_inc(tail_dve, 1)
                if 3 in stages:
                    for e in range(4):
                        cols = slice(512 * e, 512 * (e + 1))
                        dve.wait_ge(tail_pe, M_ALL * hb + M_SPREAD + e + 1)
                        dve.tensor_tensor(yq[:, cols], B8[6 + e % 2][0:DIN, :], yc[:, cols], ALU.mult).then_inc(tail_dve, 1)
                if 4 in stages:
                    dve.wait_ge(tail_pe, M_ALL * hb + M_GM + 1)
                    step(dve.tensor_scalar(gx[:, 2], B8[6][0:DIN, 0:8], 1.0 / DIN, 1e-6, ALU.mult, ALU.add))
                    step(dve.reciprocal(gx[:, 3], gx[:, 2]))
                    step(dve.tensor_tensor(gx[:, 4], gx[:, 1], gx[:, 3], ALU.mult))
                    step(dve.tensor_scalar(gx[:, 5], gx[:, 4], l3w[0:DIN, Q_GRN:Q_GRN + 1], 1.0, ALU.mult, ALU.add))
                    for b in range(8):
                        cols = slice(256 * b, 256 * (b + 1))
                        dve.tensor_scalar(yq[:, cols], yc[:, cols], gx[:, 5, b:b + 1], l3w[0:DIN, Q_GRN + 1:Q_GRN + 2],
                                          ALU.mult, ALU.add).then_inc(tail_dve, 1)

            for u in range(8):
                unit(u)
            tail(1, range(5))

        @block.scalar
        def _(act):
            def affine_windows(t, v, w):
                act.wait_ge(pe_zT, v)
                act.activation(t.xT[0:KA], t.bank[1][0:KA, :], ACT.Identity, scale=w[0:KA, W_GB:W_GB + 1],
                               bias=w[0:KA, W_GB + 1:W_GB + 2]).then_inc(xT_ready, 1)

            def affine_T(t, v, w):
                act.wait_ge(pe_z2T, v)
                act.activation(t.xT[0:KA], t.bank[1][0:KA, :], ACT.Identity, scale=w[0:KA, W_GB + 2:W_GB + 3],
                               bias=w[0:KA, W_GB + 3:W_GB + 4]).then_inc(xT2_ready, 1)

            def exponential(t, p, v):
                act.wait_ge(d_ready[p], v)
                act.activation(t.d[:, p], t.d[:, p], ACT.Exp).then_inc(p_ready[p], 1)

            def slot(x, y):
                if y:
                    for p in range(PAIRS):
                        act.wait_ge(pe_PT[p], y.v)
                        act.activation(y.t.pt[:, p].rearrange("p h n -> p (h n)"), y.t.bank[p][:, 0:SC], ACT.Copy).then_inc(pt_ready[p], 1)
                if x:
                    t, v = x.t, x.v
                    act.wait_ge(ld_w[x.par], x.wv)
                    affine_windows(t, v, wts[x.par])
                    act.wait_ge(pe_qk, v)
                    act.activation(t.kraw[:], t.bank[0][64:64 + C, :], ACT.Copy).then_inc(qk_ready[0], 1)
                    act.activation(t.q[0:C], t.bank[0][0:C], ACT.Copy, scale=HD ** -0.5).then_inc(qk_ready[1], 1)
                    act.wait_ge(qk_ready[0], v)
                    for h in K_ACT:
                        op = act.activation(t.k[0:C, h], t.kraw[:], ACT.Copy, scale=fn_gb[0:C, 2 + h:3 + h])
                    op.then_inc(qk_ready[4], 1)
                if y:
                    affine_T(y.t, y.v, wts[y.par])
                    for h in range(2):
                        act.wait_ge(pe_fc1[h], y.v)
                        act.activation(y.t.g[:, h, :], y.t.bank[2 + h][0:96, :], ACT.Gelu).then_inc(g_ready[h], 1)
                if x:
                    for p in range(PAIRS):
                        exponential(t, p, v)

            def last(s, v):
                act.wait_ge(pe_fin, act.snap(v + 1))
                src = tokens(st[s].bank[1][0:C, :]).rearrange("p b y (x) (j i) -> p b y x j i", j=4)
                for b in range(CHUNK_B):
                    for y in range(4):
                        dst = ypad[0:C, bass.ds(v * CHUNK_B + (b - CHUNK_B), 1), 1 + 4 * y:5 + 4 * y,
                                   1:1 + IMG].rearrange("p o j (x i) -> p (o x) j i", i=4)
                        op = act.activation(dst, src[:, b, y], ACT.Identity, scale=fn_gb[0:C, 0:1], bias=fn_gb[0:C, 1:2])
                op.then_inc(y_ready, 1)

            def first_parts(k):
                tables = slice(5 * k, 5 * k + 5)
                act.wait_ge(ld_rpb[k], 16)
                act.activation(bias_hm[0:64, tables], rpb_sb[:, tables], ACT.Copy).then_inc(rounded, 1)

            def second_parts(k, rest):
                tables = slice(5 * k, 5 * k + 5)
                act.wait_ge(split, rest)
                act.activation(bias_hm[64:128, tables], rpb_sb[:, tables], ACT.Copy).then_inc(rounded, 1)
                act.activation(bias_lm[0:64, tables], rpb_sb[:, tables], ACT.Copy).then_inc(rounded, 1)

            first_parts(0)
            first_parts(1)
            second_parts(0, 1)
            first_parts(2)
            second_parts(1, 2)
            act.wait_ge(ld_const, 16 * 4)

            pipeline(act, slot, None, last, None, lambda: second_parts(2, 4))

            act.wait_ge(fin[5], 8)
            for k in range(2):
                act.wait_ge(ld_w[k], 16 * (GROUPS * 3 + 1))
                act.wait_ge(ld_x[k], 16 * (GROUPS + 1))
            act.wait_ge(pe_fin, 9)
            act.wait_ge(y_copied, 8)
            act.wait_ge(ld_late, 16 * 7)
            for t in (0, 2, 4, 6):
                act.wait_ge(conv_done, t + 1)
                act.activation(y2[:, 2 * t:2 * t + 2, :].rearrange("p i w -> p (i w)"), B8[t][0:C, :], ACT.Copy).then_inc(act_maps, 1)

            def affine(k, bk, col):
                for n in range(4):
                    act.wait_ge(zT_done, 4 * k + n + 1)
                    act.activation(xs[:, 4 * (n // 2):4 * (n // 2) + 4, 128 * (n % 2):128 * (n % 2) + 128],
                                   B8[bk + n][0:96, :].rearrange("p (a w) -> p a w", a=4), ACT.Identity,
                                   scale=l1w[0:96, col:col + 1], bias=l1w[0:96, col + 1:col + 2]).then_inc(xs_ready, 1)

            affine(0, 4, V_GB)
            for t in range(4):
                act.wait_ge(sed_done, t + 1)
                act.activation(hs[:, 2 * t:2 * t + 2, :].rearrange("p c w -> p (c w)"), B8[t][0:96, :], ACT.Gelu).then_inc(h_ready, 1)
            affine(1, 0, V_GB + 2)
            for t in range(4):
                for u in range(4):
                    act.wait_ge(fc1_done, 4 * t + u + 1)
                    act.activation(g1[:, u, 512 * t:512 * (t + 1)], B8[4 + u][0:96, :], ACT.Gelu,
                                   bias=l1w[0:96, V_F1B + u % 2:V_F1B + u % 2 + 1]).then_inc(g1_ready, 1)
            act.wait_ge(late_set, 5)
            for k in (0, 2, 4, 6):
                act.wait_ge(x2T_done, k + 1)
                act.activation(x2_rows(k), B8[(4 + k) % 8][0:C, :].rearrange("p (i y x) -> p y x i", i=4, x=4), ACT.Copy).then_inc(act_maps, 1)

            def take_gates(u, e):
                cols = slice(512 * e, 512 * (e + 1))
                for k in range(3):
                    act.wait_ge(gate_done[k], 4 * u + e + 1)
                    act.activation((gsum[u % 2], mag[0], mag[1])[k][:, cols], B8[k][0:DIN, :], ACT.Abs)
                    act.activation(gate[u % 2][k][:, cols], B8[k][0:DIN, :], ACT.Copy).then_inc(gate_taken[k], 1)

            act.wait_ge(late_set, 7)
            for e in range(4):
                act.wait_ge(a_ready, 8 * e + 8)
                for shift in range(2):
                    src = a2[0:C, 2 * e:2 * e + 2, shift:PADW, :]
                    dst = a3[0][64 * shift:64 * shift + C, 2 * e:2 * e + 2, 0:PADW - shift, :]
                    act.activation(dst.rearrange("p b y x -> p b (y x)"), src.rearrange("p b y x -> p b (y x)"), ACT.Copy).then_inc(maps_copied[0], 1)
            act.wait_ge(a_ready, 32)
            for e in range(9):
                if e < 8:
                    act.wait_ge(x3_done, e + 1)
                    act.activation(x3[:, 2 * e:2 * e + 2, :].rearrange("p b k -> p (b k)"), B8[(3, 6)[e % 2]][0:DIN, :], ACT.Identity,
                                   bias=l3w[0:DIN, Q_BDW:Q_BDW + 1]).then_inc(x3_ready, 1)
                if e:
                    act.wait_ge(px_done, e)
                    act.activation(xb[:, e - 1, :], B8[4 + (e - 1) % 2][:], ACT.Copy).then_inc(px_hi, 1)
                if e >= 5:
                    take_gates(0, e - 5)

            def tail(hb, stages):
                if 0 in stages:
                    for e in range(4):
                        cols = slice(512 * e, 512 * (e + 1))
                        act.wait_ge(tail_dve, D_ALL * hb + D_YC + e + 1)
                        act.activation(yq[:, cols], yc[:, cols], ACT.Square).then_inc(yq_ready, 1)
                if 1 in stages:
                    for e in range(4):
                        cols = slice(512 * e, 512 * (e + 1))
                        act.wait_ge(tail_dve, D_ALL * hb + D_YN + e + 1)
                        act.activation(yc[:, cols], yq[:, cols], ACT.Identity, scale=l3w[0:DIN, Q_LN:Q_LN + 1],
                                       bias=l3w[0:DIN, Q_LN + 1:Q_LN + 2]).then_inc(v_norm, 1)
                        act.wait_ge(v_norm, 4 * hb + e + 1)
                        for b in (2 * e, 2 * e + 1):
                            cols = slice(256 * b, 256 * (b + 1))
                            act.activation(yq[:, cols], yc[:, cols], ACT.Square, accum_out=gx[:, 0, b:b + 1]).then_inc(gx2_ready, 1)
                if 2 in stages:
                    for e in range(4):
                        act.wait_ge(tail_pe, M_ALL * hb + M_OUT + e + 1)
                        act.activation(ob[:, 2 * e:2 * e + 2, :].rearrange("p b k -> p (b k)"), B8[6 + e % 2][0:C, :],
                                       ACT.Copy).then_inc(out_ready, 1)

            for u in range(8):
                if u >= 2:
                    act.wait_ge(lud_taken, 12 * (u - 1))
                    act.wait_ge(y_added, 2 * u - 2)
                if u:
                    for e in range(4):
                        take_gates(u, e)
                act.wait_ge(sum_ready, 2 * u + 2)
                act.activation(mag[1][:], gsum[u % 2][:], ACT.Ln, bias=gate_eps[0:DIN]).then_inc(guess_ready, 1)
                act.wait_ge(guess_ready, 2 * u + 1)
                act.activation(mag[1][:], mag[1][:], ACT.Exp, scale=-1.0).then_inc(guess_ready, 1)
                if u in (5, 6):
                    tail(0, (u - 5,))
                if u < 7:
                    act.wait_ge(recip_done, 2 * u + 2)
            tail(0, (2,))
            tail(1, (0, 1, 2))

        @block.tensor
        def _(pe):
            def windows_T(t, shifted, v):
                pe.wait_ge(ln1[5], v)
                for i in range(TILES):
                    b, half = i // 2, i % 2
                    if not shifted:
                        dst = t.bank[1][0:ZW, :].rearrange("p (u v b y i) -> p u b y v i", u=2, v=2, b=2, y=2)
                        op = pe.matmul(dst[:, half, b], t.z[:, i, :], ident[:], start=True, stop=True)
                    else:
                        dst = t.bank[1][0:ZW, :].rearrange("p (u v b y x i) -> p b y x u v i", u=2, v=2, b=2, y=2, x=2)
                        cols = ident[:].rearrange("p (u v i) -> p u v i", u=2, v=4)
                        cols = cols if half else cols[:, ::-1]
                        for x, pick in enumerate((cols[:, :, 1::-1], cols[:, :, 2:4])):
                            op = pe.matmul(dst[:, b, half, x], t.z[:, i, :], pick, start=True, stop=True)
                op.then_inc(pe_zT, 1)

            def transpose_z(t, chain, done, v):
                pe.wait_ge(chain[5], v)
                for i in range(TILES):
                    op = pe.transpose(t.bank[1][0:ZW, i * 128:(i + 1) * 128], t.z[:, i, :], ident[:])
                op.then_inc(done, 1)

            def project_qk(t, w, v):
                pe.wait_ge(xT_ready, v)
                pe.matmul(t.bank[0][:], w[:, W_QK:W_QK + 128], t.xT[:], start=True, stop=True).then_inc(pe_qk, 1)

            def project_v(t, w, v):
                for p in range(PAIRS):
                    op = pe.matmul(t.bank[2][:, p * C:(p + 1) * C], t.xT[:, 128 * p:128 * (p + 1)],
                                   w[:, W_V:W_V + C], start=True, stop=True)
                op.then_inc(pe_v, 1)

            def bias(t, shifted, lp, v, p):
                if p == 0:
                    pe.wait_ge(qk_ready[0], v)
                    pe.wait_ge(qk_ready[1], v)
                if p == 2:
                    pe.wait_ge(v_ready, v)
                for part, table in enumerate((bias_hm, bias_lm)):
                    if shifted:
                        rhs = table[:, bass.ds(lp * 4 + (3 + p), 1), :]
                    else:
                        rhs = table[:, bass.ds(lp, 1), :]
                    pe.matmul(t.bank[p][:, 0:SC], ident2[:], rhs.rearrange("p o c -> p (o c)"), start=(part == 0), stop=(part == 1))

            def scores(t, v, p):
                if p == 0:
                    pe.wait_ge(qk_ready[1], v)
                    for part in (2, 3, 4):
                        pe.wait_ge(qk_ready[part], v)
                for b in range(2):
                    cols = slice(128 * p + 64 * b, 128 * p + 64 * b + 64)
                    op = pe.matmul(t.bank[p][64 * b:64 * b + 64, 0:SC], t.q[:, cols], t.k[:, :, cols],
                                   start=False, stop=True, skip_group_check=True)
                op.then_inc(pe_S[p], 1)

            def probs_T(t, v):
                for p in range(PAIRS):
                    pe.wait_ge(p_ready[p], v)
                    for h in range(HP):
                        op = pe.transpose(t.bank[p][:, 128 * h:128 * (h + 1)],
                                          t.d[:, p, 2 * h:2 * h + 2].rearrange("p h m -> p (h m)"), ident[:])
                    op.then_inc(pe_PT[p], 1)

            def values(t, v):
                for p in range(PAIRS):
                    pe.wait_ge(pt_ready[p], v)
                    for b in range(2):
                        for h in range(HP):
                            op = pe.matmul(t.bank[0][64 * b:64 * b + 64, p * VO:(p + 1) * VO], t.pt[:, p, h, 64 * b:64 * b + 64],
                                           t.v[:, 2 * p + b, h * VO:(h + 1) * VO], start=(h == 0), stop=(h == HP - 1))
                op.then_inc(pe_O, 1)

            def values_T(t, shifted, v):
                pe.wait_ge(on_ready, v)
                dst = tokens(t.bank[1][0:ZW, :])
                for p in range(PAIRS):
                    ys, xs = blocks_of(shifted, p // 2), blocks_of(shifted, p % 2)
                    o = t.on[:, p * C:p * C + ZW]
                    if xs.step is None:
                        op = pe.matmul(dst[:, :, ys, xs].rearrange("p b y x i -> p b y (x i)"), o, ident[:], start=True, stop=True)
                    else:
                        cols = ident[:].rearrange("p (b y x i) -> p x b y i", b=2, y=2, x=2)
                        for k, x in enumerate((0, 3)):
                            op = pe.matmul(dst[:, :, ys, x], o, cols[:, k], start=True, stop=True)
                op.then_inc(pe_OT, 1)

            def proj(t, w, v):
                pe.wait_ge(o_ready, v)
                for i in range(TILES):
                    op = pe.matmul(t.bank[2][:, i * C:(i + 1) * C], t.oT[:, i * 128:(i + 1) * 128],
                                   w[:, W_PROJ:W_PROJ + C], start=True, stop=True)
                op.then_inc(pe_proj, 1)

            def fc1(t, w, v):
                pe.wait_ge(xT2_ready, v)
                for h in range(2):
                    pe.matmul(t.bank[2 + h][0:96, :], w[:, W_FC1 + 96 * h:W_FC1 + 96 * (h + 1)], t.xT[:],
                              start=True, stop=True).then_inc(pe_fc1[h], 1)

            def fc2(t, w, v):
                pe.wait_ge(g_ready[0], v)
                pe.wait_ge(g_ready[1], v)
                for i in range(TILES):
                    for h in range(2):
                        op = pe.matmul(t.bank[0][:, i * C:(i + 1) * C], t.g[:, h, i * 128:(i + 1) * 128],
                                       w[0:96, W_FC2 + C * h:W_FC2 + C * (h + 1)], start=(h == 0), stop=(h == 1))
                op.then_inc(pe_fc2, 1)

            def slot(x, y):
                if y:
                    probs_T(y.t, y.v)
                    values(y.t, y.v)
                    values_T(y.t, y.par == 1, y.v)
                if x:
                    if x.before is not None:
                        pe.wait_ge(y_ready, x.before)
                    windows_T(x.t, x.par == 1, x.v)
                    bias(x.t, x.par == 1, x.lp, x.v, 3)
                if y:
                    proj(y.t, wts[y.par], y.v)
                if x:
                    pe.wait_ge(ld_w[x.par], x.wv)
                    project_qk(x.t, wts[x.par], x.v)
                    project_v(x.t, wts[x.par], x.v)
                    bias(x.t, x.par == 1, x.lp, x.v, 1)
                    bias(x.t, x.par == 1, x.lp, x.v, 0)
                if y:
                    transpose_z(y.t, ln2, pe_z2T, y.v)
                if x:
                    scores(x.t, x.v, 0)
                    scores(x.t, x.v, 1)
                if y:
                    fc1(y.t, wts[y.par], y.v)
                if x:
                    bias(x.t, x.par == 1, x.lp, x.v, 2)
                    scores(x.t, x.v, 2)
                    scores(x.t, x.v, 3)
                if y:
                    fc2(y.t, wts[y.par], y.v)

            pe.wait_ge(ld_const, 16 * 4)
            pe.wait_ge(split, 4)
            pe.wait_ge(setup, 10 * STREAMS)
            pipeline(pe, slot, None, lambda s, v: transpose_z(st[s], fin, pe_fin, v), None, lambda: pe.wait_ge(split, 6))

            pe.wait_ge(y_ready, 9)
            pe.wait_ge(y_copied, 8)
            pe.wait_ge(conv_ready, 1)
            for i in range(16):
                y, x = i // 4, i % 4
                for kx in range(3):
                    for ky in (0, 2):
                        op = pe.matmul(B8[i // 2][0:C, 256 * (i % 2):256 * (i % 2) + 256],
                                       conv_w[:, kx + 3 * (ky // 2), :],
                                       ypad[:, :, y + ky:y + ky + 13:4, x + kx:x + kx + 13:4],
                                       start=(kx == 0 and ky == 0), stop=(kx == 2 and ky == 2))
                if i % 2:
                    op.then_inc(conv_done, 1)
            for n in range(4):
                pe.wait_ge(act_maps, 2 + 2 * (n // 2))
                pe.wait_ge(dve_maps, 2 + 2 * (n // 2))
                for i in range(8):
                    op = pe.transpose(B8[n][:, C * i:C * (i + 1)], y2[:, 8 * (n // 2) + i, 128 * (n % 2):128 * (n % 2) + 128],
                                      ident[0:C, 0:C])
                op.then_inc(back_done, 1)

            def pairs_T(k, bk):
                for n in range(4):
                    pe.wait_ge(norm_ready, 4 * k + n + 1)
                    z = z1[:, n % 2, 8 * (n // 2):8 * (n // 2) + 8, :].rearrange("p i c -> p (i c)")
                    for a in range(4):
                        op = pe.transpose(B8[bk + n][0:96, 128 * a:128 * (a + 1)], z[:, 96 * a:96 * (a + 1)], ident[:])
                    op.then_inc(zT_done, 1)

            pairs_T(0, 4)
            pe.wait_ge(xs_ready, 4)
            pe.wait_ge(sed_ready, 1)
            sw = sed_w[0:96, :].rearrange("p (a c m) -> p a c m", a=8, c=8)
            for c in range(8):
                for a in range(8):
                    op = pe.matmul(B8[c // 2][0:96, 256 * (c % 2):256 * (c % 2) + 256], sw[:, a, c, :], xs[:, a, :],
                                   start=(a == 0), stop=(a == 7))
                if c % 2:
                    op.then_inc(sed_done, 1)
            for c in range(8):
                pe.wait_ge(h_ready, c // 2 + 1)
                for h in range(2):
                    op = pe.matmul(B8[4 + h + 2 * (c // 4)][:, 96 * (c % 4):96 * (c % 4) + 96], hs[:, c, 128 * h:128 * h + 128],
                                   l1w[0:96, V_PROJ:V_PROJ + 96], start=True, stop=True)
                if c % 4 == 3:
                    op.then_inc(proj1_done, 1)
            pairs_T(1, 0)

            def fc2_late(t):
                pe.wait_ge(g1_ready, 4 * t + 4)
                pe.wait_ge(xs_ready, 8)
                for c in (2 * t, 2 * t + 1):
                    for h in range(2):
                        for r in range(2):
                            col = 96 * (c % 4) + C * r
                            for k in range(2):
                                op = pe.matmul(B8[h + 2 * (c // 4)][:, col:col + C], g1[:, 2 * r + k, 256 * c + 128 * h:256 * c + 128 * h + 128],
                                               l1w[0:96, V_FC2 + C * k:V_FC2 + C * (k + 1)], start=(k == 0), stop=(k == 1))
                if t % 2:
                    op.then_inc(fc2_done, 1)

            for t in range(4):
                pe.wait_ge(xs_ready, 6 + 2 * (t // 2))
                for u in range(4):
                    if t:
                        pe.wait_ge(g1_ready, 4 * (t - 1) + u + 1)
                    pe.matmul(B8[4 + u][0:96, :], l1w[0:96, V_FC1 + 96 * u:V_FC1 + 96 * (u + 1)],
                              xs[:, 2 * t:2 * t + 2, :].rearrange("p c w -> p (c w)"), start=True, stop=True).then_inc(fc1_done, 1)
                if t:
                    fc2_late(t - 1)
            fc2_late(3)

            for k in range(8):
                pe.wait_ge(x1_final, 2 if k < 4 else 4)
                if k == 4:
                    pe.wait_ge(x1_final, 4)
                for i in range(4):
                    op = pe.transpose(B8[(4 + k) % 8][0:C, 128 * i:128 * (i + 1)], x1[:, k % 2, 4 * (k // 2) + i, :], ident[:])
                op.then_inc(x2T_done, 1)
            pe.wait_ge(pooled_ready, 1)
            pe.matmul(B8[4][0:64, 0:8], l2w[0:112, U_W1:U_W1 + 64], pooled[:], start=True, stop=True).then_inc(t_done, 1)
            pe.wait_ge(t_ready, 1)
            for tap in range(4):
                op = pe.matmul(B8[5][0:112, 8 * tap:8 * tap + 8], l2w[0:64, U_W2 + 112 * tap:U_W2 + 112 * (tap + 1)], t2[:, 2],
                               start=True, stop=True)
            op.then_inc(wt_done, 1)

            gw = gates_w[:].rearrange("p (g d c) -> p g d c", g=6, d=4)

            def gate_mm(u, e, g, bk, done):
                pe.matmul(B8[bk][0:DIN, :], gw[:, g, u % 4, :], xb[:, 4 * (u // 4) + e, :], start=True, stop=True).then_inc(done, 1)

            def gates(u, pairs=range(4)):
                for e in pairs:
                    for k in range(3):
                        n = 4 * u + e
                        if n:
                            pe.wait_ge(gate_taken[k], n)
                        gate_mm(u, e, k, k, gate_done[k])

            pe.wait_ge(ld_late, 16 * 7)
            for e in range(9):
                if e < 8:
                    h, j = e // 4, 2 * (e % 4)
                    pe.wait_ge(maps_copied[h], 2 * (e % 4) + 2)
                    if e >= 2:
                        pe.wait_ge(x3_ready, e - 1)
                    for kx in range(3):
                        for ky in (0, 2):
                            op = pe.matmul(B8[(3, 6)[e % 2]][0:DIN, :], taps_w[:, kx + 3 * (ky // 2), :],
                                           a3[h][:, j:j + 2, ky:ky + 16, kx:kx + 16],
                                           start=(kx == 0 and ky == 0), stop=(kx == 2 and ky == 2))
                    op.then_inc(x3_done, 1)
                if e:
                    pe.wait_ge(x3_ready, e)
                    if e >= 3:
                        pe.wait_ge(px_left, e - 2)
                    pe.matmul(B8[4 + (e - 1) % 2][:], l3w[0:DIN, Q_XD:Q_XD + 128], x3[:, 2 * e - 2:2 * e, :].rearrange("p b k -> p (b k)"),
                              start=True, stop=True).then_inc(px_done, 1)
                if e >= 5:
                    pe.wait_ge(xb_ready, 2 * (e - 5) + 2)
                    gates(0, (e - 5,))

            def lud(u, i, e, g):
                n = 12 * u + i
                if n >= 3:
                    pe.wait_ge(lud_taken, n - 2)
                gate_mm(u, e, g, 3 + i % 3, lud_done)

            def in_gates(u):
                for i in range(8):
                    lud(u, i, i // 2, (3, 5)[i % 2])

            def out_gates(u):
                for e in range(4):
                    lud(u, 8 + e, e, 4)

            def tail(hb, stages):
                ones = l3w[0:DIN, Q_ONE:Q_ONE + DIN]
                if 0 in stages:
                    pe.wait_ge(y_added, 8 * hb + 8)
                    for e in range(4):
                        if e >= 2:
                            pe.wait_ge(tail_dve, D_ALL * hb + D_YC + e - 1)
                        if hb and e == 0:
                            pe.wait_ge(out_ready, 4)
                        pe.matmul(B8[6 + e % 2][0:DIN, :], ones, ysum[hb][:, 512 * e:512 * (e + 1)],
                                  start=True, stop=True).then_inc(tail_pe, 1)
                if 1 in stages:
                    for t in range(16):
                        if hb and t % 4 == 0:
                            pe.wait_ge(yq_ready, 4 * hb + t // 4 + 1)
                        if not hb and t == 0:
                            pe.wait_ge(yq_ready, 4)
                        op = pe.matmul(B8[VAR_BANK[hb]][:, t:t + 1], yq[:, 128 * t:128 * (t + 1)], ones[:, 0:1], start=True, stop=True)
                    op.then_inc(tail_pe, 1)
                if 2 in stages:
                    pe.wait_ge(trstd_ready, hb + 1)
                    pe.transpose(B8[7][0:16, 0:128], tvar[:, 1, :], ident[:]).then_inc(tail_pe, 1)
                if 3 in stages:
                    pe.wait_ge(tail_dve, D_ALL * hb + D_RT + 1)
                    for e in range(4):
                        if e >= 2:
                            pe.wait_ge(tail_dve, D_ALL * hb + D_YN + e - 1)
                        for t in range(4):
                            op = pe.matmul(B8[6 + e % 2][0:DIN, 128 * t:128 * (t + 1)], spread[:, 4 * e + t, :], rT[:],
                                           start=True, stop=True)
                        op.then_inc(tail_pe, 1)
                if 4 in stages:
                    pe.wait_ge(gx_ready, hb + 1)
                    pe.matmul(B8[6][0:DIN, 0:8], ones, gx[:, 1], start=True, stop=True).then_inc(tail_pe, 1)
                if 5 in stages:
                    for e in range(4):
                        pe.wait_ge(tail_dve, D_ALL * hb + D_V2 + 2 * e + 2)
                        if e >= 2:
                            pe.wait_ge(out_ready, 4 * hb + e - 1)
                        pe.matmul(B8[6 + e % 2][0:C, :], l3w[0:DIN, Q_OUT:Q_OUT + C], yq[:, 512 * e:512 * (e + 1)],
                                  start=True, stop=True).then_inc(tail_pe, 1)

            pe.wait_ge(xb_ready, 16)
            for u in range(8):
                in_gates(u)
                if u >= 5:
                    tail(0, ((0,), (3,), (5,))[u - 5])
                if u < 7:
                    gates(u + 1)
                if u in (5, 6):
                    tail(0, (1,) if u == 5 else (4,))
                out_gates(u)
                if u == 5:
                    tail(0, (2,))
            tail(1, range(6))


def rel_pos_index():
    ws = 8
    coords = np.stack(np.meshgrid(np.arange(ws), np.arange(ws), indexing="ij")).reshape(2, -1)
    rel = (coords[:, :, None] - coords[:, None, :]).transpose(1, 2, 0)
    rel[:, :, 0] += ws - 1
    rel[:, :, 1] += ws - 1
    rel[:, :, 0] *= 2 * ws - 1
    return rel.sum(-1)


def window_order(shifted, u, v):
    order = []
    swap_y, swap_x = shifted and u == 1, shifted and v == 1
    for sy in range(2):
        for sx in range(2):
            y0, x0 = (1 - sy if swap_y else sy), (1 - sx if swap_x else sx)
            for iy in range(4):
                for ix in range(4):
                    order.append((4 * y0 + iy) * 8 + 4 * x0 + ix)
    return np.array(order)


def attn_mask(u, v):
    ids = np.zeros((8, 8))
    if u == 1:
        ids[4:, :] += 2
    if v == 1:
        ids[:, 4:] += 1
    ids = ids.reshape(-1)
    return np.where(ids[None, :] != ids[:, None], -100.0, 0.0)


def bias_layout(rpb):
    rpi = rel_pos_index()
    gathered, masks = [None] * 15, [None] * 15
    for l in range(3):
        for shifted in (False, True):
            for u in range(2):
                for v in range(2):
                    if not shifted and (u, v) != (0, 0):
                        continue
                    o = window_order(shifted, u, v)
                    idx = 3 + 4 * l + 2 * u + v if shifted else l
                    gathered[idx] = rpb[2 * l + shifted][rpi[o][:, o]].transpose(0, 2, 1)
                    m = attn_mask(u, v)[o][:, o] if shifted else np.zeros((64, 64))
                    masks[idx] = np.repeat(m[:, None, :], HEADS, 1)
    return np.stack(gathered, 1).reshape(64, 15, SC), np.stack(masks, 1).reshape(64, 15, SC)


def pack_l0(qkv_w, qkv_b, proj_w, proj_b, n1_g, n1_b, n2_g, n2_b, fc1_w, fc1_b, fc2_w, fc2_b):
    wp = np.zeros((8, 128, W_COLS), np.float32)
    for i in range(8):
        l = i % 6
        for j in range(2):
            wp[i, :C, W_QK + 64 * j:W_QK + 64 * j + C] = qkv_w[l][C * j:C * (j + 1)].T
            wp[i, C, W_QK + 64 * j:W_QK + 64 * j + C] = qkv_b[l][C * j:C * (j + 1)]
        wp[i, :C, W_V:W_V + C] = qkv_w[l][96:144].T
        wp[i, C, W_V:W_V + C] = qkv_b[l][96:144]
        wp[i, :C, W_PROJ:W_PROJ + C] = proj_w[l].T
        wp[i, :C, W_FC1:W_FC1 + MLP] = fc1_w[l].T
        wp[i, C, W_FC1:W_FC1 + MLP] = fc1_b[l]
        wp[i, :96, W_FC2:W_FC2 + 96] = fc2_w[l].T.reshape(2, 96, C).transpose(1, 0, 2).reshape(96, 96)
        for j, a in enumerate((n1_g, n1_b, n2_g, n2_b)):
            wp[i, :C, W_GB + j] = a[l]
            wp[i, C, W_GB + j] = 1.0 - j % 2
        wp[i, :, W_PB:W_PB + C] = proj_b[l]
        wp[i, :, W_B2:W_B2 + C] = fc2_b[l]
    return wp


def sedenion_signs():
    def conj(x):
        return x if len(x) == 1 else np.concatenate([conj(x[:len(x) // 2]), -x[len(x) // 2:]])

    def mult(a, b):
        if len(a) == 1:
            return a * b
        h = len(a) // 2
        a1, a2, b1, b2 = a[:h], a[h:], b[:h], b[h:]
        return np.concatenate([mult(a1, b1) - mult(conj(b2), a2), mult(b2, a1) + mult(a2, conj(b1))])

    eye = np.eye(16, dtype=np.float32)
    return np.array([[mult(eye[i], eye[i ^ k])[k] for k in range(16)] for i in range(16)], np.float32)


def late_arrays(inp):
    l0 = {k[8:]: v for k, v in inp.items() if k.startswith("L0_conv_")}
    l1 = {k[8:]: v for k, v in inp.items() if k.startswith("L1_conv_")}
    l2 = {k[8:]: v for k, v in inp.items() if k.startswith("L2_conv_")}
    cw = np.zeros((112, 6, C), np.float32)
    w = l0["conv_w"].transpose(1, 2, 3, 0)
    cw[:C, 0:3], cw[64:, 0:3], cw[:C, 3:6] = w[:, 0], w[:, 1], w[:, 2]
    i, k = np.arange(16)[:, None], np.arange(16)[None, :]
    sed = l1["w_sed"][i ^ k]
    sed = sed.reshape(8, 2, 16, C, C).transpose(1, 3, 0, 2, 4).reshape(96, 16 * SC)
    signs = sedenion_signs().reshape(8, 2, 16).transpose(1, 0, 2)
    signs = np.repeat(signs.reshape(2, 1, 128), C, 1).reshape(96, 128)
    lw = np.zeros((128, L1_COLS), np.float32)
    for r in range(2):
        rows = slice(C * r, C * r + C)
        lw[rows, V_PROJ + C * r:V_PROJ + C * (r + 1)] = l1["proj_w"]
        lw[rows, V_FC1 + 192 * r:V_FC1 + 192 * (r + 1)] = l1["fc1_w"]
        for j, a in enumerate(("norm1_g", "norm1_b", "norm2_g", "norm2_b")):
            lw[rows, V_GB + j] = l1[a]
    lw[:96, V_FC2:V_FC2 + 96] = l1["fc2_w"].reshape(2, 96, C).transpose(1, 0, 2).reshape(96, 96)
    lw[:96, V_F1B:V_F1B + 2] = l1["fc1_b"].reshape(2, 96).T
    lw[:, V_PB:V_PB + C], lw[:, V_B2:V_B2 + C] = l1["proj_b"], l1["fc2_b"]
    mw = np.zeros((128, L2_COLS), np.float32)
    mw[:64, U_BN + 3] = 1.0
    for h in range(2):
        ch, hid = slice(64 * h, 64 * h + C), slice(32 * h, 32 * h + 12)
        mw[ch, U_W1 + 32 * h:U_W1 + 32 * h + 12] = l2["w1"].T
        w2, b2 = l2["w2"].reshape(C, 9, 12), l2["b2"].reshape(C, 9)
        for t in range(4):
            c0 = U_W2 + 112 * t + 64 * h
            mw[hid, c0:c0 + C] = w2[:, t].T
            mw[ch, U_B2 + t] = b2[:, t]
        mw[ch, U_BIAS] = l2["bias"]
        for j, a in enumerate(("gamma", "beta", "running_mean", "running_var")):
            mw[hid, U_BN + j] = l2[a]
    l3 = {k[8:]: v for k, v in inp.items() if k.startswith("L3_conv_")}
    front = np.zeros((112, 96), np.float32)
    taps = np.zeros((112, 6, 96), np.float32)
    dw = l3["W_dw"].reshape(96, 3, 3).transpose(1, 2, 0)
    taps[:C, 0:3], taps[64:, 0:3], taps[:C, 3:6] = dw[0], dw[1], dw[2]
    for h in range(2):
        front[64 * h:64 * h + C] = l3["W_in"].T
    raw = np.concatenate([l3["W_w"], l3["W_l"], l3["W_u"], l3["W_d"]]).T
    raw = np.tile(raw, (8, 1))
    qw = np.zeros((128, L3_COLS), np.float32)
    qw[:96, Q_XD:Q_XD + 128] = np.tile(l3["W_xd"].T, (1, 8))
    qw[:96, Q_OUT:Q_OUT + 48] = l3["W_out"].T
    qw[:, Q_ONE:Q_ONE + 96] = 1.0
    for c, a in ((Q_BDW, "b_dw"), (Q_LN, "ln_w"), (Q_LN + 1, "ln_b"), (Q_GRN, "grn_gamma"), (Q_GRN + 1, "grn_beta")):
        qw[:96, c] = l3[a]
    qw[:, Q_WM:Q_WM + 4] = l3["w_m"]
    for blk, part in enumerate((0, 1, 0, 1, 2, None, 0, 1)):
        if part is not None:
            qw[16 * blk:16 * blk + 16, Q_MASK + part] = 1.0
    spread = np.zeros((16, 16, 96), np.float32)
    spread[np.arange(16), np.arange(16)] = 1.0
    return {"conv_in": cw, "sed_in": sed, "sign_in": signs, "l1_in": lw, "l2_in": mw,
            "front_in": front, "taps_in": taps, "gates_in": raw, "l3_in": qw, "spread_in": spread}


def first_layer_arrays(inp):
    x = inp["x"].reshape(8, 2, C, 2, 2, 4, 4, 4)
    x = x.transpose(0, 4, 6, 5, 7, 1, 3, 2).reshape(8, 128, TILES, C)
    x = np.concatenate([x, x[-2:]], 0)
    l0 = {k[8:]: v for k, v in inp.items() if k.startswith("L0_conv_")}
    bias, mask = bias_layout(l0["rpb"])
    fn = np.zeros((KA, 2 + HEADS), np.float32)
    fn[np.arange(C), 2 + np.arange(C) // HD] = 1.0
    fn[:C, 0], fn[:C, 1] = l0["fn_g"], l0["fn_b"]
    fn[C, 0] = 1.0
    return {
        "x_tok": np.ascontiguousarray(x),
        "wpack": pack_l0(*[l0[k] for k in ("qkv_w", "qkv_b", "proj_w", "proj_b", "n1_g", "n1_b", "n2_g", "n2_b",
                                         "fc1_w", "fc1_b", "fc2_w", "fc2_b")]),
        "rpb_raw": np.ascontiguousarray(bias),
        "mask_in": mask.astype(np.dtype("bfloat16")),
        "ident_in": np.eye(128, dtype=np.float32),
        "ident2_in": np.tile(np.eye(64), (2, 2)).astype(np.dtype("bfloat16")),
        "en_in": np.broadcast_to(np.stack([l0["en_g"], l0["en_b"]]), (128, 2, C)).copy(),
        "fn_in": fn,
    }


_ARGS = ["x_tok", "wpack", "rpb_raw", "mask_in", "ident_in", "ident2_in", "en_in", "fn_in", "conv_in", "sed_in", "sign_in",
         "l1_in", "l2_in", "front_in", "taps_in", "gates_in", "l3_in", "spread_in"]


def kernel(**inputs):
    import concourse.bacc as bacc
    from concourse.bass_utils import run_bass_kernel_spmd as run

    inp = {name: np.asarray(a) for name, a in inputs.items()}
    laid = {**first_layer_arrays(inp), **late_arrays(inp)}
    nc = bacc.Bacc("TRN2", target_bir_lowering=False, num_devices=1)
    arrays, args = {}, []
    for name in _ARGS:
        a = np.ascontiguousarray(laid[name])
        arrays[f"in_{name}"] = a
        args.append(nc.dram_tensor(f"in_{name}", a.shape, mybir.dt.from_np(a.dtype), kind="ExternalInput").ap())
    args.append(nc.dram_tensor("out_0", (B, C, IMG, IMG), F32, kind="ExternalOutput").ap())
    build(nc, *args)
    r = run(nc, [arrays], core_ids=[0])
    return r.results[0]["out_0"]
```
